# Optimizing a Trainium2 kernel written in Bass

```python
import numpy as np
import jax
import jax.numpy as jnp

def _softmax(x, axis=-1):
    return jax.nn.softmax(x, axis=axis)

def _gelu(x):
    return jax.nn.gelu(x, approximate=True)

def _silu(x):
    return jax.nn.silu(x)

def _sigmoid(x):
    return jax.nn.sigmoid(x)

def _layernorm(x, axis=-1, eps=1e-05):
    m = jnp.mean(x, axis=axis, keepdims=True)
    v = jnp.var(x, axis=axis, keepdims=True)
    return (x - m) / jnp.sqrt(v + eps)

def _scatter_add(tgt, idx, src, axis=0):
    return tgt.at[idx].add(src)

def _segment_sum(src, seg, n):
    return jax.ops.segment_sum(src, seg, n)
kernel_name = 'mk_xattn_ffn_d4_seqx_r4_d7092f'

def setup_inputs(seed: int=0):
    np.random.seed(seed)
    _w = jnp.asarray

    def _rec_inputs():
        import jax
        import jax.numpy as jnp
        _rk = jax.random.key(seed)
        x = -0.0003929 + 0.9999 * jax.random.normal(jax.random.fold_in(_rk, 1), (16, 128, 256), jnp.float32)
        _lenS = 128 - jax.random.randint(jax.random.fold_in(_rk, 7), (16,), 0, max(1, 128 // 4) + 1, jnp.int32)
        _lenS2 = 128 - jax.random.randint(jax.random.fold_in(_rk, 8), (16,), 0, max(1, 128 // 4) + 1, jnp.int32)
        _ctx_1024P = jax.random.normal(jax.random.fold_in(_rk, 11), (16, 16, 256), jnp.float32)
        _ctx_1024c = jax.random.dirichlet(jax.random.fold_in(_rk, 511), 0.3 * jnp.ones((16,), jnp.float32), (16, 128))
        _ctx_1024t = jnp.einsum('bsk,bkd->bsd', _ctx_1024c, _ctx_1024P)
        _ctx_1024t = _ctx_1024t * jax.lax.rsqrt(jnp.mean(jnp.square(_ctx_1024t)) + 1e-12) * 0.953939
        ctx_1024 = 2.81802e-05 + 1.00001 * (_ctx_1024t + 0.3 * jax.random.normal(jax.random.fold_in(_rk, 611), (16, 128, 256), jnp.float32))
        return (x, ctx_1024)
    x, ctx_1024 = _rec_inputs()

    def _L0_xattn_setup():
        import jax, jax.numpy as jnp
        import numpy as np
        import math
        D_MODEL = 256
        N_HEADS = 16
        C = 1
        B, L = (8, 512)

        def _glorot(key, fan):
            lim = np.sqrt(6.0 / (fan + fan)).astype(np.float32)
            return jax.random.uniform(key, (fan, fan), jnp.float32, -lim, lim)
        key = jax.random.key(seed)
        ks = jax.random.split(key, 7)
        queries = jax.random.normal(ks[0], (B, L, D_MODEL), jnp.float32)
        keys = jax.random.normal(ks[1], (B, L, D_MODEL), jnp.float32)
        values = jax.random.normal(ks[2], (B, L, D_MODEL), jnp.float32)
        wq = _glorot(ks[3], D_MODEL)
        wk = _glorot(ks[4], D_MODEL)
        wv = _glorot(ks[5], D_MODEL)
        wo = _glorot(ks[6], D_MODEL)
        return {'queries': queries, 'keys': keys, 'values': values, 'wq': wq, 'wk': wk, 'wv': wv, 'wo': wo}
    _L0_xattn_all = _L0_xattn_setup()
    _L0_xattn_in = {k: v for k, v in _L0_xattn_all.items() if k in ('wq', 'wk', 'wv', 'wo')}
    del _L0_xattn_all

    def _L0_ffn_setup():
        import jax, jax.numpy as jnp
        import numpy as np
        BLOCK = 32
        W_BITS = 4
        ACT_BITS = 16

        def act_qdq(x):
            qmax = 2.0 ** (ACT_BITS - 1) - 1.0
            scale = jnp.maximum(jnp.max(jnp.abs(x)) / qmax, 1e-12)
            return jnp.clip(jnp.round(x / scale), -qmax - 1.0, qmax) * scale

        def fixed_qdq_u16(x):
            scale = 1.0 / 65536.0
            return jnp.clip(jnp.round(x / scale), 0.0, 65535.0) * scale

        def lpbq_dequant(w):
            O, I = w.shape
            qmax = 2.0 ** (W_BITS - 1) - 1.0
            wb = w.reshape(O, I // BLOCK, BLOCK)
            s = jnp.maximum(jnp.max(jnp.abs(wb), axis=-1, keepdims=True) / qmax, 1e-12)
            wq = jnp.clip(jnp.round(wb / s), -qmax - 1.0, qmax) * s
            return wq.reshape(O, I)
        key = jax.random.key(seed)
        k1, k2, k3, k4 = jax.random.split(key, 4)
        B, S, H, I = (2, 1024, 256, 768)
        x = jax.random.normal(k1, (B, S, H), jnp.float32)
        w_gate = jax.random.normal(k2, (I, H), jnp.float32) * 0.02
        w_up = jax.random.normal(k3, (I, H), jnp.float32) * 0.02
        w_down = jax.random.normal(k4, (H, I), jnp.float32) * 0.02
        return {'x': x, 'w_gate': w_gate, 'w_up': w_up, 'w_down': w_down}
    _L0_ffn_all = _L0_ffn_setup()
    _L0_ffn_in = {k: v for k, v in _L0_ffn_all.items() if k in ('w_gate', 'w_up', 'w_down')}
    del _L0_ffn_all

    def _L1_xattn_setup():
        import jax, jax.numpy as jnp
        import numpy as np
        import math
        D_MODEL = 256
        N_HEADS = 16
        HEAD_DIM = D_MODEL // N_HEADS
        WINDOW = 64
        B, S = (2, 512)

        def _window_mask(seq_len: int, w: int) -> jnp.ndarray:
            idx = jnp.arange(seq_len)
            return jnp.abs(idx[:, None] - idx[None, :]) <= w
        key = jax.random.key(seed)
        ks = jax.random.split(key, 11)
        s = 1.0 / math.sqrt(D_MODEL)
        return {'query': jax.random.normal(ks[0], (B, S, D_MODEL), jnp.float32), 'key': jax.random.normal(ks[1], (B, S, D_MODEL), jnp.float32), 'value': jax.random.normal(ks[2], (B, S, D_MODEL), jnp.float32), 'Wq': jax.random.normal(ks[3], (D_MODEL, D_MODEL), jnp.float32) * s, 'bq': jnp.zeros((D_MODEL,), jnp.float32), 'Wk': jax.random.normal(ks[4], (D_MODEL, D_MODEL), jnp.float32) * s, 'bk': jnp.zeros((D_MODEL,), jnp.float32), 'Wv': jax.random.normal(ks[5], (D_MODEL, D_MODEL), jnp.float32) * s, 'bv': jnp.zeros((D_MODEL,), jnp.float32), 'Wo': jax.random.normal(ks[6], (D_MODEL, D_MODEL), jnp.float32) * s, 'bo': jnp.zeros((D_MODEL,), jnp.float32)}
    _L1_xattn_all = _L1_xattn_setup()
    _L1_xattn_in = {k: v for k, v in _L1_xattn_all.items() if k in ('Wq', 'bq', 'Wk', 'bk', 'Wv', 'bv', 'Wo', 'bo')}
    del _L1_xattn_all

    def _L1_ffn_setup():
        import jax, jax.numpy as jnp
        import numpy as np
        B, SEQ, DIM = (2, 1024, 256)
        E, S = (8, 128)
        HID = 4 * DIM
        SCALE = DIM ** 0.5

        def rmsnorm(x, gamma):
            n = jnp.linalg.norm(x, axis=-1, keepdims=True)
            return x / jnp.maximum(n, 1e-12) * SCALE * gamma
        key = jax.random.key(seed)
        ks = jax.random.split(key, 4)
        w_init = lambda k, shape: jax.random.normal(k, shape, dtype=jnp.float32) * 0.02
        return {'x': jax.random.normal(ks[0], (B, SEQ, DIM), dtype=jnp.float32), 'norm_gamma': jnp.ones((DIM,), jnp.float32), 'slot_norm_gamma': jnp.ones((DIM,), jnp.float32), 'slot_embeds': jax.random.normal(ks[1], (E, S, DIM), dtype=jnp.float32), 'w1': w_init(ks[2], (E, DIM, HID)), 'b1': jnp.zeros((E, HID), jnp.float32), 'w2': w_init(ks[3], (E, HID, DIM)), 'b2': jnp.zeros((E, DIM), jnp.float32)}
    _L1_ffn_all = _L1_ffn_setup()
    _L1_ffn_in = {k: v for k, v in _L1_ffn_all.items() if k in ('norm_gamma', 'slot_norm_gamma', 'slot_embeds', 'w1', 'b1', 'w2', 'b2')}
    del _L1_ffn_all

    def _L2_xattn_setup():
        import jax, jax.numpy as jnp
        import numpy as np
        import math
        D = 256
        H = 16
        DH = D // H
        key = jax.random.key(seed)
        ks = jax.random.split(key, 11)
        B, L = (2, 512)
        s = 1.0 / math.sqrt(D)
        return {'Q': jax.random.normal(ks[0], (B, L, D), jnp.float32), 'K': jax.random.normal(ks[1], (B, L, D), jnp.float32), 'V': jax.random.normal(ks[2], (B, L, D), jnp.float32), 'Wq': jax.random.normal(ks[3], (D, D), jnp.float32) * s, 'bq': jnp.zeros((D,), jnp.float32), 'Wk': jax.random.normal(ks[4], (D, D), jnp.float32) * s, 'bk': jnp.zeros((D,), jnp.float32), 'Wv': jax.random.normal(ks[5], (D, D), jnp.float32) * s, 'bv': jnp.zeros((D,), jnp.float32), 'Wo': jax.random.normal(ks[6], (D, D), jnp.float32) * s, 'bo': jnp.zeros((D,), jnp.float32)}
    _L2_xattn_all = _L2_xattn_setup()
    _L2_xattn_in = {k: v for k, v in _L2_xattn_all.items() if k in ('Wq', 'bq', 'Wk', 'bk', 'Wv', 'bv', 'Wo', 'bo')}
    del _L2_xattn_all

    def _L2_ffn_setup():
        import jax, jax.numpy as jnp
        import numpy as np
        DIM = 256

        def _reference_tuple_inner(x, W_r, W_k, W_v, mu_r, mu_k):
            B, T, C = x.shape
            x_prev = jnp.concatenate([jnp.zeros((B, 1, C), x.dtype), x[:, :-1, :]], axis=1)
            xr = mu_r * x + (1.0 - mu_r) * x_prev
            xk = mu_k * x + (1.0 - mu_k) * x_prev
            r = jax.nn.sigmoid(jnp.einsum('btc,dc->btd', xr, W_r))
            k = jnp.einsum('btc,dc->btd', xk, W_k)
            k_act = jnp.square(jax.nn.relu(k))
            out = r * jnp.einsum('btc,dc->btd', k_act, W_v)
            new_state = x[:, -1, :]
            return (out, new_state)
        key = jax.random.key(seed)
        ks = jax.random.split(key, 6)
        B, T, C = (8, 512, DIM)
        x = jax.random.normal(ks[0], (B, T, C), dtype=jnp.float32)
        s = 1.0 / np.sqrt(C)
        W_r = jax.random.uniform(ks[1], (C, C), jnp.float32, -s, s)
        W_k = jax.random.uniform(ks[2], (C, C), jnp.float32, -s, s)
        W_v = jax.random.uniform(ks[3], (C, C), jnp.float32, -s, s)
        mu_r = jax.random.uniform(ks[4], (C,), jnp.float32)
        mu_k = jax.random.uniform(ks[5], (C,), jnp.float32)
        return {'x': x, 'W_r': W_r, 'W_k': W_k, 'W_v': W_v, 'mu_r': mu_r, 'mu_k': mu_k}
    _L2_ffn_all = _L2_ffn_setup()
    _L2_ffn_in = {k: v for k, v in _L2_ffn_all.items() if k in ('W_r', 'W_k', 'W_v', 'mu_r', 'mu_k')}
    del _L2_ffn_all

    def _L3_xattn_setup():
        import jax, jax.numpy as jnp
        import numpy as np
        D_MODEL = 256
        NUM_HEADS = 16
        HEAD_DIM = D_MODEL // NUM_HEADS
        MAX_SEQ = 128

        def rope_tables(seq_len, dim):
            inv_freq = 1.0 / 10000.0 ** (jnp.arange(0, dim, 2, dtype=jnp.float32) / dim)
            t = jnp.arange(seq_len, dtype=jnp.float32)
            freqs = jnp.einsum('i,j->ij', t, inv_freq)
            emb = jnp.concatenate([freqs, freqs], axis=-1)
            return (jnp.cos(emb), jnp.sin(emb))

        def rotate_half(x):
            x1, x2 = jnp.split(x, 2, axis=-1)
            return jnp.concatenate([-x2, x1], axis=-1)
        key = jax.random.key(seed)
        ks = jax.random.split(key, 12)
        B, S, D = (16, 128, D_MODEL)
        s = 1.0 / np.sqrt(D)
        inp = {'query': jax.random.normal(ks[0], (B, S, D), jnp.float32), 'key': jax.random.normal(ks[1], (B, S, D), jnp.float32), 'value': jax.random.normal(ks[2], (B, S, D), jnp.float32), 'Wq': jax.random.normal(ks[3], (D, D), jnp.float32) * s, 'bq': jnp.zeros((D,), jnp.float32), 'Wk': jax.random.normal(ks[4], (D, D), jnp.float32) * s, 'bk': jnp.zeros((D,), jnp.float32), 'Wv': jax.random.normal(ks[5], (D, D), jnp.float32) * s, 'bv': jnp.zeros((D,), jnp.float32), 'Wo': jax.random.normal(ks[6], (D, D), jnp.float32) * s, 'bo': jnp.zeros((D,), jnp.float32)}
        return inp
    _L3_xattn_all = _L3_xattn_setup()
    _L3_xattn_in = {k: v for k, v in _L3_xattn_all.items() if k in ('Wq', 'bq', 'Wk', 'bk', 'Wv', 'bv', 'Wo', 'bo')}
    del _L3_xattn_all

    def _L3_ffn_setup():
        import jax, jax.numpy as jnp
        import numpy as np
        B, S, D = (4, 512, 256)
        EXP = 4
        H = EXP * D
        E = 8
        TOP_K = 2
        key = jax.random.key(seed)
        ks = jax.random.split(key, 8)
        scale1 = 1.0 / np.sqrt(D)
        scale2 = 1.0 / np.sqrt(H)
        x = jax.random.normal(ks[0], (B, S, D), dtype=jnp.float32)
        W1 = jax.random.uniform(ks[1], (E, D, H), jnp.float32, -scale1, scale1)
        b1 = jax.random.uniform(ks[2], (E, H), jnp.float32, -scale1, scale1)
        W2 = jax.random.uniform(ks[3], (E, H, D), jnp.float32, -scale2, scale2)
        b2 = jax.random.uniform(ks[4], (E, D), jnp.float32, -scale2, scale2)
        Wr = jax.random.uniform(ks[5], (D, E), jnp.float32, -scale1, scale1)
        br = jax.random.uniform(ks[6], (E,), jnp.float32, -scale1, scale1)
        return {'input_emb': x, 'W1': W1, 'b1': b1, 'W2': W2, 'b2': b2, 'Wr': Wr, 'br': br}
    _L3_ffn_all = _L3_ffn_setup()
    _L3_ffn_in = {k: v for k, v in _L3_ffn_all.items() if k in ('W1', 'b1', 'W2', 'b2', 'Wr', 'br')}
    del _L3_ffn_all
    return {'x': x, 'ctx_1024': ctx_1024, 'L0_xattn_wq': _L0_xattn_in['wq'], 'L0_xattn_wk': _L0_xattn_in['wk'], 'L0_xattn_wv': _L0_xattn_in['wv'], 'L0_xattn_wo': _L0_xattn_in['wo'], 'L0_ffn_w_gate': _L0_ffn_in['w_gate'], 'L0_ffn_w_up': _L0_ffn_in['w_up'], 'L0_ffn_w_down': _L0_ffn_in['w_down'], 'L1_xattn_Wq': _L1_xattn_in['Wq'], 'L1_xattn_bq': _L1_xattn_in['bq'], 'L1_xattn_Wk': _L1_xattn_in['Wk'], 'L1_xattn_bk': _L1_xattn_in['bk'], 'L1_xattn_Wv': _L1_xattn_in['Wv'], 'L1_xattn_bv': _L1_xattn_in['bv'], 'L1_xattn_Wo': _L1_xattn_in['Wo'], 'L1_xattn_bo': _L1_xattn_in['bo'], 'L1_ffn_norm_gamma': _L1_ffn_in['norm_gamma'], 'L1_ffn_slot_norm_gamma': _L1_ffn_in['slot_norm_gamma'], 'L1_ffn_slot_embeds': _L1_ffn_in['slot_embeds'], 'L1_ffn_w1': _L1_ffn_in['w1'], 'L1_ffn_b1': _L1_ffn_in['b1'], 'L1_ffn_w2': _L1_ffn_in['w2'], 'L1_ffn_b2': _L1_ffn_in['b2'], 'L2_xattn_Wq': _L2_xattn_in['Wq'], 'L2_xattn_bq': _L2_xattn_in['bq'], 'L2_xattn_Wk': _L2_xattn_in['Wk'], 'L2_xattn_bk': _L2_xattn_in['bk'], 'L2_xattn_Wv': _L2_xattn_in['Wv'], 'L2_xattn_bv': _L2_xattn_in['bv'], 'L2_xattn_Wo': _L2_xattn_in['Wo'], 'L2_xattn_bo': _L2_xattn_in['bo'], 'L2_ffn_W_r': _L2_ffn_in['W_r'], 'L2_ffn_W_k': _L2_ffn_in['W_k'], 'L2_ffn_W_v': _L2_ffn_in['W_v'], 'L2_ffn_mu_r': _L2_ffn_in['mu_r'], 'L2_ffn_mu_k': _L2_ffn_in['mu_k'], 'L3_xattn_Wq': _L3_xattn_in['Wq'], 'L3_xattn_bq': _L3_xattn_in['bq'], 'L3_xattn_Wk': _L3_xattn_in['Wk'], 'L3_xattn_bk': _L3_xattn_in['bk'], 'L3_xattn_Wv': _L3_xattn_in['Wv'], 'L3_xattn_bv': _L3_xattn_in['bv'], 'L3_xattn_Wo': _L3_xattn_in['Wo'], 'L3_xattn_bo': _L3_xattn_in['bo'], 'L3_ffn_W1': _L3_ffn_in['W1'], 'L3_ffn_b1': _L3_ffn_in['b1'], 'L3_ffn_W2': _L3_ffn_in['W2'], 'L3_ffn_b2': _L3_ffn_in['b2'], 'L3_ffn_Wr': _L3_ffn_in['Wr'], 'L3_ffn_br': _L3_ffn_in['br']}

def reference(x, ctx_1024, L0_xattn_wq, L0_xattn_wk, L0_xattn_wv, L0_xattn_wo, L0_ffn_w_gate, L0_ffn_w_up, L0_ffn_w_down, L1_xattn_Wq, L1_xattn_bq, L1_xattn_Wk, L1_xattn_bk, L1_xattn_Wv, L1_xattn_bv, L1_xattn_Wo, L1_xattn_bo, L1_ffn_norm_gamma, L1_ffn_slot_norm_gamma, L1_ffn_slot_embeds, L1_ffn_w1, L1_ffn_b1, L1_ffn_w2, L1_ffn_b2, L2_xattn_Wq, L2_xattn_bq, L2_xattn_Wk, L2_xattn_bk, L2_xattn_Wv, L2_xattn_bv, L2_xattn_Wo, L2_xattn_bo, L2_ffn_W_r, L2_ffn_W_k, L2_ffn_W_v, L2_ffn_mu_r, L2_ffn_mu_k, L3_xattn_Wq, L3_xattn_bq, L3_xattn_Wk, L3_xattn_bk, L3_xattn_Wv, L3_xattn_bv, L3_xattn_Wo, L3_xattn_bo, L3_ffn_W1, L3_ffn_b1, L3_ffn_W2, L3_ffn_b2, L3_ffn_Wr, L3_ffn_br):
    import jax
    import jax.numpy as jnp

    def _L0_xattn_ref(queries, keys, values, wq, wk, wv, wo):
        import jax, jax.numpy as jnp
        import numpy as np
        import math
        D_MODEL = 256
        N_HEADS = 16
        C = 1
        B, L = (8, 512)

        def _glorot(key, fan):
            lim = np.sqrt(6.0 / (fan + fan)).astype(np.float32)
            return jax.random.uniform(key, (fan, fan), jnp.float32, -lim, lim)
        Bv, Lv, _ = queries.shape
        H = N_HEADS
        Dh = D_MODEL // N_HEADS
        Q = (queries @ wq).reshape(Bv, Lv, H, Dh).transpose(0, 2, 3, 1)
        K = (keys @ wk).reshape(Bv, Lv, H, Dh).transpose(0, 2, 3, 1)
        V = (values @ wv).reshape(Bv, Lv, H, Dh).transpose(0, 2, 3, 1)
        corr = jnp.fft.irfft(jnp.fft.rfft(Q, axis=-1) * jnp.conj(jnp.fft.rfft(K, axis=-1)), n=Lv, axis=-1)
        k_top = int(math.floor(C * math.log(Lv)))
        top_vals, top_idx = jax.lax.top_k(corr, k_top)
        w = jax.nn.softmax(top_vals, axis=-1)
        t = jnp.arange(Dh)
        out = jnp.zeros_like(V)
        for i in range(k_top):
            gather_idx = (t[None, None, :] - top_idx[..., i]) % Dh
            rolled = jnp.take_along_axis(V, gather_idx[..., None], axis=2)
            out = out + w[..., i, None] * rolled
        out = out.transpose(0, 2, 1, 3).reshape(Bv, Lv, D_MODEL)
        return out @ wo

    def _L0_ffn_ref(x, w_gate, w_up, w_down):
        import jax, jax.numpy as jnp
        import numpy as np
        BLOCK = 32
        W_BITS = 4
        ACT_BITS = 16

        def act_qdq(x):
            qmax = 2.0 ** (ACT_BITS - 1) - 1.0
            scale = jnp.maximum(jnp.max(jnp.abs(x)) / qmax, 1e-12)
            return jnp.clip(jnp.round(x / scale), -qmax - 1.0, qmax) * scale

        def fixed_qdq_u16(x):
            scale = 1.0 / 65536.0
            return jnp.clip(jnp.round(x / scale), 0.0, 65535.0) * scale

        def lpbq_dequant(w):
            O, I = w.shape
            qmax = 2.0 ** (W_BITS - 1) - 1.0
            wb = w.reshape(O, I // BLOCK, BLOCK)
            s = jnp.maximum(jnp.max(jnp.abs(wb), axis=-1, keepdims=True) / qmax, 1e-12)
            wq = jnp.clip(jnp.round(wb / s), -qmax - 1.0, qmax) * s
            return wq.reshape(O, I)
        x = act_qdq(x)
        up = act_qdq(x @ lpbq_dequant(w_up).T)
        gate = act_qdq(x @ lpbq_dequant(w_gate).T)
        sig = fixed_qdq_u16(jax.nn.sigmoid(gate))
        gate = act_qdq(gate * sig)
        o = act_qdq(gate * up)
        return o @ lpbq_dequant(w_down).T

    def _L1_xattn_ref(query, key, value, Wq, bq, Wk, bk, Wv, bv, Wo, bo):
        import jax, jax.numpy as jnp
        import numpy as np
        import math
        D_MODEL = 256
        N_HEADS = 16
        HEAD_DIM = D_MODEL // N_HEADS
        WINDOW = 64
        B, S = (2, 512)

        def _window_mask(seq_len: int, w: int) -> jnp.ndarray:
            idx = jnp.arange(seq_len)
            return jnp.abs(idx[:, None] - idx[None, :]) <= w
        b, s, _ = query.shape
        Q = (query @ Wq.T + bq).reshape(b, s, N_HEADS, HEAD_DIM).transpose(0, 2, 1, 3)
        K = (key @ Wk.T + bk).reshape(b, s, N_HEADS, HEAD_DIM).transpose(0, 2, 1, 3)
        V = (value @ Wv.T + bv).reshape(b, s, N_HEADS, HEAD_DIM).transpose(0, 2, 1, 3)
        scale = 1.0 / math.sqrt(HEAD_DIM)
        scores = jnp.einsum('bhqd,bhkd->bhqk', Q, K) * scale
        mask = _window_mask(s, WINDOW)
        scores = jnp.where(mask[None, None], scores, jnp.float32(-jnp.inf))
        attn = jax.nn.softmax(scores, axis=-1)
        out = jnp.einsum('bhqk,bhkd->bhqd', attn, V)
        out = out.transpose(0, 2, 1, 3).reshape(b, s, D_MODEL)
        return out @ Wo.T + bo

    def _L1_ffn_ref(x, norm_gamma, slot_norm_gamma, slot_embeds, w1, b1, w2, b2):
        import jax, jax.numpy as jnp
        import numpy as np
        B, SEQ, DIM = (2, 1024, 256)
        E, S = (8, 128)
        HID = 4 * DIM
        SCALE = DIM ** 0.5

        def rmsnorm(x, gamma):
            n = jnp.linalg.norm(x, axis=-1, keepdims=True)
            return x / jnp.maximum(n, 1e-12) * SCALE * gamma
        xn = rmsnorm(x, norm_gamma)
        sn = rmsnorm(slot_embeds, slot_norm_gamma)
        logits = jnp.einsum('bnd,esd->bnes', xn, sn)
        dispatch = jax.nn.softmax(logits, axis=1)
        b, n, e, s = logits.shape
        combine = jax.nn.softmax(logits.reshape(b, n, e * s), axis=-1)
        slots = jnp.einsum('bnd,bnes->besd', xn, dispatch)
        h = jnp.einsum('besd,edh->besh', slots, w1) + b1[None, :, None, :]
        h = jax.nn.gelu(h, approximate=False)
        eo = jnp.einsum('besh,ehd->besd', h, w2) + b2[None, :, None, :]
        eo = eo.reshape(b, e * s, DIM)
        out = jnp.einsum('bmd,bnm->bnd', eo, combine)
        return out

    def _L2_xattn_ref(Q, K, V, Wq, bq, Wk, bk, Wv, bv, Wo, bo):
        import jax, jax.numpy as jnp
        import numpy as np
        import math
        D = 256
        H = 16
        DH = D // H
        B, Lq, _ = Q.shape
        Lk = K.shape[1]
        q = (Q @ Wq.T + bq).reshape(B, Lq, H, DH).transpose(0, 2, 1, 3)
        k = (K @ Wk.T + bk).reshape(B, Lk, H, DH).transpose(0, 2, 1, 3)
        v = (V @ Wv.T + bv).reshape(B, Lk, H, DH).transpose(0, 2, 1, 3)
        scores = jnp.einsum('bhlp,bhmp->bhlm', q, k) / math.sqrt(DH)
        attn = jax.nn.softmax(scores, axis=-1)
        out = jnp.einsum('bhlm,bhmp->bhlp', attn, v)
        out = out.transpose(0, 2, 1, 3).reshape(B, Lq, D)
        return out @ Wo.T + bo

    def _L2_ffn_ref(x, W_r, W_k, W_v, mu_r, mu_k):
        import jax, jax.numpy as jnp
        import numpy as np
        DIM = 256

        def _reference_tuple_inner(x, W_r, W_k, W_v, mu_r, mu_k):
            B, T, C = x.shape
            x_prev = jnp.concatenate([jnp.zeros((B, 1, C), x.dtype), x[:, :-1, :]], axis=1)
            xr = mu_r * x + (1.0 - mu_r) * x_prev
            xk = mu_k * x + (1.0 - mu_k) * x_prev
            r = jax.nn.sigmoid(jnp.einsum('btc,dc->btd', xr, W_r))
            k = jnp.einsum('btc,dc->btd', xk, W_k)
            k_act = jnp.square(jax.nn.relu(k))
            out = r * jnp.einsum('btc,dc->btd', k_act, W_v)
            new_state = x[:, -1, :]
            return (out, new_state)
        return _reference_tuple_inner(x, W_r, W_k, W_v, mu_r, mu_k)[0]

    def _L3_xattn_ref(query, key, value, Wq, bq, Wk, bk, Wv, bv, Wo, bo):
        import jax, jax.numpy as jnp
        import numpy as np
        D_MODEL = 256
        NUM_HEADS = 16
        HEAD_DIM = D_MODEL // NUM_HEADS
        MAX_SEQ = 128

        def rope_tables(seq_len, dim):
            inv_freq = 1.0 / 10000.0 ** (jnp.arange(0, dim, 2, dtype=jnp.float32) / dim)
            t = jnp.arange(seq_len, dtype=jnp.float32)
            freqs = jnp.einsum('i,j->ij', t, inv_freq)
            emb = jnp.concatenate([freqs, freqs], axis=-1)
            return (jnp.cos(emb), jnp.sin(emb))

        def rotate_half(x):
            x1, x2 = jnp.split(x, 2, axis=-1)
            return jnp.concatenate([-x2, x1], axis=-1)
        B, S, D = query.shape
        H, Hd = (NUM_HEADS, HEAD_DIM)
        scale = Hd ** (-0.5)

        def proj(x, W, b):
            y = jnp.einsum('bsd,ed->bse', x, W) + b
            return y.reshape(B, S, H, Hd).transpose(0, 2, 1, 3)
        q = proj(query, Wq, bq)
        k = proj(key, Wk, bk)
        v = proj(value, Wv, bv)
        cos, sin = rope_tables(S, Hd)
        cos = cos[None, None]
        sin = sin[None, None]
        q = q * cos + rotate_half(q) * sin
        k = k * cos + rotate_half(k) * sin
        attn = jnp.einsum('bhqd,bhkd->bhqk', q, k) * scale
        attn_w = jax.nn.softmax(attn, axis=-1)
        out = jnp.einsum('bhqk,bhkd->bhqd', attn_w, v)
        out = out.transpose(0, 2, 1, 3).reshape(B, S, D)
        out = jnp.einsum('bsd,ed->bse', out, Wo) + bo
        return out

    def _L3_ffn_ref(input_emb, W1, b1, W2, b2, Wr, br):
        import jax, jax.numpy as jnp
        import numpy as np
        B, S, D = (4, 512, 256)
        EXP = 4
        H = EXP * D
        E = 8
        TOP_K = 2
        logits = jnp.einsum('bsd,de->bse', input_emb, Wr) + br
        route_w = jax.nn.softmax(logits, axis=-1)
        _, topk_idx = jax.lax.top_k(route_w, TOP_K)
        mask = jax.nn.one_hot(topk_idx, E, dtype=route_w.dtype).sum(-2)
        routed = route_w * mask
        routed = routed / routed.sum(axis=-1, keepdims=True)
        h = jax.nn.relu(jnp.einsum('bsd,edh->ebsh', input_emb, W1) + b1[:, None, None, :])
        expert_out = jnp.einsum('ebsh,ehd->ebsd', h, W2) + b2[:, None, None, :]
        return jnp.einsum('bse,ebsd->bsd', routed, expert_out)
    x = x + _L0_xattn_ref(_layernorm(x, axis=-1), ctx_1024, ctx_1024, L0_xattn_wq, L0_xattn_wk, L0_xattn_wv, L0_xattn_wo)
    x = x + _L0_ffn_ref(_layernorm(x, axis=-1), L0_ffn_w_gate, L0_ffn_w_up, L0_ffn_w_down)
    x = x + _L1_xattn_ref(_layernorm(x, axis=-1), ctx_1024, ctx_1024, L1_xattn_Wq, L1_xattn_bq, L1_xattn_Wk, L1_xattn_bk, L1_xattn_Wv, L1_xattn_bv, L1_xattn_Wo, L1_xattn_bo)
    x = x + _L1_ffn_ref(_layernorm(x, axis=-1), L1_ffn_norm_gamma, L1_ffn_slot_norm_gamma, L1_ffn_slot_embeds, L1_ffn_w1, L1_ffn_b1, L1_ffn_w2, L1_ffn_b2)
    x = x + _L2_xattn_ref(_layernorm(x, axis=-1), ctx_1024, ctx_1024, L2_xattn_Wq, L2_xattn_bq, L2_xattn_Wk, L2_xattn_bk, L2_xattn_Wv, L2_xattn_bv, L2_xattn_Wo, L2_xattn_bo)
    x = x + _L2_ffn_ref(_layernorm(x, axis=-1), L2_ffn_W_r, L2_ffn_W_k, L2_ffn_W_v, L2_ffn_mu_r, L2_ffn_mu_k)
    x = x + _L3_xattn_ref(_layernorm(x, axis=-1), ctx_1024, ctx_1024, L3_xattn_Wq, L3_xattn_bq, L3_xattn_Wk, L3_xattn_bk, L3_xattn_Wv, L3_xattn_bv, L3_xattn_Wo, L3_xattn_bo)
    x = x + _L3_ffn_ref(_layernorm(x, axis=-1), L3_ffn_W1, L3_ffn_b1, L3_ffn_W2, L3_ffn_b2, L3_ffn_Wr, L3_ffn_br)
    return x

_drawn_inputs = setup_inputs


def setup_inputs(seed=0):
    import zlib

    import numpy as np

    out = dict(_drawn_inputs(seed))
    spreads = {'L1_xattn_bq': (0.0, 0.56),
     'L1_xattn_bk': (0.0, 0.8),
     'L1_xattn_bv': (0.0, 0.1),
     'L1_xattn_bo': (0.0, 0.1),
     'L1_ffn_norm_gamma': (1.0, 0.2),
     'L1_ffn_slot_norm_gamma': (1.0, 0.2),
     'L1_ffn_b1': (0.0, 0.411),
     'L1_ffn_b2': (0.0, 0.1),
     'L2_xattn_bq': (0.0, 0.631),
     'L2_xattn_bk': (0.0, 0.8),
     'L2_xattn_bv': (0.0, 0.1),
     'L2_xattn_bo': (0.0, 0.1),
     'L3_xattn_bq': (0.0, 0.677),
     'L3_xattn_bk': (0.0, 0.8),
     'L3_xattn_bv': (0.0, 0.1),
     'L3_xattn_bo': (0.0, 0.1)}
    factors = {'L0_ffn_w_gate': 3.028,
     'L0_ffn_w_up': 2.853,
     'L0_ffn_w_down': 2.879,
     'L2_ffn_W_r': 4.588,
     'L2_ffn_mu_r': 8.0,
     'L2_ffn_mu_k': 2.684,
     'L3_ffn_b1': 8.0,
     'L3_ffn_b2': 8.0,
     'L3_ffn_br': 3.107}
    for name, (base, spread) in spreads.items():
        noise = np.random.default_rng([zlib.crc32(name.encode()), seed]).standard_normal(out[name].shape)
        drawn = base * np.exp(spread * noise) if base else spread * noise
        out[name] = jnp.asarray(drawn.astype(out[name].dtype))
    for name, factor in factors.items():
        out[name] = (out[name] * factor).astype(out[name].dtype)
    return out
```

```python
from contextlib import ExitStack

import numpy as np

import concourse.bass as bass
from concourse import mybir

F32 = mybir.dt.float32
BF16 = mybir.dt.bfloat16
F16 = mybir.dt.float16
U32 = mybir.dt.uint32
I32 = mybir.dt.int32
ALU = mybir.AluOpType
ACT = mybir.ActivationFunctionType
AX = mybir.AxisListType
RMAX = bass.bass_isa.ReduceOp.max

B, L, D = 16, 128, 256
P = 128
C = D // P
H, DH = 16, 16
HC = H // C
LN_EPS = 1e-5
WINDOW = 64
PAIRS = B // 2 - 1


def enough(eng, sem, value):
    if not isinstance(value, int) or value > 0:
        eng.wait_ge(sem, value)


class Links:

    def __init__(self, eng, sem, per, n):
        self.eng, self.sem, self.per, self.base, self.k = eng, sem, per, n * per, 0

    def __call__(self, ins):
        self.k += 1
        ins.then_inc(self.sem, 1)
        self.eng.wait_ge(self.sem, self.base + self.k)

    def done(self):
        assert self.k == self.per, (self.k, self.per)


class Tiles:

    def __init__(self, nc, ctx, name):
        self.nc, self.ctx, self.name = nc, ctx, name
        self.sems = []
        ctx.callback(self.clear)

    def clear(self):
        self.nc.clear_and_free_semaphores(self.sems)
        self.nc.all_engine_barrier()

    def sb(self, name, shape, dt=F32):
        return self.ctx.enter_context(self.nc.sbuf_tensor(f"{self.name}_{name}", shape, dt))

    def ps(self, name, shape, dt=F32):
        return self.ctx.enter_context(self.nc.psum_tensor(f"{self.name}_{name}", shape, dt))

    def sem(self, name):
        self.sems.append(self.nc.alloc_semaphore(name=f"{self.name}_{name}"))
        return self.sems[-1]


def walk(eng, step):
    step(0, 0, True, True)
    step(1, 1, True, True)
    with eng.Fori(1, PAIRS) as j:
        step(2 * j, 0, True, True)
        step(2 * j + 1, 1, True, True)
    step(B - 2, 0, True, False)
    step(B - 1, 1, False, False)


def batch_stats(dve, X, stats, n):
    return dve.bn_stats(stats[:, n, :], X[:, n, :])


RSQRT_MAGIC = float(0x5F3759DF)
NEWTON_STEPS = 3


def layernorm_begin(dve, t):
    link = Links(dve, t.ln_link, 4 + 3 * NEWTON_STEPS, 0)
    for n in range(B):
        last = dve.bn_aggr(t.meanvar[:, n, :], t.stats[:, n, :])
    link(last)
    link(dve.tensor_scalar(t.ln_var[:], t.meanvar[:, :, 1:2], LN_EPS, None, ALU.add))
    link(dve.tensor_scalar(t.ln_half[:], t.ln_var[:].bitcast(I32), 1, None, ALU.logical_shift_right))
    link(dve.tensor_scalar(t.rstd[:].bitcast(I32), t.ln_half[:], -1.0, RSQRT_MAGIC, ALU.mult, ALU.add))
    for _ in range(NEWTON_STEPS):
        link(dve.scalar_tensor_tensor(t.ln_tmp[:], t.rstd[:], -0.5, t.rstd[:], ALU.mult, ALU.mult))
        link(dve.tensor_tensor(t.ln_tmp[:], t.ln_tmp[:], t.ln_var[:], ALU.mult))
        link(dve.scalar_tensor_tensor(t.rstd[:], t.ln_tmp[:], 1.5, t.rstd[:], ALU.add, ALU.mult))
    link.done()


def layernorm_apply(dve, t, n, parity):
    enough(dve, t.xn_used, n - 1)
    dve.tensor_scalar(t.xn[:, parity, :], t.X[:, n, :], t.meanvar[:, n, 0:1], t.rstd[:, n, :],
                      ALU.subtract, ALU.mult).then_inc(t.xn_ready, 1)


def layernorm_tiles(t, env):
    t.X, t.stats = env.X, env.stats
    t.meanvar = t.sb("meanvar", [P, B, 2])
    t.ln_var = t.sb("ln_var", [P, B, 1])
    t.ln_half = t.sb("ln_half", [P, B, 1], I32)
    t.ln_tmp = t.sb("ln_tmp", [P, B, 1])
    t.rstd = t.sb("rstd", [P, B, 1])
    t.xn = t.sb("xn", [P, 2, D])
    t.ln_link = t.sem("ln_link")
    t.xn_ready = t.sem("xn_ready")


def add_to_x(dve, t, n, change, change_made, added):
    link = Links(dve, t.add_link, 1, n)
    dve.wait_ge(change_made, n + 1)
    link(dve.tensor_tensor(t.X[:, n, :], t.X[:, n, :], change, ALU.add))
    link.done()
    batch_stats(dve, t.X, t.stats, n).then_inc(added, 1)


def load_context(sp, t, n, parity):
    enough(sp, t.ctx_used, n - 1)
    sp.dma_start(t.ctx_in[:, parity, :], t.ctx_dram[n]).then_inc(t.ctx_ready[parity], 16)


def context_tiles(t, ctx_dram):
    t.ctx_dram = ctx_dram
    t.ctx_in = t.sb("ctx_in", [P, 2, D])
    t.ctx_ready = [t.sem(f"ctx_ready{i}") for i in range(2)]


def context_count(n, parity):
    return 8 * (n - parity) + 16


def autocorrelation(nc, env):
    A, K = env.inputs, env.consts
    with ExitStack() as ctx:
        t = Tiles(nc, ctx, "ac")
        layernorm_tiles(t, env)
        t.add_link = t.sem("add_link")
        context_tiles(t, A["ctx_1024"])
        FX = 4 * P
        wq, wk, wv, wo = (t.sb(f"w{n}", [P, C, D]) for n in "qkvo")
        dft = t.sb("dft", [P, 3 * P])
        idft = t.sb("idft", [P, 2, L])
        head_mask = t.sb("head_mask", [P, HC, DH])
        iota = t.sb("iota", [P, DH])
        row_mod = t.sb("row_mod", [P, 1])
        specT = t.sb("specT", [P, 2, C, FX])
        qv = t.sb("qv", [P, 2, 2 * D])
        prod = t.sb("prod", [P, 2, 2, D])
        corr = t.sb("corr", [P, 2, C, L])
        top = t.sb("top", [P, C, 8])
        lag = t.sb("lag", [P, C, 8], U32)
        src_f = t.sb("src_f", [P, C, 4])
        src_i = t.sb("src_i", [P, C, 4], I32)
        src = t.sb("src", [P, C, 4], I32)
        below = t.sb("below", [P, C, 4])
        ew = t.sb("ew", [P, C, 4])
        ew_sum = t.sb("ew_sum", [P, C])
        ew_inv = t.sb("ew_inv", [P, C])
        hit = t.sb("hit", [P, C, DH, 4])
        hit_w = t.sb("hit_w", [P, C, DH, 4])
        mix = t.sb("mix", [P, C, DH])
        mix_n = t.sb("mix_n", [P, C, DH])
        mix_block = t.sb("mix_block", [P, 2, C, HC, DH])
        mixT = t.sb("mixT", [P, 2, C, P])
        rolled = t.sb("rolled", [P, 2, 2, DH, H // 2])
        ident = t.sb("ident", [P, P])

        ps_spec = t.ps("ps_spec", [P, C, FX])
        ps_qv = t.ps("ps_qv", [P, 2 * D])
        ps_k = t.ps("ps_k", [P, 2, D])
        ps_corr = t.ps("ps_corr", [P, C, L])
        ps_mixT = t.ps("ps_mixT", [P, C, P])
        ps_rolled = t.ps("ps_rolled", [P, H // 2, 2, DH])
        ps_out = t.ps("ps_out", [P, D])

        consts_in = t.sem("consts_in")
        spec_made, spec_ready = t.sem("spec_made"), t.sem("spec_ready")
        t.xn_used = t.ctx_used = spec_made
        qkv_made = t.sem("qkv_made")
        qv_ready = t.sem("qv_ready")
        prod_ready = t.sem("prod_ready")
        corr_made, corr_ready = t.sem("corr_made"), t.sem("corr_ready")
        top_link = t.sem("top_link")
        below_ready = t.sem("below_ready")
        ew_ready = t.sem("ew_ready")
        mix_ready = t.sem("mix_ready")
        mixT_made, mixT_ready = t.sem("mixT_made"), t.sem("mixT_ready")
        rolled_made, rolled_ready = t.sem("rolled_made"), t.sem("rolled_ready")
        out_made, out_added = t.sem("out_made"), t.sem("out_added")
        TOP_LINKS = 9

        block = ctx.enter_context(nc.Block())

        @block.sync
        def _(sp):
            for w, name in ((wq, "wq"), (wk, "wk"), (wv, "wv"), (wo, "wo")):
                sp.dma_start(w[:], A[f"L0_xattn_{name}"].rearrange("(c p) n -> p c n", p=P)).then_inc(consts_in, 16)
            for tile, name in ((dft, "dft"), (iota, "iota"), (row_mod, "row_mod"), (ident, "ident")):
                sp.dma_start(tile[:], K[name]).then_inc(consts_in, 16)
            sp.dma_start(idft[:], K["idft"].rearrange("p (a n) -> p a n", a=2)).then_inc(consts_in, 16)
            sp.dma_start(head_mask[:], K["head_mask"].rearrange("p (a n) -> p a n", a=HC)).then_inc(consts_in, 16)
            load_context(sp, t, 0, 0)
            load_context(sp, t, 1, 1)

            def step(n, parity, one_ahead, two_ahead):
                if two_ahead:
                    load_context(sp, t, n + 2, parity)
            walk(sp, step)
        CONSTS = 10 * 16

        @block.tensor
        def _(pe):
            def spectra(n, parity):
                pe.wait_ge(t.xn_ready, n + 1)
                pe.wait_ge(t.ctx_ready[parity], context_count(n, parity))
                enough(pe, spec_ready, n)
                for c in range(C):
                    cs = slice(c * P, (c + 1) * P)
                    pe.matmul(ps_spec[:, c, 0:P], t.xn[:, parity, cs], dft[:, 0:P], start=True, stop=True)
                    last = pe.matmul(ps_spec[:, c, P:FX], t.ctx_in[:, parity, cs], dft[:], start=True, stop=True)
                last.then_inc(spec_made, 1)

            def project(n, parity):
                pe.wait_ge(spec_ready, n + 1)
                enough(pe, prod_ready, n)
                for c in range(C):
                    pe.matmul(ps_qv[:, 0:D], specT[:, parity, c, 0:P], wq[:, c, :], start=c == 0, stop=c == C - 1)
                for m in range(C):
                    for c in range(C):
                        pe.matmul(ps_qv[:, D + m * P:D + (m + 1) * P], wv[:, c, m * P:(m + 1) * P],
                                  specT[:, parity, c, 2 * P:3 * P], start=c == 0, stop=c == C - 1)
                for a, at in ((0, P), (1, 3 * P)):
                    for c in range(C):
                        last = pe.matmul(ps_k[:, a, :], specT[:, parity, c, at:at + P], wk[:, c, :],
                                         start=c == 0, stop=c == C - 1)
                last.then_inc(qkv_made, 1)

            def correlate(n, parity):
                pe.wait_ge(prod_ready, n + 1)
                enough(pe, corr_ready, n)
                for c in range(C):
                    for a in range(2):
                        last = pe.matmul(ps_corr[:, c, :], prod[:, parity, a, c * P:(c + 1) * P], idft[:, a, :],
                                         start=a == 0, stop=a == 1)
                last.then_inc(corr_made, 1)

            def turn_mix(n, parity):
                pe.wait_ge(mix_ready, n + 1)
                enough(pe, mixT_ready, n)
                for c in range(C):
                    last = pe.transpose(ps_mixT[:, c, :], mix_block[:, parity, c].rearrange("p h d -> p (h d)"),
                                        ident[:])
                last.then_inc(mixT_made, 1)

            def roll_values(n, parity):
                pe.wait_ge(mixT_ready, n + 1)
                enough(pe, rolled_ready, n)
                for c in range(C):
                    last = pe.matmul(ps_rolled[:, c * HC // 2:(c + 1) * HC // 2].rearrange("p k a d -> p (k a d)"),
                                     qv[:, parity, D + c * P:D + (c + 1) * P], mixT[:, parity, c, :],
                                     start=True, stop=True)
                last.then_inc(rolled_made, 1)

            def output(n, parity):
                pe.wait_ge(rolled_ready, n + 1)
                enough(pe, out_added, n)
                for a in range(2):
                    last = pe.matmul(ps_out[:], rolled[:, parity, a].rearrange("p d k -> p (d k)"), wo[:, a, :],
                                     start=a == 0, stop=a == 1)
                last.then_inc(out_made, 1)

            pe.wait_ge(consts_in, CONSTS)
            spectra(0, 0)
            project(0, 0)
            correlate(0, 0)

            def step(n, parity, one_ahead, two_ahead):
                if one_ahead:
                    spectra(n + 1, 1 - parity)
                    project(n + 1, 1 - parity)
                turn_mix(n, parity)
                if one_ahead:
                    correlate(n + 1, 1 - parity)
                roll_values(n, parity)
                output(n, parity)
            walk(pe, step)

        @block.scalar
        def _(act):
            def spectra_out(n, parity):
                act.wait_ge(spec_made, n + 1)
                enough(act, qkv_made, n - 1)
                act.activation(specT[:, parity], ps_spec[:], ACT.Copy).then_inc(spec_ready, 1)

            def qv_out(n, parity):
                act.wait_ge(qkv_made, n + 1)
                enough(act, rolled_made, n - 1)
                act.activation(qv[:, parity], ps_qv[:], ACT.Copy).then_inc(qv_ready, 1)

            def correlation_out(n, parity):
                act.wait_ge(corr_made, n + 1)
                enough(act, mix_ready, n - 1)
                act.activation(corr[:, parity], ps_corr[:], ACT.Copy).then_inc(corr_ready, 1)

            def weights(n, parity):
                act.wait_ge(below_ready, n + 1)
                enough(act, mix_ready, n)
                act.activation(ew[:], below[:], ACT.Exp).then_inc(ew_ready, 1)

            def mixT_out(n, parity):
                act.wait_ge(mixT_made, n + 1)
                enough(act, rolled_made, n - 1)
                act.activation(mixT[:, parity], ps_mixT[:], ACT.Copy).then_inc(mixT_ready, 1)

            def rolled_out(n, parity):
                act.wait_ge(rolled_made, n + 1)
                enough(act, out_made, n - 1)
                act.activation(rolled[:, parity], ps_rolled[:].rearrange("p k a d -> p a d k"),
                               ACT.Copy).then_inc(rolled_ready, 1)

            spectra_out(0, 0)
            qv_out(0, 0)
            correlation_out(0, 0)

            def step(n, parity, one_ahead, two_ahead):
                if one_ahead:
                    spectra_out(n + 1, 1 - parity)
                weights(n, parity)
                if one_ahead:
                    qv_out(n + 1, 1 - parity)
                mixT_out(n, parity)
                if one_ahead:
                    correlation_out(n + 1, 1 - parity)
                rolled_out(n, parity)
            walk(act, step)

        @block.vector
        def _(dve):
            def products(n, parity):
                dve.wait_ge(qv_ready, n + 1)
                enough(dve, corr_made, n - 1)
                dve.tensor_tensor(prod[:, parity], qv[:, parity, 0:D].unsqueeze(1).to_broadcast([P, 2, D]), ps_k[:],
                                  ALU.mult).then_inc(prod_ready, 1)

            def make_mix(n, parity):
                link = Links(dve, top_link, TOP_LINKS, n)
                dve.max(top[:, 0, :], corr[:, parity, 0, :])
                link(dve.max(top[:, 1, :], corr[:, parity, 1, :]))
                dve.tensor_tensor(below[:], top[:, :, 0:4], top[:, :, 0:1].to_broadcast([P, C, 4]),
                                  ALU.subtract).then_inc(below_ready, 1)
                dve.max_index(lag[:, 0, :], top[:, 0, :], corr[:, parity, 0, :])
                link(dve.max_index(lag[:, 1, :], top[:, 1, :], corr[:, parity, 1, :]))
                link(dve.tensor_scalar(src_f[:], lag[:, :, 0:4], -1.0, row_mod[:, 0:1], ALU.mult, ALU.add))
                link(dve.tensor_copy(src_i[:], src_f[:]))
                link(dve.tensor_scalar(src[:], src_i[:], DH - 1, None, ALU.bitwise_and))
                link(dve.tensor_tensor(hit[:], iota[:].unsqueeze(1).unsqueeze(3).to_broadcast([P, C, DH, 4]),
                                       src[:].unsqueeze(2).to_broadcast([P, C, DH, 4]), ALU.is_equal))
                dve.wait_ge(ew_ready, n + 1)
                dve.tensor_tensor(hit_w[:], hit[:], ew[:].unsqueeze(2).to_broadcast([P, C, DH, 4]), ALU.mult)
                link(dve.tensor_reduce(ew_sum[:], ew[:], AX.X, ALU.add))
                dve.tensor_reduce(mix[:], hit_w[:], AX.X, ALU.add)
                link(dve.reciprocal(ew_inv[:], ew_sum[:]))
                link(dve.tensor_tensor(mix_n[:], mix[:], ew_inv[:].unsqueeze(2).to_broadcast([P, C, DH]), ALU.mult))
                enough(dve, mixT_made, n - 1)
                for c in range(C):
                    last = dve.tensor_tensor(mix_block[:, parity, c], head_mask[:],
                                             mix_n[:, c, :].unsqueeze(1).to_broadcast([P, HC, DH]), ALU.mult)
                last.then_inc(mix_ready, 1)
                link.done()

            dve.wait_ge(consts_in, CONSTS)
            layernorm_begin(dve, t)
            for n in range(2):
                layernorm_apply(dve, t, n, n)
            products(0, 0)

            def step(n, parity, one_ahead, two_ahead):
                dve.wait_ge(corr_ready, n + 1)
                if two_ahead:
                    layernorm_apply(dve, t, n + 2, parity)
                make_mix(n, parity)
                if one_ahead:
                    products(n + 1, 1 - parity)
                add_to_x(dve, t, n, ps_out[:], out_made, out_added)
            walk(dve, step)


HUGE_NEGATIVE = -1e30
R = 4
HR = H // R
BANK_PAIRS = ((0, 1), (2, 3))


def attention(nc, env, layer, windowed=False, rotary=False):
    A, K = env.inputs, env.consts
    SCALE = float(DH) ** -0.5
    with ExitStack() as ctx:
        t = Tiles(nc, ctx, f"at{layer}")
        layernorm_tiles(t, env)
        context_tiles(t, A["ctx_1024"])
        t.add_link = t.sem("add_link")
        w_raw = t.sb("w_raw", [P, 4, C, D])
        wT = t.sb("wT", [P, 4, C, D])
        ident = t.sb("ident", [P, P])
        ident_b = t.sb("ident_b", [P, P], BF16)
        slot_sel = t.sb("slot_sel", [P, R, 4, P], BF16)
        head_of_row = t.sb("head_of_row", [P, HC])
        bias_cols = t.sb("bias_cols", [P, 2, C])
        bv = t.sb("bv", [P, D])
        bo = t.sb("bo", [P, D])
        xcT = t.sb("xcT", [P, 2, 2, C, P])
        qT = t.sb("qT", [P, C, P])
        kT = t.sb("kT", [P, 2, C, P])
        qz = t.sb("qz", [P, 2, C, HC, P])
        qzb = t.sb("qzb", [P, C, HC, P], BF16)
        kb = t.sb("kb", [P, C, P], BF16)
        v1 = t.sb("v1", [P, 2, H, 32])
        neg_max = t.sb("neg_max", [P, R, 32], BF16)
        neg_maxT = t.sb("neg_maxT", [P, P], BF16)
        probT = t.sb("probT", [P, R, HR, P])
        sumsT = t.sb("sumsT", [P, HR, P])
        inv_sum = t.sb("inv_sum", [P, HR, R, 1])
        att = t.sb("att", [P, D])
        attT = t.sb("attT", [P, C, P])
        change = t.sb("change", [P, D])

        ps_sc = t.ps("ps_sc", [P, R, 4, P])
        ps_a = t.ps("ps_a", [P, 2, C, P])
        ps_qk = t.ps("ps_qk", [P, 2, C, P])
        ps_d = t.ps("ps_d", [P, 4, P])
        ps_sums = ps_d[:].rearrange("p j (r i) -> p j r i", r=R)
        ps_v = ps_qk[:, 0].rearrange("p c l -> p (c l)")
        ps_max = ps_a[:, 0, 0, 0:P // 2].bitcast(BF16)
        flat = "p c l -> p (c l)"

        consts_in, weights_in = t.sem("consts_in"), t.sem("weights_in")
        made_consts = t.sem("made_consts")
        w_turned, w_ready = t.sem("w_turned"), t.sem("w_ready")
        turned, xcT_ready = t.sem("turned"), t.sem("xcT_ready")
        qk_made, q_ready, k_ready, qz_ready = (t.sem(n) for n in ("qk_made", "q_ready", "k_ready", "qz_ready"))
        v_made, v_ready = t.sem("v_made"), t.sem("v_ready")
        scores_made, max_ready = t.sem("scores_made"), t.sem("max_ready")
        max_turned, maxT_ready = t.sem("max_turned"), t.sem("maxT_ready")
        shifted_made, prob_ready = t.sem("shifted_made"), t.sem("prob_ready")
        qzb_ready, kb_ready = t.sem("qzb_ready"), t.sem("kb_ready")
        pv_made, sumsT_ready, sums_turned = t.sem("pv_made"), t.sem("sumsT_ready"), t.sem("sums_turned")
        att_link, att_ready = t.sem("att_link"), t.sem("att_ready")
        att_turned, attT_ready = t.sem("att_turned"), t.sem("attT_ready")
        out_made, out_taken, out_added = t.sem("out_made"), t.sem("out_taken"), t.sem("out_added")
        t.xn_used = t.ctx_used = turned
        consts = [(ident, "ident"), (head_of_row, "head_of_row")]
        if windowed:
            window = t.sb("window", [P, P])
            window_b = t.sb("window_b", [P, P], BF16)
            consts.append((window, "window"))
        if rotary:
            cosT, sinT, rot = t.sb("cosT", [P, P]), t.sb("sinT", [P, P]), t.sb("rot", [P, P])
            consts += [(cosT, "cosT"), (sinT, "sinT"), (rot, "rot")]
            wT_rot = t.sb("wT_rot", [P, 2, C, D])
            bias_rot = t.sb("bias_rot", [P, 2, C])
            ps_rot = t.ps("ps_rot", [P, 2, C, P])
            by_cos = t.sb("by_cos", [P, 2, C, P])
            by_sin = t.sb("by_sin", [P, 2, C, P])
            rope_link = t.sem("rope_link")
        CONSTS = 16 * (len(consts) + 4)
        MADE = 3 + windowed
        W_TURNED = 4 + (3 if rotary else 0)
        block = ctx.enter_context(nc.Block())

        @block.sync
        def _(sp):
            for i, name in enumerate(("Wq", "Wk", "Wv", "Wo")):
                sp.dma_start(w_raw[:, i], A[f"L{layer}_xattn_{name}"].rearrange("(c p) n -> p c n", p=P)).then_inc(weights_in, 16)
            for tile, name in consts:
                sp.dma_start(tile[:], K[name]).then_inc(consts_in, 16)
            for i, name in enumerate(("bq", "bk")):
                sp.dma_start(bias_cols[:, i], A[f"L{layer}_xattn_{name}"].rearrange("(c p) -> p c", p=P),
                             allow_slow_non_contiguous=True).then_inc(consts_in, 16)
            for tile, name in ((bv, "bv"), (bo, "bo")):
                sp.dma_start(tile[:], A[f"L{layer}_xattn_{name}"].unsqueeze(0).to_broadcast([P, D])).then_inc(consts_in, 16)
            load_context(sp, t, 0, 0)
            load_context(sp, t, 1, 1)

            def step(n, parity, one_ahead, two_ahead):
                if two_ahead:
                    load_context(sp, t, n + 2, parity)
            walk(sp, step)

        @block.tensor
        def _(pe):
            def turn_weights():
                pe.wait_ge(consts_in, CONSTS)
                pe.wait_ge(weights_in, 64)
                for i in range(4):
                    for k in range(C):
                        for o in range(C):
                            last = pe.transpose(ps_sc[:, i].rearrange("p a l -> p (a l)")[:, (k * C + o) * P:(k * C + o + 1) * P],
                                                w_raw[:, i, o, k * P:(k + 1) * P], ident[:])
                    last.then_inc(w_turned, 1)
                if rotary:
                    for i, ps in enumerate((ps_qk, ps_rot)):
                        for k in range(C):
                            for o in range(C):
                                last = pe.matmul(ps[:, k, o], w_raw[:, i, o, k * P:(k + 1) * P], rot[:], start=True, stop=True)
                        last.then_inc(w_turned, 1)
                    pe.matmul(ps_a[:, 0, 0, 0:4], rot[:], bias_cols[:].rearrange("p a c -> p (a c)"),
                              start=True, stop=True).then_inc(w_turned, 1)

            def turn_inputs(n, parity):
                pe.wait_ge(t.xn_ready, n + 1)
                pe.wait_ge(t.ctx_ready[parity], context_count(n, parity))
                enough(pe, xcT_ready, n)
                enough(pe, out_taken, n - 3)
                for c in range(C):
                    cs = slice(c * P, (c + 1) * P)
                    pe.transpose(ps_a[:, 0, c], t.xn[:, parity, cs], ident[:])
                    last = pe.transpose(ps_a[:, 1, c], t.ctx_in[:, parity, cs], ident[:])
                last.then_inc(turned, 1)

            def project_heads(n, parity):
                pe.wait_ge(xcT_ready, n + 1)
                enough(pe, v_ready, n)
                for i in range(2):
                    for o in range(C):
                        for k in range(C):
                            last = pe.matmul(ps_qk[:, i, o], wT[:, i, k, o * P:(o + 1) * P], xcT[:, parity, i, k],
                                             start=k == 0, stop=k == C - 1)
                        if rotary:
                            for k in range(C):
                                last = pe.matmul(ps_rot[:, i, o], wT_rot[:, i, k, o * P:(o + 1) * P], xcT[:, parity, i, k],
                                                 start=k == 0, stop=k == C - 1)
                last.then_inc(qk_made, 1)

            def project_values(n, parity):
                pe.wait_ge(q_ready, n + 1)
                pe.wait_ge(k_ready, n + 1)
                for k in range(C):
                    last = pe.matmul(ps_v, xcT[:, parity, 1, k], wT[:, 2, k], start=k == 0, stop=k == C - 1)
                last.then_inc(v_made, 1)

            def add_window(banks):
                for r in banks:
                    pe.matmul(ps_sc[:, r], ident_b[:], window_b[:].unsqueeze(1).to_broadcast([P, 4, P]),
                              start=True, stop=False, skip_group_check=True)

            def scores(n):
                pe.wait_ge(kb_ready, n + 1)
                pe.wait_ge(qzb_ready, n + 1)
                for c, banks in enumerate(BANK_PAIRS):
                    enough(pe, prob_ready, R * (n - 1) + banks[1] + 1)
                    if windowed:
                        add_window(banks)
                    for i in range(HC):
                        last = pe.matmul(ps_sc[:, banks[i // HR], i % HR], qzb[:, c, i], kb[:, c],
                                         start=not windowed, stop=True, skip_group_check=windowed)
                    last.then_inc(scores_made, 1)

            def turn_maxima(n, inputs):
                pe.wait_ge(max_ready, 2 * (n + 1))
                pe.wait_ge(xcT_ready, inputs)
                enough(pe, out_taken, n - 2)
                pe.transpose(ps_max, neg_max[:].rearrange("p r i -> p (r i)"), ident_b[:]).then_inc(max_turned, 1)

            def shifted_scores(n, parity, c):
                pe.wait_ge(maxT_ready, n + 1)
                if windowed:
                    add_window(BANK_PAIRS[c])
                for half, r in enumerate(BANK_PAIRS[c]):
                    pe.matmul(ps_sc[:, r], kT[:, parity, c], qz[:, parity, c, HR * half:HR * (half + 1)],
                              start=not windowed, stop=False, skip_group_check=True)
                    for j in range(HR):
                        last = pe.matmul(ps_sc[:, r, j], slot_sel[:, r, j], neg_maxT[:],
                                         start=False, stop=True, skip_group_check=True)
                last.then_inc(shifted_made, 1)

            def weigh_values(n, parity):
                pe.wait_ge(prob_ready, R * (n + 1))
                pe.wait_ge(v_ready, n + 1)
                enough(pe, att_ready, n)
                for j in range(HR):
                    for r in range(R):
                        last = pe.matmul(ps_d[32 * r:32 * r + 32, j], v1[:, parity, HR * r + j], probT[:, r, j],
                                         start=True, stop=True)
                last.then_inc(pv_made, 1)

            def turn_sums(n):
                pe.wait_ge(sumsT_ready, n + 1)
                for j in range(HR):
                    last = pe.transpose(ps_d[:, j], sumsT[:, j], ident[:])
                last.then_inc(sums_turned, 1)

            def turn_attended(n):
                pe.wait_ge(att_ready, n + 1)
                enough(pe, out_taken, n)
                for c in range(C):
                    last = pe.transpose(ps_a[:, 0, c], att[:, c * P:(c + 1) * P], ident[:])
                last.then_inc(att_turned, 1)

            def output(n):
                pe.wait_ge(attT_ready, n + 1)
                for c in range(C):
                    last = pe.matmul(ps_a[:, 0].rearrange(flat), attT[:, c], wT[:, 3, c], start=c == 0, stop=c == C - 1)
                last.then_inc(out_made, 1)

            turn_weights()
            pe.wait_ge(w_ready, W_TURNED)
            pe.wait_ge(made_consts, MADE)
            turn_inputs(0, 0)
            project_heads(0, 0)
            project_values(0, 0)

            def step(n, parity, one_ahead, two_ahead):
                behind = not (isinstance(n, int) and n == 0)
                two_behind = not (isinstance(n, int) and n <= 1)
                if one_ahead:
                    turn_inputs(n + 1, 1 - parity)
                scores(n)
                if one_ahead:
                    project_heads(n + 1, 1 - parity)
                if behind:
                    weigh_values(n - 1, 1 - parity)
                turn_maxima(n, n + 2 if one_ahead else B)
                if one_ahead:
                    project_values(n + 1, 1 - parity)
                shifted_scores(n, parity, 0)
                if two_behind:
                    turn_attended(n - 2)
                if behind:
                    turn_sums(n - 1)
                shifted_scores(n, parity, 1)
                if two_behind:
                    output(n - 2)
            walk(pe, step)
            turn_attended(B - 2)
            weigh_values(B - 1, 1)
            output(B - 2)
            turn_sums(B - 1)
            turn_attended(B - 1)
            output(B - 1)

        @block.scalar
        def _(act):
            def inputs_out(n, parity):
                act.wait_ge(turned, n + 1)
                enough(act, v_made, n - 1)
                act.activation(xcT[:, parity], ps_a[:], ACT.Copy).then_inc(xcT_ready, 1)

            def heads_out(n, parity):
                act.wait_ge(qk_made, n + 1)
                enough(act, qz_ready, n)
                for c in range(C):
                    last = act.activation(qT[:, c], ps_qk[:, 0, c], ACT.Identity, bias=bias_cols[:, 0, c:c + 1])
                last.then_inc(q_ready, 1)
                enough(act, shifted_made, 2 * (n - 1))
                for c in range(C):
                    last = act.activation(kT[:, parity, c], ps_qk[:, 1, c], ACT.Identity, bias=bias_cols[:, 1, c:c + 1])
                last.then_inc(k_ready, 1)

            def round_heads(n, parity):
                act.wait_ge(qz_ready, n + 1)
                enough(act, scores_made, 2 * n)
                act.activation(qzb[:], qz[:, parity], ACT.Copy).then_inc(qzb_ready, 1)

            def maxima_out(n):
                act.wait_ge(max_turned, n + 1)
                enough(act, shifted_made, 2 * n)
                act.activation(neg_maxT[:], ps_max, ACT.Copy).then_inc(maxT_ready, 1)

            def sums_out(n):
                act.wait_ge(pv_made, n + 1)
                enough(act, sums_turned, n)
                act.activation(sumsT[:], ps_d[:], ACT.Copy).then_inc(sumsT_ready, 1)

            def exponentials(n, c):
                act.wait_ge(shifted_made, 2 * n + c + 1)
                enough(act, pv_made, n)
                for r in BANK_PAIRS[c]:
                    act.activation(probT[:, r], ps_sc[:, r], ACT.Exp, scale=SCALE).then_inc(prob_ready, 1)

            def attended_out(n):
                act.wait_ge(att_turned, n + 1)
                enough(act, out_made, n)
                act.activation(attT[:], ps_a[:, 0], ACT.Copy).then_inc(attT_ready, 1)

            for i in range(4):
                act.wait_ge(w_turned, i + 1)
                act.activation(wT[:, i].rearrange("p c n -> p (c n)"), ps_sc[:, i].rearrange("p a l -> p (a l)"),
                               ACT.Copy).then_inc(w_ready, 1)
            if rotary:
                for i, ps in enumerate((ps_qk, ps_rot)):
                    act.wait_ge(w_turned, 5 + i)
                    act.activation(wT_rot[:, i].rearrange("p c n -> p (c n)"), ps[:].rearrange("p a c l -> p (a c l)"),
                                   ACT.Copy).then_inc(w_ready, 1)
                act.wait_ge(w_turned, 7)
                act.activation(bias_rot[:].rearrange("p a c -> p (a c)"), ps_a[:, 0, 0, 0:4], ACT.Copy).then_inc(w_ready, 1)
            act.wait_ge(made_consts, MADE)
            inputs_out(0, 0)
            if not rotary:
                heads_out(0, 0)
            round_heads(0, 0)

            def step(n, parity, one_ahead, two_ahead):
                behind = not (isinstance(n, int) and n == 0)
                two_behind = not (isinstance(n, int) and n <= 1)
                if one_ahead:
                    inputs_out(n + 1, 1 - parity)
                    if not rotary:
                        heads_out(n + 1, 1 - parity)
                maxima_out(n)
                if behind:
                    sums_out(n - 1)
                if one_ahead:
                    round_heads(n + 1, 1 - parity)
                exponentials(n, 0)
                if two_behind:
                    attended_out(n - 2)
                exponentials(n, 1)
            walk(act, step)
            attended_out(B - 2)
            sums_out(B - 1)
            attended_out(B - 1)

        @block.vector
        def _(dve):
            def prepare():
                dve.memset(neg_max[:], 0.0).then_inc(made_consts, 1)
                dve.memset(v1[:], 1.0).then_inc(made_consts, 1)
                dve.wait_ge(consts_in, CONSTS)
                if windowed:
                    dve.tensor_copy(window_b[:], window[:]).then_inc(made_consts, 1)
                dve.tensor_copy(ident_b[:], ident[:])
                dve.tensor_copy(slot_sel[:], ident[:].rearrange("p (r i) -> p r i", r=R)[:, :, 0:4].unsqueeze(3)
                                .to_broadcast([P, R, 4, P])).then_inc(made_consts, 1)
                dve.wait_ge(made_consts, MADE)
                if rotary:
                    dve.wait_ge(w_ready, W_TURNED)

            def rope(n, parity):
                link = Links(dve, rope_link, 1, n)
                dve.wait_ge(qk_made, n + 1)
                for i in range(2):
                    for c in range(C):
                        dve.scalar_tensor_tensor(by_cos[:, i, c], ps_qk[:, i, c], bias_cols[:, i, c:c + 1], cosT[:], ALU.add, ALU.mult)
                        last = dve.scalar_tensor_tensor(by_sin[:, i, c], ps_rot[:, i, c], bias_rot[:, i, c:c + 1], sinT[:], ALU.add, ALU.mult)
                link(last)
                link.done()
                enough(dve, shifted_made, 2 * (n - 1))
                dve.tensor_tensor(kT[:, parity], by_cos[:, 1], by_sin[:, 1], ALU.add).then_inc(k_ready, 1)
                enough(dve, qz_ready, n)
                dve.tensor_tensor(qT[:], by_cos[:, 0], by_sin[:, 0], ALU.add).then_inc(q_ready, 1)

            def spread_heads(n, parity):
                dve.wait_ge(q_ready, n + 1)
                enough(dve, shifted_made, 2 * (n - 1))
                dve.tensor_tensor(qz[:, parity], qT[:].unsqueeze(2).to_broadcast([P, C, HC, P]),
                                  head_of_row[:].unsqueeze(1).unsqueeze(3).to_broadcast([P, C, HC, P]),
                                  ALU.mult).then_inc(qz_ready, 1)
                dve.wait_ge(k_ready, n + 1)
                enough(dve, scores_made, 2 * n)
                dve.tensor_copy(kb[:], kT[:, parity]).then_inc(kb_ready, 1)

            def values_out(n, parity):
                dve.wait_ge(v_made, n + 1)
                enough(dve, pv_made, n - 1)
                dve.tensor_tensor(v1[:, parity, :, 0:DH], ps_v.rearrange("p (h d) -> p h d", d=DH),
                                  bv[:].rearrange("p (h d) -> p h d", d=DH), ALU.add).then_inc(v_ready, 1)

            def maxima(n):
                for pair, banks in enumerate(BANK_PAIRS):
                    bs = slice(banks[0], banks[1] + 1)
                    dve.wait_ge(scores_made, 2 * n + pair + 1)
                    enough(dve, max_turned, n)
                    dve.tensor_reduce(neg_max[:, bs, 0:4], ps_sc[:, bs], AX.X, ALU.max, negate=True).then_inc(max_ready, 1)

            def normalise(n):
                link = Links(dve, att_link, 1, n)
                dve.wait_ge(sums_turned, n + 1)
                link(dve.reciprocal(inv_sum[:], ps_sums[:, :, :, DH:DH + 1]))
                link.done()
                enough(dve, att_turned, n)
                dve.tensor_tensor(att[:].rearrange("p (r j d) -> p j r d", r=R, j=HR), ps_sums[:, :, :, 0:DH],
                                  inv_sum[:].to_broadcast([P, HR, R, DH]), ALU.mult).then_inc(att_ready, 1)

            def add_output(n):
                link = Links(dve, out_taken, 1, n)
                dve.wait_ge(out_made, n + 1)
                link(dve.tensor_tensor(change[:], ps_a[:, 0].rearrange(flat), bo[:], ALU.add))
                link.done()
                add_to_x(dve, t, n, change[:], out_made, out_added)

            prepare()
            layernorm_begin(dve, t)
            for n in range(2):
                layernorm_apply(dve, t, n, n)
            if rotary:
                rope(0, 0)
            spread_heads(0, 0)
            values_out(0, 0)

            def step(n, parity, one_ahead, two_ahead):
                maxima(n)
                if one_ahead:
                    if rotary:
                        rope(n + 1, 1 - parity)
                    spread_heads(n + 1, 1 - parity)
                if two_ahead:
                    layernorm_apply(dve, t, n + 2, parity)
                if one_ahead:
                    values_out(n + 1, 1 - parity)
                if not (isinstance(n, int) and n == 0):
                    normalise(n - 1)
                if not (isinstance(n, int) and n <= 1):
                    add_output(n - 2)
            walk(dve, step)
            add_output(B - 2)
            normalise(B - 1)
            add_output(B - 1)


def windowed_attention(nc, env):
    attention(nc, env, 1, windowed=True)


def full_attention(nc, env):
    attention(nc, env, 2)


def rotary_attention(nc, env):
    attention(nc, env, 3, rotary=True)


def turned_tiles(t, consts_in):
    t.xT = t.sb("xT", [P, C, B, L])
    t.ps_x = t.ps("ps_x", [P, 2, 512])
    t.x_turned = t.sem("x_turned")
    t.xT_ready = t.sem("xT_ready")
    t.xn_used = t.x_turned


def turn_x(pe, t, ident):
    def step(n, parity, one_ahead, two_ahead):
        pe.wait_ge(t.xn_ready, n + 1)
        enough(pe, t.xT_ready, n - 1)
        for c in range(C):
            last = pe.transpose(t.ps_x[:, parity, c * P:(c + 1) * P], t.xn[:, parity, c * P:(c + 1) * P], ident[:])
        last.then_inc(t.x_turned, 1)
    walk(pe, step)


def turned_x_out(act, t):
    def step(n, parity, one_ahead, two_ahead):
        act.wait_ge(t.x_turned, n + 1)
        act.activation(t.xT[:, :, n, :], t.ps_x[:, parity, 0:D].rearrange("p (c l) -> p c l", c=C),
                       ACT.Copy).then_inc(t.xT_ready, 1)
    walk(act, step)


def receptance_ffn(nc, env):
    A, K = env.inputs, env.consts
    with ExitStack() as ctx:
        t = Tiles(nc, ctx, "rf")
        layernorm_tiles(t, env)
        t.add_link = t.sem("add_link")
        w_raw = t.sb("w_raw", [P, 3, C, D])
        wT = t.sb("wT", [P, 3, C, D])
        ident = t.sb("ident", [P, P])
        mu = t.sb("mu", [P, 2, C])
        mu_rest = t.sb("mu_rest", [P, 2, C])
        xT = t.sb("xT", [P, 2, C, 1 + L])
        now = t.sb("now", [P, 2, C, L])
        mixedT = t.sb("mixedT", [P, 2, 2, C, L])
        keyT = t.sb("keyT", [P, 2, C, L])
        gate = t.sb("gate", [P, 2, D])
        change = t.sb("change", [P, D])
        ps_x = t.ps("ps_x", [P, C, L])
        ps_w = t.ps("ps_w", [P, 3, 512])
        ps_r, ps_k, ps_v = (t.ps(f"ps_{n}", [P, D]) for n in "rkv")

        consts_in, weights_in = t.sem("consts_in"), t.sem("weights_in")
        w_turned, w_ready, made_consts = t.sem("w_turned"), t.sem("w_ready"), t.sem("made_consts")
        turned, xT_ready = t.sem("turned"), t.sem("xT_ready")
        mix_link, mixed_ready = t.sem("mix_link"), t.sem("mixed_ready")
        rk_made, key_ready, gate_ready = t.sem("rk_made"), t.sem("key_ready"), t.sem("gate_ready")
        v_made, change_made, out_added = t.sem("v_made"), t.sem("change_made"), t.sem("out_added")
        key_link = t.sem("key_link")
        t.xn_used = turned
        block = ctx.enter_context(nc.Block())

        @block.sync
        def _(sp):
            for i, name in enumerate(("W_r", "W_k", "W_v")):
                sp.dma_start(w_raw[:, i], A[f"L2_ffn_{name}"].rearrange("(c p) n -> p c n", p=P)).then_inc(weights_in, 16)
            sp.dma_start(ident[:], K["ident"]).then_inc(consts_in, 16)
            for i, name in enumerate(("mu_r", "mu_k")):
                sp.dma_start(mu[:, i], A[f"L2_ffn_{name}"].rearrange("(c p) -> p c", p=P),
                             allow_slow_non_contiguous=True).then_inc(consts_in, 16)

        @block.tensor
        def _(pe):
            def turn(n, parity):
                pe.wait_ge(t.xn_ready, n + 1)
                enough(pe, xT_ready, n)
                for c in range(C):
                    last = pe.transpose(ps_x[:, c], t.xn[:, parity, c * P:(c + 1) * P], ident[:])
                last.then_inc(turned, 1)

            def receptance_and_key(n, parity):
                pe.wait_ge(mixed_ready, n + 1)
                enough(pe, gate_ready, n)
                enough(pe, key_ready, n)
                for k in range(C):
                    pe.matmul(ps_r[:], mixedT[:, parity, 0, k], wT[:, 0, k], start=k == 0, stop=k == C - 1)
                for o in range(C):
                    for k in range(C):
                        last = pe.matmul(ps_k[:, o * P:(o + 1) * P], wT[:, 1, k, o * P:(o + 1) * P],
                                         mixedT[:, parity, 1, k], start=k == 0, stop=k == C - 1)
                last.then_inc(rk_made, 1)

            def value(n, parity):
                pe.wait_ge(key_ready, n + 1)
                enough(pe, out_added, n)
                for k in range(C):
                    last = pe.matmul(ps_v[:], keyT[:, parity, k], wT[:, 2, k], start=k == 0, stop=k == C - 1)
                last.then_inc(v_made, 1)

            pe.wait_ge(consts_in, 48)
            pe.wait_ge(weights_in, 48)
            for i in range(3):
                for k in range(C):
                    for o in range(C):
                        last = pe.transpose(ps_w[:, i, (k * C + o) * P:(k * C + o + 1) * P],
                                            w_raw[:, i, o, k * P:(k + 1) * P], ident[:])
                last.then_inc(w_turned, 1)
            turn(0, 0)
            pe.wait_ge(w_ready, 3)
            receptance_and_key(0, 0)

            def step(n, parity, one_ahead, two_ahead):
                if one_ahead:
                    turn(n + 1, 1 - parity)
                value(n, parity)
                if one_ahead:
                    receptance_and_key(n + 1, 1 - parity)
            walk(pe, step)

        @block.scalar
        def _(act):
            def x_out(n, parity):
                act.wait_ge(turned, n + 1)
                enough(act, mixed_ready, n - 1)
                act.activation(xT[:, parity, :, 1:1 + L], ps_x[:], ACT.Copy).then_inc(xT_ready, 1)

            def gate_out(n, parity):
                act.wait_ge(rk_made, n + 1)
                enough(act, out_added, n - 1)
                act.activation(gate[:, parity], ps_r[:], ACT.Sigmoid).then_inc(gate_ready, 1)

            for i in range(3):
                act.wait_ge(w_turned, i + 1)
                act.activation(wT[:, i].rearrange("p c n -> p (c n)"), ps_w[:, i], ACT.Copy).then_inc(w_ready, 1)
            act.wait_ge(made_consts, 1)
            x_out(0, 0)
            gate_out(0, 0)

            def step(n, parity, one_ahead, two_ahead):
                if one_ahead:
                    x_out(n + 1, 1 - parity)
                    gate_out(n + 1, 1 - parity)
            walk(act, step)

        @block.vector
        def _(dve):
            def mix(n, parity):
                link = Links(dve, mix_link, 1, n)
                dve.wait_ge(xT_ready, n + 1)
                for i in range(2):
                    for c in range(C):
                        last = dve.tensor_scalar(now[:, i, c], xT[:, parity, c, 1:1 + L], mu[:, i, c:c + 1], None, ALU.mult)
                link(last)
                link.done()
                enough(dve, rk_made, n - 1)
                for i in range(2):
                    for c in range(C):
                        last = dve.scalar_tensor_tensor(mixedT[:, parity, i, c], xT[:, parity, c, 0:L],
                                                        mu_rest[:, i, c:c + 1], now[:, i, c], ALU.mult, ALU.add)
                last.then_inc(mixed_ready, 1)

            def key(n, parity):
                link = Links(dve, key_link, 1, n)
                dve.wait_ge(rk_made, n + 1)
                enough(dve, v_made, n - 1)
                flat = keyT[:, parity].rearrange("p c l -> p (c l)")
                link(dve.tensor_scalar(flat, ps_k[:], 0.0, None, ALU.max))
                link.done()
                dve.tensor_tensor(flat, flat, flat, ALU.mult).then_inc(key_ready, 1)

            def add_output(n, parity):
                dve.wait_ge(v_made, n + 1)
                dve.wait_ge(gate_ready, n + 1)
                dve.tensor_tensor(change[:], gate[:, parity], ps_v[:], ALU.mult).then_inc(change_made, 1)
                add_to_x(dve, t, n, change[:], change_made, out_added)

            dve.memset(xT[:], 0.0).then_inc(made_consts, 1)
            layernorm_begin(dve, t)
            dve.wait_ge(consts_in, 48)
            dve.tensor_scalar(mu_rest[:], mu[:], -1.0, 1.0, ALU.mult, ALU.add).then_inc(made_consts, 1)
            dve.wait_ge(made_consts, 2)
            for n in range(2):
                layernorm_apply(dve, t, n, n)
            mix(0, 0)
            key(0, 0)

            def step(n, parity, one_ahead, two_ahead):
                if two_ahead:
                    layernorm_apply(dve, t, n + 2, parity)
                if one_ahead:
                    mix(n + 1, 1 - parity)
                add_output(n, parity)
                if one_ahead:
                    key(n + 1, 1 - parity)
            walk(dve, step)


ROUND = 1.5 * 2.0 ** 23
FF = 768
FC = FF // P
QBLOCK = 32
NBLOCKS = FF * D // P // QBLOCK
G4 = B // 4


def quantised_ffn(nc, env):
    A, K = env.inputs, env.consts
    QMAX, WQMAX, SIG_STEPS = 2.0 ** 15 - 1, 7.0, 65536.0
    with ExitStack() as ctx:
        t = Tiles(nc, ctx, "qf")
        layernorm_tiles(t, env)
        t.add_link = t.sem("add_link")
        turned_tiles(t, None)
        ident = t.sb("ident", [P, P])
        upT = t.sb("upT", [P, FC, B, L])
        gateT = t.sb("gateT", [P, FC, B, L])
        raw = [upT[:, i].rearrange("p b l -> p (b l)")[:, 0:FF * C] for i in range(3)]
        raw_t = [gateT[:, i].rearrange("p b l -> p (b l)")[:, 0:FF * C] for i in range(3)]
        w_inT = t.sb("w_inT", [P, 2, C, FF])
        w_outT = t.sb("w_outT", [P, FC, D])
        wmax = t.sb("wmax", [P, 3, NBLOCKS])
        wscale = t.sb("wscale", [P, 3, NBLOCKS])
        winv = t.sb("winv", [P, 3, NBLOCKS])
        part_max = t.sb("part_max", [P, 5, G4 * FC, 1])
        own_max = t.sb("own_max", [P, 5])
        all_max = t.sb("all_max", [P, 5])
        scale = t.sb("scale", [P, 5])
        inv = t.sb("inv", [P, 5])
        rounder = t.sb("rounder", [P, 1])
        sig = t.sb("sig", [P, 2, B * L])
        prod_r = t.sb("prod_r", [P, 2, FC, L])
        prodT = t.sb("prodT", [P, 2, FC, L])
        ps = t.ps("ps", [P, 4, 512])
        ps_out = t.ps("ps_out", [P, 2, 512])

        XS, US, GS, SS, PS = range(5)
        SCALE_STEPS = 4
        consts_in, weights_in = t.sem("consts_in"), t.sem("weights_in")
        made_consts = t.sem("made_consts")
        w_link, w_quantised = t.sem("w_link"), t.sem("w_quantised")
        w_turned, w_ready = t.sem("w_turned"), t.sem("w_ready")
        x_max, max_made, max_all, scale_made = t.sem("x_max"), t.sem("max_made"), t.sem("max_all"), t.sem("scale_made")
        x_scaled, x_ready = t.sem("x_scaled"), t.sem("x_ready")
        hidden_made, hidden_out, hidden_max = t.sem("hidden_made"), t.sem("hidden_out"), t.sem("hidden_max")
        gate_scaled, gate_ready, sig_ready = t.sem("gate_scaled"), t.sem("gate_ready"), t.sem("sig_ready")
        up_scaled, up_ready = t.sem("up_scaled"), t.sem("up_ready")
        silu_link, silu_ready = t.sem("silu_link"), t.sem("silu_ready")
        silu_scaled, prod_ready = t.sem("silu_scaled"), t.sem("prod_ready")
        prod_scaled, prodT_ready = t.sem("prod_scaled"), t.sem("prodT_ready")
        prod_link = t.sem("prod_link")
        out_made, out_added = t.sem("out_made"), t.sem("out_added")
        block = ctx.enter_context(nc.Block())
        HID = 2 * FC

        @block.sync
        def _(sp):
            sp.dma_start(ident[:], K["ident"]).then_inc(consts_in, 16)
            for i, name in enumerate(("w_up", "w_gate", "w_down")):
                w = A[f"L0_ffn_{name}"]
                sp.dma_start(raw[i].rearrange("p (c n) -> p c n", n=w.shape[1]),
                             w.rearrange("(c p) n -> p c n", p=P)).then_inc(weights_in, 16)

        @block.gpsimd
        def _(pool):
            for i in range(5):
                pool.wait_ge(max_made, i + 1)
                pool.partition_all_reduce(all_max[:, i:i + 1], own_max[:, i:i + 1], P, RMAX).then_inc(max_all, 1)
                if i == GS:
                    for c in range(FC):
                        pool.wait_ge(up_scaled, c + 1)
                        pool.tensor_scalar(upT[:, c], upT[:, c], ROUND, scale[:, US:US + 1],
                                           ALU.subtract, ALU.mult).then_inc(up_ready, 1)

        @block.tensor
        def _(pe):
            pe.wait_ge(consts_in, 16)
            turn_x(pe, t, ident)
            for i in range(3):
                pe.wait_ge(w_quantised, i + 1)
                for m in range(3):
                    if 3 * i + m >= 4:
                        pe.wait_ge(w_ready, 3 * i + m - 3)
                    for a in range(4):
                        if i < 2:
                            k, o = (4 * m + a) // FC, (4 * m + a) % FC
                            block_in = raw[i][:, o * D + k * P:o * D + (k + 1) * P]
                        else:
                            k, o = (4 * m + a) // C, (4 * m + a) % C
                            block_in = raw[i][:, o * FF + k * P:o * FF + (k + 1) * P]
                        last = pe.transpose(ps[:, (3 * i + m) % 4, a * P:(a + 1) * P], block_in, ident[:])
                    last.then_inc(w_turned, 1)
            pe.wait_ge(w_ready, 9)
            pe.wait_ge(x_ready, C)

            def hidden(g):
                for i in range(2):
                    for c in range(FC):
                        q = HID * g + i * FC + c
                        enough(pe, hidden_out, q - 3)
                        for k in range(C):
                            last = pe.matmul(ps[:, (i * FC + c) % 4], w_inT[:, i, k, c * P:(c + 1) * P],
                                             t.xT[:, k].rearrange("p (g b) l -> p g (b l)", g=G4)[:, g],
                                             start=k == 0, stop=k == C - 1)
                        last.then_inc(hidden_made, 1)
            hidden(0)
            with pe.Fori(1, G4) as g:
                hidden(g)

            def step(n, parity, one_ahead, two_ahead):
                pe.wait_ge(prodT_ready, n + 1)
                enough(pe, out_added, n - 1)
                for c in range(FC):
                    last = pe.matmul(ps_out[:, parity, 0:D], prodT[:, parity, c], w_outT[:, c], start=c == 0, stop=c == FC - 1)
                last.then_inc(out_made, 1)
            walk(pe, step)

        @block.scalar
        def _(act):
            turned_x_out(act, t)
            for m in range(9):
                act.wait_ge(w_turned, m + 1)
                flat = w_inT[:].rearrange("p i k n -> p (i k n)") if m < 6 else w_outT[:].rearrange("p c n -> p (c n)")
                at = m % 6 * 512
                act.activation(flat[:, at:at + 512], ps[:, m % 4], ACT.Copy).then_inc(w_ready, 1)
            act.wait_ge(made_consts, 1)
            act.wait_ge(scale_made, SCALE_STEPS * (XS + 1))
            for c in range(C):
                act.activation(t.xT[:, c], t.xT[:, c], ACT.Identity, bias=rounder[:], scale=inv[:, XS:XS + 1]).then_inc(x_scaled, 1)

            def hidden(g):
                for i, h in enumerate((upT, gateT)):
                    for c in range(FC):
                        act.wait_ge(hidden_made, HID * g + i * FC + c + 1)
                        act.activation(h[:, c].rearrange("p (g b) l -> p g (b l)", g=G4)[:, g], ps[:, (i * FC + c) % 4],
                                       ACT.Copy).then_inc(hidden_out, 1)
            hidden(0)
            with act.Fori(1, G4) as g:
                hidden(g)
            act.wait_ge(scale_made, SCALE_STEPS * (GS + 1))
            for c in range(FC):
                act.activation(gateT[:, c], gateT[:, c], ACT.Identity, bias=rounder[:], scale=inv[:, GS:GS + 1]).then_inc(gate_scaled, 1)
                act.activation(upT[:, c], upT[:, c], ACT.Identity, bias=rounder[:], scale=inv[:, US:US + 1]).then_inc(up_scaled, 1)
                act.wait_ge(gate_ready, c + 1)
                if c >= 2:
                    act.wait_ge(silu_ready, c - 1)
                act.activation(sig[:, c % 2], gateT[:, c].rearrange("p b l -> p (b l)"), ACT.Sigmoid).then_inc(sig_ready, 1)
            act.wait_ge(scale_made, SCALE_STEPS * (SS + 1))
            for c in range(FC):
                act.activation(gateT[:, c], gateT[:, c], ACT.Identity, bias=rounder[:], scale=inv[:, SS:SS + 1]).then_inc(silu_scaled, 1)
            act.wait_ge(scale_made, SCALE_STEPS * (PS + 1))

            def step(n, parity, one_ahead, two_ahead):
                enough(act, prodT_ready, n - 1)
                act.activation(prod_r[:, parity], gateT[:, :, n, :], ACT.Identity, bias=rounder[:],
                               scale=inv[:, PS:PS + 1]).then_inc(prod_scaled, 1)
            walk(act, step)

        @block.vector
        def _(dve):
            def quantise_weights(i):
                link = Links(dve, w_link, 5, i)
                w = raw[i].rearrange("p (m q) -> p m q", q=QBLOCK)
                wt = raw_t[i].rearrange("p (m q) -> p m q", q=QBLOCK)
                wide = [P, NBLOCKS, QBLOCK]
                dve.wait_ge(weights_in, 48)
                link(dve.tensor_reduce(wmax[:, i], w, AX.X, ALU.max, apply_absolute_value=True))
                link(dve.tensor_scalar(wscale[:, i], wmax[:, i], 1.0 / WQMAX, 1e-12, ALU.mult, ALU.max))
                link(dve.reciprocal(winv[:, i], wscale[:, i]))
                link(dve.tensor_tensor(wt, w, winv[:, i].unsqueeze(2).to_broadcast(wide), ALU.mult))
                link(dve.tensor_scalar(wt, wt, ROUND, ROUND, ALU.add, ALU.subtract))
                link.done()
                dve.tensor_tensor(w, wt, wscale[:, i].unsqueeze(2).to_broadcast(wide), ALU.mult).then_inc(w_quantised, 1)

            def set_scale(i, count):
                link = Links(dve, scale_made, SCALE_STEPS, i)
                one = slice(i, i + 1)
                link(dve.tensor_reduce(own_max[:, one], part_max[:, i, 0:count, 0], AX.X, ALU.max))
                if i == PS:
                    dve.tensor_tensor(own_max[:, one], own_max[:, one], scale[:, SS:SS + 1], ALU.mult).then_inc(max_made, 1)
                else:
                    dve.tensor_copy(own_max[:, one], own_max[:, one]).then_inc(max_made, 1)
                dve.wait_ge(max_all, i + 1)
                link(dve.tensor_scalar(scale[:, one], all_max[:, one], 1.0 / QMAX, 1e-12, ALU.mult, ALU.max))
                link(dve.reciprocal(inv[:, one], scale[:, one]))
                if i == PS:
                    link(dve.tensor_tensor(inv[:, one], inv[:, one], scale[:, SS:SS + 1], ALU.mult))
                else:
                    link(dve.tensor_copy(inv[:, one], inv[:, one]))
                link.done()

            dve.memset(rounder[:], ROUND).then_inc(made_consts, 1)
            layernorm_begin(dve, t)

            def x_step(n, parity, one_ahead, two_ahead):
                layernorm_apply(dve, t, n, parity)
                dve.wait_ge(t.xn_ready, n + 1)
                dve.tensor_reduce(part_max[:, XS, n], t.xn[:, parity], AX.X, ALU.max,
                                  apply_absolute_value=True).then_inc(x_max, 1)
            walk(dve, x_step)
            dve.wait_ge(x_max, B)
            set_scale(XS, B)
            for i in range(3):
                quantise_weights(i)
            for c in range(C):
                dve.wait_ge(x_scaled, c + 1)
                dve.tensor_scalar(t.xT[:, c], t.xT[:, c], ROUND, scale[:, XS:XS + 1], ALU.subtract, ALU.mult).then_inc(x_ready, 1)

            def hidden(g):
                for i, (which, h) in enumerate(((US, upT), (GS, gateT))):
                    maxima = part_max[:, which].rearrange("p (g c) a -> p g c a", g=G4)
                    for c in range(FC):
                        dve.wait_ge(hidden_out, HID * g + i * FC + c + 1)
                        dve.tensor_reduce(maxima[:, g, c], h[:, c].rearrange("p (g b) l -> p g (b l)", g=G4)[:, g], AX.X, ALU.max,
                                          apply_absolute_value=True).then_inc(hidden_max, 1)
            hidden(0)
            with dve.Fori(1, G4) as g:
                hidden(g)
            dve.wait_ge(hidden_max, HID * G4)
            set_scale(US, G4 * FC)
            set_scale(GS, G4 * FC)
            for c in range(FC):
                flat = gateT[:, c].rearrange("p b l -> p (b l)")
                link = Links(dve, silu_link, 3, c)
                dve.wait_ge(gate_scaled, c + 1)
                dve.tensor_scalar(flat, flat, ROUND, scale[:, GS:GS + 1], ALU.subtract, ALU.mult).then_inc(gate_ready, 1)
                dve.wait_ge(sig_ready, c + 1)
                link(dve.tensor_scalar(sig[:, c % 2], sig[:, c % 2], SIG_STEPS, ROUND, ALU.mult, ALU.add))
                link(dve.tensor_scalar(sig[:, c % 2], sig[:, c % 2], ROUND, SIG_STEPS - 1, ALU.subtract, ALU.min))
                link(dve.scalar_tensor_tensor(flat, sig[:, c % 2], 1.0 / SIG_STEPS, flat, ALU.mult, ALU.mult))
                link.done()
                dve.tensor_reduce(part_max[:, SS, c], flat, AX.X, ALU.max, apply_absolute_value=True).then_inc(silu_ready, 1)
            dve.wait_ge(silu_ready, FC)
            set_scale(SS, FC)
            for c in range(FC):
                flat = gateT[:, c].rearrange("p b l -> p (b l)")
                dve.wait_ge(silu_scaled, c + 1)
                dve.wait_ge(up_ready, c + 1)
                dve.scalar_tensor_tensor(flat, flat, ROUND, upT[:, c].rearrange("p b l -> p (b l)"),
                                         ALU.subtract, ALU.mult).then_inc(prod_link, 1)
                dve.wait_ge(prod_link, c + 1)
                dve.tensor_reduce(part_max[:, PS, c], flat, AX.X, ALU.max, apply_absolute_value=True).then_inc(prod_ready, 1)
            dve.wait_ge(prod_ready, FC)
            set_scale(PS, FC)

            def quantise_product(n, parity):
                dve.wait_ge(prod_scaled, n + 1)
                enough(dve, out_made, n - 1)
                dve.tensor_scalar(prodT[:, parity], prod_r[:, parity], ROUND, scale[:, PS:PS + 1],
                                  ALU.subtract, ALU.mult).then_inc(prodT_ready, 1)
            quantise_product(0, 0)

            def step(n, parity, one_ahead, two_ahead):
                if one_ahead:
                    quantise_product(n + 1, 1 - parity)
                add_to_x(dve, t, n, ps_out[:, parity, 0:D], out_made, out_added)
            walk(dve, step)


E = 8
HID = 1024
HJ = HID // P
STEPS = E * G4


def expert_walk(eng, step, last_step):
    for half in range(2):
        for g in range(G4):
            step(half, half, g)
    with eng.Fori(1, E // 2) as j:
        for half in range(2):
            for g in range(G4):
                step(2 * j + half, half, g)
    last_step()


def before(half, g):
    return (half, g - 1) if g else (1 - half, G4 - 1)


def is_first(e, g):
    return isinstance(e, int) and e == 0 and g == 0


def expert_weights(sp, t, w1, w2, used_for):
    def load(e, half):
        sp.dma_start(t.w1[:, half], w1[e].rearrange("(k p) h -> p k h", p=P)).then_inc(t.w_in[half], 16)
        sp.dma_start(t.w2[:, half], w2[e].rearrange("(j p) n -> p j n", p=P)).then_inc(t.w_in[half], 16)
    load(0, 0)
    load(1, 1)
    with sp.Fori(1, E // 2) as j:
        for half in range(2):
            sp.wait_ge(t.eo_made, used_for(2 * j + half - 2))
            load(2 * j + half, half)


def weights_count(e, half):
    return 16 * (e - half) + 32


def expert_tiles(t):
    t.w1 = t.sb("w1", [P, 2, C, HID])
    t.w2 = t.sb("w2", [P, 2, HJ, D])
    t.b1_rows = t.sb("b1_rows", [E * HJ, P])
    t.b1T = t.sb("b1T", [P, E, HJ])
    t.b1 = t.sb("b1", [P, 2, HJ])
    t.w_in = [t.sem(f"w_in{i}") for i in range(2)]
    t.eo_made = t.sem("eo_made")
    t.b1_ready = t.sem("b1_ready")


def routed_ffn(nc, env):
    A, K = env.inputs, env.consts
    with ExitStack() as ctx:
        t = Tiles(nc, ctx, "mo")
        layernorm_tiles(t, env)
        turned_tiles(t, None)
        expert_tiles(t)
        ident = t.sb("ident", [P, P])
        iota = t.sb("iota", [P, DH])
        wr = t.sb("wr", [P, C, E])
        br = t.sb("br", [E, 1])
        b2 = t.sb("b2", [E, D])
        logitsT = t.sb("logitsT", [E, B, L])
        logits = t.sb("logits", [P, B, E])
        top = t.sb("top", [P, B, 8])
        place = t.sb("place", [P, B, 8], U32)
        gap = t.sb("gap", [P, B, 1])
        ratio = t.sb("ratio", [P, B, 1])
        share = t.sb("share", [P, 2, B, 1])
        hit = t.sb("hit", [P, 2, B, E])
        route = t.sb("route", [P, B, E])
        routeT = t.sb("routeT", [E, B, P])
        route_e = t.sb("route_e", [P, 2, B])
        hT = t.sb("hT", [P, 2, HJ, 512])
        ps_h = t.ps("ps_h", [P, 3, 512])
        ps_eo = t.ps("ps_eo", [P, 3, 512])

        consts_in = t.sem("consts_in")
        logits_made, logits_out = t.sem("logits_made"), t.sem("logits_out")
        logits_turned, logits_ready = t.sem("logits_turned"), t.sem("logits_ready")
        route_link, gap_ready, ratio_ready, route_ready = (t.sem(n) for n in ("route_link", "gap_ready", "ratio_ready", "route_ready"))
        b1_turned = t.sem("b1_turned")
        route_turned, routeT_ready = t.sem("route_turned"), t.sem("routeT_ready")
        bias_made, bias_added = t.sem("bias_made"), t.sem("bias_added")
        h_made, h_ready = t.sem("h_made"), t.sem("h_ready")
        expert_in, eo_added = t.sem("expert_in"), t.sem("eo_added")
        block = ctx.enter_context(nc.Block())
        CONSTS = 16 * 6
        XT = t.xT[:].rearrange("p c (g b) l -> p c g (b l)", g=G4)

        @block.sync
        def _(sp):
            sp.dma_start(ident[:], K["ident"]).then_inc(consts_in, 16)
            sp.dma_start(iota[:], K["iota"]).then_inc(consts_in, 16)
            sp.dma_start(wr[:], A["L3_ffn_Wr"].rearrange("(c p) e -> p c e", p=P)).then_inc(consts_in, 16)
            sp.dma_start(br[:], A["L3_ffn_br"].unsqueeze(1)).then_inc(consts_in, 16)
            sp.dma_start(b2[:], A["L3_ffn_b2"]).then_inc(consts_in, 16)
            sp.dma_start(t.b1_rows[:], A["L3_ffn_b1"].rearrange("e (j p) -> (e j) p", p=P)).then_inc(consts_in, 16)
            expert_weights(sp, t, A["L3_ffn_W1"], A["L3_ffn_W2"], lambda e: B * (e + 1))

        @block.tensor
        def _(pe):
            pe.wait_ge(consts_in, CONSTS)
            pe.transpose(ps_h[:, 0, 0:E * HJ], t.b1_rows[:], ident[0:E * HJ, 0:E * HJ]).then_inc(b1_turned, 1)
            turn_x(pe, t, ident)
            pe.wait_ge(t.xT_ready, B)
            for g in range(G4):
                if g >= 2:
                    pe.wait_ge(logits_out, g - 1)
                for k in range(C):
                    last = pe.matmul(ps_eo[0:E, g % 2], wr[:, k], XT[:, k, g], start=k == 0, stop=k == C - 1)
                last.then_inc(logits_made, 1)
            pe.wait_ge(logits_out, G4)
            for n in range(B):
                last = pe.transpose(ps_eo[:, 2, n * E:(n + 1) * E], logitsT[:, n], ident[0:E, 0:E])
            last.then_inc(logits_turned, 1)

            def turn_routes():
                pe.wait_ge(route_ready, 1)
                for g in range(G4):
                    pe.wait_ge(logits_ready, 1)
                    if g >= 2:
                        pe.wait_ge(routeT_ready, g - 1)
                    for b in range(4):
                        last = pe.transpose(ps_eo[0:E, g % 2, b * P:(b + 1) * P], route[:, 4 * g + b], ident[:])
                    last.then_inc(route_turned, 1)
                pe.wait_ge(routeT_ready, G4)
                for n in range(B):
                    if n >= 3:
                        pe.wait_ge(bias_added, n - 2)
                    pe.matmul(ps_eo[:, n % 3, 0:D], routeT[:, n], b2[:], start=True, stop=True).then_inc(bias_made, 1)

            def hidden(e, half, g):
                pe.wait_ge(t.w_in[half], weights_count(e, half))
                for j in range(HJ):
                    q = 8 * (G4 * e + g) + j
                    bank = (8 * (G4 * half + g) + j) % 2
                    enough(pe, h_ready, q - 1)
                    for k in range(C):
                        last = pe.matmul(ps_h[:, bank], t.w1[:, half, k, j * P:(j + 1) * P], XT[:, k, g],
                                         start=k == 0, stop=k == C - 1)
                    last.then_inc(h_made, 1)

            def out(e, half, g, counted_from):
                pe.wait_ge(h_ready, 8 * (counted_from + 1))
                for b in range(4):
                    n = 4 * counted_from + b
                    bank = b % 2
                    enough(pe, eo_added, n - 1)
                    for j in range(HJ):
                        last = pe.matmul(ps_eo[:, bank, 0:D], hT[:, g % 2, j, b * P:(b + 1) * P], t.w2[:, half, j],
                                         start=j == 0, stop=j == HJ - 1)
                    last.then_inc(t.eo_made, 1)

            def step(e, half, g):
                hidden(e, half, g)
                if is_first(e, g):
                    turn_routes()
                    pe.wait_ge(bias_added, B)
                else:
                    out(e, *before(half, g), G4 * e + g - 1)
            expert_walk(pe, step, lambda: out(E - 1, 1, G4 - 1, STEPS - 1))

        @block.scalar
        def _(act):
            act.wait_ge(b1_turned, 1)
            act.activation(t.b1T[:].rearrange("p e j -> p (e j)"), ps_h[:, 0, 0:E * HJ], ACT.Copy).then_inc(t.b1_ready, 1)
            turned_x_out(act, t)
            act.wait_ge(consts_in, CONSTS)
            for g in range(G4):
                act.wait_ge(logits_made, g + 1)
                act.activation(logitsT[:, 4 * g:4 * g + 4].rearrange("e b l -> e (b l)"), ps_eo[0:E, g % 2], ACT.Identity,
                               bias=br[:]).then_inc(logits_out, 1)
            act.wait_ge(logits_turned, 1)
            act.activation(logits[:].rearrange("p b e -> p (b e)"), ps_eo[:, 2, 0:B * E], ACT.Copy).then_inc(logits_ready, 1)
            act.wait_ge(gap_ready, 1)
            act.activation(ratio[:], gap[:], ACT.Exp).then_inc(ratio_ready, 1)

            def step(e, half, g):
                act.wait_ge(expert_in, e + 1)
                for j in range(HJ):
                    q = 8 * (G4 * e + g) + j
                    act.wait_ge(h_made, q + 1)
                    act.activation(hT[:, g % 2, j], ps_h[:, (8 * (G4 * half + g) + j) % 2], ACT.Relu,
                                   bias=t.b1[:, half, j:j + 1]).then_inc(h_ready, 1)
                if is_first(e, g):
                    for g2 in range(G4):
                        act.wait_ge(route_turned, g2 + 1)
                        act.activation(routeT[:, 4 * g2:4 * g2 + 4].rearrange("e b l -> e (b l)"), ps_eo[0:E, g2 % 2],
                                       ACT.Copy).then_inc(routeT_ready, 1)
            expert_walk(act, step, lambda: None)

        @block.gpsimd
        def _(pool):
            pool.wait_ge(t.b1_ready, 1)
            pool.wait_ge(route_ready, 1)

            def fetch(e, half):
                pool.tensor_copy(t.b1[:, half], t.b1T[:, e])
                pool.tensor_copy(route_e[:, half], route[:, :, e]).then_inc(expert_in, 1)
            fetch(0, 0)
            fetch(1, 1)
            with pool.Fori(1, E // 2) as i:
                for half in range(2):
                    pool.wait_ge(eo_added, B * (2 * i + half - 1))
                    fetch(2 * i + half, half)

        @block.vector
        def _(dve):
            layernorm_begin(dve, t)

            def x_step(n, parity, one_ahead, two_ahead):
                layernorm_apply(dve, t, n, parity)
            walk(dve, x_step)
            dve.wait_ge(consts_in, CONSTS)
            link = Links(dve, route_link, 7, 0)
            dve.wait_ge(logits_ready, 1)
            for n in range(B):
                last = dve.max(top[:, n], logits[:, n])
            link(last)
            dve.tensor_tensor(gap[:], top[:, :, 1:2], top[:, :, 0:1], ALU.subtract).then_inc(gap_ready, 1)
            for n in range(B):
                last = dve.max_index(place[:, n], top[:, n], logits[:, n])
            link(last)
            for i in range(2):
                last = dve.tensor_tensor(hit[:, i], iota[:, 0:E].unsqueeze(1).to_broadcast([P, B, E]),
                                         place[:, :, i:i + 1].to_broadcast([P, B, E]), ALU.is_equal)
            link(last)
            dve.wait_ge(ratio_ready, 1)
            link(dve.tensor_scalar(share[:, 1], ratio[:], 1.0, None, ALU.add))
            link(dve.reciprocal(share[:, 0], share[:, 1]))
            link(dve.tensor_tensor(share[:, 1], share[:, 0], ratio[:], ALU.mult))
            for i in range(2):
                last = dve.tensor_tensor(hit[:, i], hit[:, i], share[:, i].to_broadcast([P, B, E]), ALU.mult)
            link(last)
            link.done()
            dve.tensor_tensor(route[:], hit[:, 0], hit[:, 1], ALU.add).then_inc(route_ready, 1)
            for n in range(B):
                dve.wait_ge(bias_made, n + 1)
                dve.tensor_tensor(t.X[:, n], t.X[:, n], ps_eo[:, n % 3, 0:D], ALU.add).then_inc(bias_added, 1)

            def add(half, g, counted_from):
                for b in range(4):
                    n = 4 * counted_from + b
                    dve.wait_ge(t.eo_made, n + 1)
                    at = 4 * g + b
                    dve.scalar_tensor_tensor(t.X[:, at], ps_eo[:, b % 2, 0:D], route_e[:, half, at:at + 1], t.X[:, at],
                                             ALU.mult, ALU.add).then_inc(eo_added, 1)

            def step(e, half, g):
                if g == 0:
                    dve.wait_ge(expert_in, e + 1)
                if not is_first(e, g):
                    add(*before(half, g), G4 * e + g - 1)
            expert_walk(dve, step, lambda: add(1, G4 - 1, STEPS - 1))


def newton_rsqrt(dve, link, out, var, half, tmp):
    link(dve.tensor_scalar(half, var.bitcast(I32), 1, None, ALU.logical_shift_right))
    link(dve.tensor_scalar(out.bitcast(I32), half, -1.0, RSQRT_MAGIC, ALU.mult, ALU.add))
    for _ in range(NEWTON_STEPS):
        link(dve.scalar_tensor_tensor(tmp, out, -0.5, out, ALU.mult, ALU.mult))
        link(dve.tensor_tensor(tmp, tmp, var, ALU.mult))
        link(dve.scalar_tensor_tensor(out, tmp, 1.5, out, ALU.add, ALU.mult))


def slot_ffn(nc, env):
    A, K = env.inputs, env.consts
    ES = E * P
    NT = B + E
    with ExitStack() as ctx:
        t = Tiles(nc, ctx, "sl")
        layernorm_tiles(t, env)
        expert_tiles(t)
        ident = t.sb("ident", [P, P])
        ident_b = t.sb("ident_b", [P, P], BF16)
        row_sel = t.sb("row_sel", [P, B, P], BF16)
        gamma = t.sb("gamma", [P, 2, D])
        b2 = t.sb("b2", [P, E, D])
        xr = t.sb("xr", [P, B, D])
        slots = t.sb("slots", [P, E, D])
        xrT = t.sb("xrT", [P, C, B, L])
        slotsT = t.sb("slotsT", [P, C, E, P])
        slotT_e = t.sb("slotT_e", [P, 2, C, P])
        squares = t.sb("squares", [P, 2, D])
        norm2 = t.sb("norm2", [P, NT])
        r_half = t.sb("r_half", [P, NT], I32)
        r_tmp = t.sb("r_tmp", [P, NT])
        r_norm = t.sb("r_norm", [P, NT])
        neg_rmax = t.sb("neg_rmax", [P, P], BF16)
        neg_rmaxT = t.sb("neg_rmaxT", [P, P], BF16)
        neg_smax = t.sb("neg_smax", [P, 2, 4])
        dispT = t.sb("dispT", [P, 2, 4, L])
        disp_sum = t.sb("disp_sum", [P, 2, 4, 1])
        disp_inv = t.sb("disp_inv", [P, 2, 4, 1])
        disp = t.sb("disp", [P, 2, 4, P])
        combT = t.sb("combT", [P, 2, 4, L])
        slot_inT = t.sb("slot_inT", [P, 2, C, 4, P])
        hT = t.sb("hT", [P, HJ, 512])
        acc_max = t.sb("acc_max", [P, B, 2, 1])
        result = t.sb("result", [P, 2, D + 1])
        acc = t.sb("acc", [P, B, D + 1])
        ps_lt = t.ps("ps_lt", [P, 4, L])
        ps_in = t.ps("ps_in", [P, C, 4, P])
        ps_h = t.ps("ps_h", [P, 2, 512])
        ps_eo = t.ps("ps_eo", [P, 2, 512])
        ps_out = t.ps("ps_out", [P, 512])

        consts_in, made_consts = t.sem("consts_in"), t.sem("made_consts")
        squared, rms_link, rms_ready = t.sem("squared"), t.sem("rms_link"), t.sem("rms_ready")
        rows_turned, rowsT_ready = t.sem("rows_turned"), t.sem("rowsT_ready")
        b1_turned, expert_in = t.sem("b1_turned"), t.sem("expert_in")
        all_logits, rmax_ready, rmax_turned, rmaxT_ready = (t.sem(n) for n in ("all_logits", "rmax_ready", "rmax_turned", "rmaxT_ready"))
        logits_made, smax_ready, dispT_made = t.sem("logits_made"), t.sem("smax_ready"), t.sem("dispT_made")
        disp_link, dispT_ready = t.sem("disp_link"), t.sem("dispT_ready")
        disp_turned, disp_ready = t.sem("disp_turned"), t.sem("disp_ready")
        shifted, comb_ready = t.sem("shifted"), t.sem("comb_ready")
        in_made, in_ready = t.sem("in_made"), t.sem("in_ready")
        h_made, h_ready = t.sem("h_made"), t.sem("h_ready")
        result_ready, out_made, out_added = t.sem("result_ready"), t.sem("out_made"), t.sem("out_added")
        end_link = t.sem("end_link")
        block = ctx.enter_context(nc.Block())
        CONSTS = 16 * 6
        XT = xrT[:].rearrange("p c (g b) l -> p c g (b l)", g=G4)

        @block.sync
        def _(sp):
            sp.dma_start(ident[:], K["ident"]).then_inc(consts_in, 16)
            for i, name in enumerate(("norm_gamma", "slot_norm_gamma")):
                sp.dma_start(gamma[:, i], A[f"L1_ffn_{name}"].unsqueeze(0).to_broadcast([P, D])).then_inc(consts_in, 16)
            sp.dma_start(slots[:], A["L1_ffn_slot_embeds"].rearrange("e s d -> s e d")).then_inc(consts_in, 16)
            sp.dma_start(b2[:], A["L1_ffn_b2"].unsqueeze(0).to_broadcast([P, E, D])).then_inc(consts_in, 16)
            sp.dma_start(t.b1_rows[:], A["L1_ffn_b1"].rearrange("e (j p) -> (e j) p", p=P)).then_inc(consts_in, 16)
            expert_weights(sp, t, A["L1_ffn_w1"], A["L1_ffn_w2"], lambda e: B * (e + 1))

        @block.tensor
        def _(pe):
            pe.wait_ge(consts_in, CONSTS)
            pe.transpose(ps_out[:, 0:E * HJ], t.b1_rows[:], ident[0:E * HJ, 0:E * HJ]).then_inc(b1_turned, 1)
            for m in range(NT):
                pe.wait_ge(rms_ready, m + 1)
                if m >= 2:
                    pe.wait_ge(rowsT_ready, m - 1)
                rows = slots[:, m] if m < E else xr[:, m - E]
                for c in range(C):
                    last = pe.transpose(ps_h[:, m % 2, c * P:(c + 1) * P], rows[:, c * P:(c + 1) * P], ident[:])
                last.then_inc(rows_turned, 1)
            pe.wait_ge(rowsT_ready, NT)
            for n in range(B):
                for i in range(2):
                    q = 2 * n + i
                    if q >= 2:
                        pe.wait_ge(rmax_ready, q - 1)
                    for k in range(C):
                        last = pe.matmul(ps_eo[:, i], xrT[:, k, n], slotsT[:, k, 4 * i:4 * i + 4].rearrange("p e s -> p (e s)"),
                                         start=k == 0, stop=k == C - 1)
                    last.then_inc(all_logits, 1)
            pe.wait_ge(rmax_ready, 2 * B + 1)
            pe.wait_ge(made_consts, 3)
            pe.transpose(ps_lt[:].rearrange("p b l -> p (b l)").bitcast(BF16)[:, 0:P], neg_rmax[:], ident_b[:]).then_inc(rmax_turned, 1)
            pe.wait_ge(rmaxT_ready, 1)

            def logits(e, half, g, q):
                pe.wait_ge(expert_in, e + 1)
                enough(pe, comb_ready, q)
                for k in range(C):
                    last = pe.matmul(ps_lt[:].rearrange("p b l -> p (b l)"), slotT_e[:, half, k], XT[:, k, g],
                                     start=k == 0, stop=k == C - 1)
                last.then_inc(logits_made, 1)

            def turn_dispatch(g, q):
                pe.wait_ge(dispT_ready, q + 1)
                enough(pe, in_ready, q)
                for b in range(4):
                    last = pe.transpose(ps_in[:, 0, b], dispT[:, g % 2, b], ident[:])
                last.then_inc(disp_turned, 1)

            def shift(g, q):
                pe.wait_ge(dispT_made, 4 * (q + 1))
                for b in range(4):
                    last = pe.matmul(ps_lt[:, b], row_sel[:, 4 * g + b], neg_rmaxT[:], start=False, stop=True,
                                     skip_group_check=True)
                last.then_inc(shifted, 1)

            def slot_inputs(g, q):
                pe.wait_ge(disp_ready, q + 1)
                for b in range(4):
                    for c in range(C):
                        last = pe.matmul(ps_in[:, c, b], xr[:, 4 * g + b, c * P:(c + 1) * P], disp[:, g % 2, b],
                                         start=True, stop=True)
                last.then_inc(in_made, 1)

            def hidden(half, g, q, e):
                pe.wait_ge(t.w_in[half], weights_count(e, half))
                pe.wait_ge(in_ready, q + 1)
                for j in range(HJ):
                    enough(pe, h_ready, 8 * q + j - 1)
                    for k in range(C):
                        last = pe.matmul(ps_h[:, j % 2], t.w1[:, half, k, j * P:(j + 1) * P],
                                         slot_inT[:, g % 2, k].rearrange("p b s -> p (b s)"), start=k == 0, stop=k == C - 1)
                    last.then_inc(h_made, 1)

            def results(half, g, q):
                pe.wait_ge(h_ready, 8 * (q + 1))
                pe.wait_ge(comb_ready, q + 1)

                def combine(b):
                    pe.wait_ge(result_ready, 4 * q + b + 1)
                    enough(pe, out_added, 4 * q + b)
                    pe.matmul(ps_out[:, 0:D + 1], combT[:, g % 2, b], result[:, b % 2], start=True, stop=True).then_inc(out_made, 1)
                for b in range(4):
                    enough(pe, result_ready, 4 * q + b - 1)
                    for j in range(HJ):
                        last = pe.matmul(ps_eo[:, b % 2, 0:D], hT[:, j, b * P:(b + 1) * P], t.w2[:, half, j],
                                         start=j == 0, stop=j == HJ - 1)
                    last.then_inc(t.eo_made, 1)
                    if b >= 1:
                        combine(b - 1)
                combine(3)

            def step(e, half, g):
                q = G4 * e + g
                logits(e, half, g, q)
                if is_first(e, g):
                    turn_dispatch(g, q)
                    shift(g, q)
                else:
                    h0, g0 = before(half, g)
                    hidden(h0, g0, q - 1, e if g else e - 1)
                    turn_dispatch(g, q)
                    shift(g, q)
                    results(h0, g0, q - 1)
                slot_inputs(g, q)

            def last_step():
                hidden(1, G4 - 1, STEPS - 1, E - 1)
                results(1, G4 - 1, STEPS - 1)
            expert_walk(pe, step, last_step)

        @block.scalar
        def _(act):
            act.wait_ge(b1_turned, 1)
            act.activation(t.b1T[:].rearrange("p e j -> p (e j)"), ps_out[:, 0:E * HJ], ACT.Copy).then_inc(t.b1_ready, 1)
            act.wait_ge(consts_in, CONSTS)
            for m in range(NT):
                if m >= E:
                    act.wait_ge(t.xn_ready, m - E + 1)
                if m >= 2:
                    act.wait_ge(squared, m - 1)
                rows = slots[:, m] if m < E else xr[:, m - E]
                act.activation(squares[:, m % 2], rows, ACT.Square, accum_out=norm2[:, m:m + 1]).then_inc(squared, 1)
            for m in range(NT):
                act.wait_ge(rows_turned, m + 1)
                to = slotsT[:, :, m] if m < E else xrT[:, :, m - E]
                act.activation(to, ps_h[:, m % 2, 0:D].rearrange("p (c l) -> p c l", c=C), ACT.Copy).then_inc(rowsT_ready, 1)
            act.wait_ge(rmax_turned, 1)
            act.activation(neg_rmaxT[:], ps_lt[:].rearrange("p b l -> p (b l)").bitcast(BF16)[:, 0:P], ACT.Copy).then_inc(rmaxT_ready, 1)

            def weights(g, q):
                act.wait_ge(smax_ready, q + 1)
                enough(act, disp_turned, q - 1)
                for b in range(4):
                    act.activation(dispT[:, g % 2, b], ps_lt[:, b], ACT.Exp, bias=neg_smax[:, g % 2, b:b + 1],
                                   accum_out=disp_sum[:, g % 2, b]).then_inc(dispT_made, 1)

            def combine_weights(g, q):
                act.wait_ge(shifted, q + 1)
                enough(act, out_made, 4 * (q - 1))
                act.activation(combT[:, g % 2], ps_lt[:], ACT.Exp).then_inc(comb_ready, 1)

            def inputs_out(g, q):
                act.wait_ge(in_made, q + 1)
                enough(act, h_made, 8 * (q - 1))
                act.activation(slot_inT[:, g % 2], ps_in[:], ACT.Copy).then_inc(in_ready, 1)

            def hidden(half, g, q):
                for j in range(HJ):
                    act.wait_ge(h_made, 8 * q + j + 1)
                    act.activation(hT[:, j], ps_h[:, j % 2], ACT.Gelu, bias=t.b1[:, half, j:j + 1]).then_inc(h_ready, 1)

            def step(e, half, g):
                q = G4 * e + g
                weights(g, q)
                if is_first(e, g):
                    combine_weights(g, q)
                else:
                    h0, g0 = before(half, g)
                    hidden(h0, g0, q - 1)
                    combine_weights(g, q)
                inputs_out(g, q)
            expert_walk(act, step, lambda: hidden(1, G4 - 1, STEPS - 1))

        @block.gpsimd
        def _(pool):
            pool.wait_ge(t.b1_ready, 1)
            pool.wait_ge(rowsT_ready, E)

            def fetch(e, half):
                pool.tensor_copy(t.b1[:, half], t.b1T[:, e])
                pool.tensor_copy(slotT_e[:, half], slotsT[:, :, e]).then_inc(expert_in, 1)
            fetch(0, 0)
            fetch(1, 1)
            with pool.Fori(1, E // 2) as i:
                for half in range(2):
                    pool.wait_ge(t.eo_made, B * (2 * i + half - 1))
                    fetch(2 * i + half, half)

        @block.vector
        def _(dve):
            layernorm_begin(dve, t)
            for n in range(B):
                dve.tensor_scalar(xr[:, n], t.X[:, n], t.meanvar[:, n, 0:1], t.rstd[:, n], ALU.subtract, ALU.mult).then_inc(t.xn_ready, 1)
            dve.memset(acc[:], 0.0).then_inc(made_consts, 1)
            dve.memset(result[:], 1.0).then_inc(made_consts, 1)
            dve.memset(neg_rmax[:], 0.0)
            dve.wait_ge(consts_in, CONSTS)
            dve.tensor_copy(ident_b[:], ident[:])
            dve.tensor_copy(row_sel[:], ident[:, 0:B].unsqueeze(2).to_broadcast([P, B, P])).then_inc(made_consts, 1)
            dve.wait_ge(squared, NT)
            dve.wait_ge(t.xn_ready, B)
            link = Links(dve, rms_link, 4 + 3 * NEWTON_STEPS, 0)
            link(dve.tensor_scalar(norm2[:], norm2[:], 1e-24, None, ALU.max))
            newton_rsqrt(dve, link, r_norm[:], norm2[:], r_half[:], r_tmp[:])
            link(dve.tensor_scalar(r_norm[:], r_norm[:], float(D) ** 0.5, None, ALU.mult))
            link.done()
            for m in range(NT):
                rows = slots[:, m] if m < E else xr[:, m - E]
                dve.scalar_tensor_tensor(rows, rows, r_norm[:, m:m + 1], gamma[:, int(m < E)], ALU.mult, ALU.mult).then_inc(rms_ready, 1)
            for q in range(2 * B):
                dve.wait_ge(all_logits, q + 1)
                dve.tensor_reduce(acc_max[:, q // 2, q % 2], ps_eo[:, q % 2], AX.X, ALU.max, negate=True).then_inc(rmax_ready, 1)
            dve.wait_ge(rmax_ready, 2 * B)
            dve.tensor_tensor(neg_rmax[:, 0:B], acc_max[:, :, 0, 0], acc_max[:, :, 1, 0], ALU.min).then_inc(rmax_ready, 1)

            def slot_max(g, q):
                dve.wait_ge(logits_made, q + 1)
                dve.tensor_reduce(neg_smax[:, g % 2], ps_lt[:], AX.X, ALU.max, negate=True).then_inc(smax_ready, 1)

            def normalise_dispatch(g, q):
                link = Links(dve, disp_link, 1, q)
                dve.wait_ge(dispT_made, 4 * (q + 1))
                link(dve.reciprocal(disp_inv[:, g % 2], disp_sum[:, g % 2]))
                link.done()
                dve.tensor_tensor(dispT[:, g % 2], dispT[:, g % 2], disp_inv[:, g % 2].to_broadcast([P, 4, L]),
                                  ALU.mult).then_inc(dispT_ready, 1)

            def dispatch_out(g, q):
                dve.wait_ge(disp_turned, q + 1)
                enough(dve, in_made, q - 1)
                dve.tensor_copy(disp[:, g % 2], ps_in[:, 0]).then_inc(disp_ready, 1)

            def results(e, g, q):
                def add(b):
                    at = 4 * g + b
                    dve.wait_ge(out_made, 4 * q + b + 1)
                    dve.tensor_tensor(acc[:, at], acc[:, at], ps_out[:, 0:D + 1], ALU.add).then_inc(out_added, 1)
                for b in range(4):
                    dve.wait_ge(t.eo_made, 4 * q + b + 1)
                    enough(dve, out_made, 4 * q + b - 1)
                    dve.tensor_tensor(result[:, b % 2, 0:D], ps_eo[:, b % 2, 0:D], b2[:, e], ALU.add).then_inc(result_ready, 1)
                    if b >= 1:
                        add(b - 1)
                add(3)

            def step(e, half, g):
                q = G4 * e + g
                slot_max(g, q)
                normalise_dispatch(g, q)
                dispatch_out(g, q)
                if not is_first(e, g):
                    _, g0 = before(half, g)
                    results(e if g else e - 1, g0, q - 1)
            expert_walk(dve, step, lambda: results(E - 1, G4 - 1, STEPS - 1))
            dve.wait_ge(out_added, B * E)
            link = Links(dve, end_link, 2, 0)
            link(dve.reciprocal(acc[:, :, D:D + 1], acc[:, :, D:D + 1]))
            for n in range(B):
                last = dve.scalar_tensor_tensor(t.X[:, n], acc[:, n, 0:D], acc[:, n, D:D + 1], t.X[:, n], ALU.mult, ALU.add)
            link(last)
            link.done()
            for n in range(B):
                batch_stats(dve, t.X, t.stats, n)


PHASES = [autocorrelation, quantised_ffn, windowed_attention, slot_ffn, full_attention, receptance_ffn, rotary_attention, routed_ffn]


class Env:

    def __init__(self, inputs, consts, X, stats):
        self.inputs, self.consts, self.X, self.stats = inputs, consts, X, stats


def load_x(nc, env):
    with ExitStack() as ctx:
        x_in = ctx.enter_context(nc.semaphore("x_in"))
        block = ctx.enter_context(nc.Block())

        @block.sync
        def _(sp):
            sp.dma_start(env.X[:], env.inputs["x"].rearrange("b l d -> l b d")).then_inc(x_in, 16)

        @block.vector
        def _(dve):
            dve.wait_ge(x_in, 16)
            for n in range(B):
                batch_stats(dve, env.X, env.stats, n)


def store_x(nc, env, out):
    with ExitStack() as ctx:
        x_out = ctx.enter_context(nc.semaphore("x_out"))
        block = ctx.enter_context(nc.Block())

        @block.sync
        def _(sp):
            sp.dma_start(out.rearrange("b l d -> l b d"), env.X[:]).then_inc(x_out, 16)
            sp.wait_ge(x_out, 16)


def build_program(nc, inputs, consts, out):
    with ExitStack() as ctx:
        X = ctx.enter_context(nc.sbuf_tensor("X", [P, B, D], F32))
        stats = ctx.enter_context(nc.sbuf_tensor("stats", [P, B, 6], F32))
        env = Env(inputs, consts, X, stats)
        load_x(nc, env)
        for phase in PHASES:
            phase(nc, env)
        store_x(nc, env, out)


def constants():
    f8 = np.float64
    tok = np.arange(L, dtype=f8)[:, None]
    freq = np.arange(L // 2, dtype=f8)[None, :]
    angle = 2 * np.pi * tok * freq / L
    cos, sin = np.cos(angle), np.sin(angle)
    sin[:, 0] = np.cos(np.pi * tok[:, 0])
    dft = np.concatenate([cos, sin, np.eye(L), sin, cos], axis=1)
    even = 2.0 / L * np.cos(angle).T
    odd = 2.0 / L * np.sin(angle).T
    nyquist = even.copy()
    even[0] = 1.0 / L
    nyquist[0] = np.cos(np.pi * tok[:, 0]) / L
    idft = np.concatenate([np.concatenate([even, nyquist]), np.concatenate([-odd, odd])], axis=1)
    row = np.arange(P)
    inv_freq = 1.0 / np.float32(10000.0) ** (np.arange(0, DH, 2, dtype=np.float32) / DH)
    position_angle = np.arange(L, dtype=np.float32)[None, :] * inv_freq[row % (DH // 2)][:, None]
    rot = np.zeros((P, P))
    rot[row, np.where(row % DH < DH // 2, row + DH // 2, row - DH // 2)] = np.where(row % DH < DH // 2, 1, -1)
    tables = {
        "head_of_row": row[:, None] // DH == np.arange(HC)[None, :],
        "window": np.where(np.abs(row[:, None] - row[None, :]) <= WINDOW, 0.0, HUGE_NEGATIVE),
        "cosT": np.cos(position_angle),
        "sinT": np.sin(position_angle),
        "rot": rot,
        "dft": dft,
        "idft": idft,
        "iota": np.broadcast_to(np.arange(DH), (P, DH)),
        "row_mod": (row % DH + P)[:, None],
        "head_mask": np.repeat((row[:, None] // DH == np.arange(HC)[None, :]), DH, axis=1),
        "ident": np.eye(P),
    }
    return {k: np.ascontiguousarray(v, dtype=np.float32) for k, v in tables.items()}


def kernel(**inputs):
    import concourse.bacc as bacc
    from concourse.bass_utils import run_bass_kernel_spmd

    nc = bacc.Bacc("TRN2", target_bir_lowering=False, num_devices=1)
    arrays = {}

    def dram(name, a):
        arrays[name] = np.ascontiguousarray(a)
        return nc.dram_tensor(name, arrays[name].shape, F32, kind="ExternalInput").ap()

    ins = {name: dram(f"in_{name}", a) for name, a in inputs.items()}
    consts = {name: dram(f"const_{name}", a) for name, a in constants().items()}
    out = nc.dram_tensor("out", [B, L, D], F32, kind="ExternalOutput").ap()
    build_program(nc, ins, consts, out)
    r = run_bass_kernel_spmd(nc, [arrays], core_ids=[0])
    return r.results[0]["out"]
```

```python
from contextlib import ExitStack

import numpy as np

import concourse.bass as bass
from concourse import mybir

F32 = mybir.dt.float32
BF16 = mybir.dt.bfloat16
F16 = mybir.dt.float16
U32 = mybir.dt.uint32
I32 = mybir.dt.int32
ALU = mybir.AluOpType
ACT = mybir.ActivationFunctionType
AX = mybir.AxisListType
RMAX = bass.bass_isa.ReduceOp.max

B, L, D = 16, 128, 256
P = 128
C = D // P
H, DH = 16, 16
HC = H // C
LN_EPS = 1e-5
WINDOW = 64
PAIRS = B // 2 - 1


def enough(eng, sem, value):
    if not isinstance(value, int) or value > 0:
        eng.wait_ge(sem, value)


class Links:

    def __init__(self, eng, sem, per, n):
        self.eng, self.sem, self.per, self.base, self.k = eng, sem, per, n * per, 0

    def __call__(self, ins):
        self.k += 1
        ins.then_inc(self.sem, 1)
        self.eng.wait_ge(self.sem, self.base + self.k)

    def done(self):
        assert self.k == self.per, (self.k, self.per)


class Tiles:

    def __init__(self, nc, ctx, name):
        self.nc, self.ctx, self.name = nc, ctx, name
        self.sems = []
        ctx.callback(self.clear)

    def clear(self):
        self.nc.clear_and_free_semaphores(self.sems)
        self.nc.all_engine_barrier()

    def sb(self, name, shape, dt=F32):
        return self.ctx.enter_context(self.nc.sbuf_tensor(f"{self.name}_{name}", shape, dt))

    def ps(self, name, shape, dt=F32):
        return self.ctx.enter_context(self.nc.psum_tensor(f"{self.name}_{name}", shape, dt))

    def sem(self, name):
        self.sems.append(self.nc.alloc_semaphore(name=f"{self.name}_{name}"))
        return self.sems[-1]


def walk(eng, step):
    step(0, 0, True, True)
    step(1, 1, True, True)
    with eng.Fori(1, PAIRS) as j:
        step(2 * j, 0, True, True)
        step(2 * j + 1, 1, True, True)
    step(B - 2, 0, True, False)
    step(B - 1, 1, False, False)


def batch_stats(dve, X, stats, n):
    return dve.bn_stats(stats[:, n, :], X[:, n, :])


RSQRT_MAGIC = float(0x5F3759DF)
NEWTON_STEPS = 3


def layernorm_begin(dve, t):
    link = Links(dve, t.ln_link, 4 + 3 * NEWTON_STEPS, 0)
    for n in range(B):
        last = dve.bn_aggr(t.meanvar[:, n, :], t.stats[:, n, :])
    link(last)
    link(dve.tensor_scalar(t.ln_var[:], t.meanvar[:, :, 1:2], LN_EPS, None, ALU.add))
    link(dve.tensor_scalar(t.ln_half[:], t.ln_var[:].bitcast(I32), 1, None, ALU.logical_shift_right))
    link(dve.tensor_scalar(t.rstd[:].bitcast(I32), t.ln_half[:], -1.0, RSQRT_MAGIC, ALU.mult, ALU.add))
    for _ in range(NEWTON_STEPS):
        link(dve.scalar_tensor_tensor(t.ln_tmp[:], t.rstd[:], -0.5, t.rstd[:], ALU.mult, ALU.mult))
        link(dve.tensor_tensor(t.ln_tmp[:], t.ln_tmp[:], t.ln_var[:], ALU.mult))
        link(dve.scalar_tensor_tensor(t.rstd[:], t.ln_tmp[:], 1.5, t.rstd[:], ALU.add, ALU.mult))
    link.done()


def layernorm_apply(dve, t, n, parity):
    enough(dve, t.xn_used, n - 1)
    dve.tensor_scalar(t.xn[:, parity, :], t.X[:, n, :], t.meanvar[:, n, 0:1], t.rstd[:, n, :],
                      ALU.subtract, ALU.mult).then_inc(t.xn_ready, 1)


def layernorm_tiles(t, env):
    t.X, t.stats = env.X, env.stats
    t.meanvar = t.sb("meanvar", [P, B, 2])
    t.ln_var = t.sb("ln_var", [P, B, 1])
    t.ln_half = t.sb("ln_half", [P, B, 1], I32)
    t.ln_tmp = t.sb("ln_tmp", [P, B, 1])
    t.rstd = t.sb("rstd", [P, B, 1])
    t.xn = t.sb("xn", [P, 2, D])
    t.ln_link = t.sem("ln_link")
    t.xn_ready = t.sem("xn_ready")


def add_to_x(dve, t, n, change, change_made, added):
    link = Links(dve, t.add_link, 1, n)
    dve.wait_ge(change_made, n + 1)
    link(dve.tensor_tensor(t.X[:, n, :], t.X[:, n, :], change, ALU.add))
    link.done()
    batch_stats(dve, t.X, t.stats, n).then_inc(added, 1)


def load_context(sp, t, n, parity):
    enough(sp, t.ctx_used, n - 1)
    sp.dma_start(t.ctx_in[:, parity, :], t.ctx_dram[n]).then_inc(t.ctx_ready[parity], 16)


def context_tiles(t, ctx_dram):
    t.ctx_dram = ctx_dram
    t.ctx_in = t.sb("ctx_in", [P, 2, D])
    t.ctx_ready = [t.sem(f"ctx_ready{i}") for i in range(2)]


def context_count(n, parity):
    return 8 * (n - parity) + 16


def autocorrelation(nc, env):
    A, K = env.inputs, env.consts
    with ExitStack() as ctx:
        t = Tiles(nc, ctx, "ac")
        layernorm_tiles(t, env)
        t.add_link = t.sem("add_link")
        context_tiles(t, A["ctx_1024"])
        FX = 4 * P
        wq, wk, wv, wo = (t.sb(f"w{n}", [P, C, D]) for n in "qkvo")
        dft = t.sb("dft", [P, 3 * P])
        idft = t.sb("idft", [P, 2, L])
        head_mask = t.sb("head_mask", [P, HC, DH])
        iota = t.sb("iota", [P, DH])
        row_mod = t.sb("row_mod", [P, 1])
        specT = t.sb("specT", [P, 2, C, FX])
        qv = t.sb("qv", [P, 2, 2 * D])
        prod = t.sb("prod", [P, 2, 2, D])
        corr = t.sb("corr", [P, 2, C, L])
        top = t.sb("top", [P, C, 8])
        lag = t.sb("lag", [P, C, 8], U32)
        src_f = t.sb("src_f", [P, C, 4])
        src_i = t.sb("src_i", [P, C, 4], I32)
        src = t.sb("src", [P, C, 4], I32)
        below = t.sb("below", [P, C, 4])
        ew = t.sb("ew", [P, C, 4])
        ew_sum = t.sb("ew_sum", [P, C])
        ew_inv = t.sb("ew_inv", [P, C])
        hit = t.sb("hit", [P, C, DH, 4])
        hit_w = t.sb("hit_w", [P, C, DH, 4])
        mix = t.sb("mix", [P, C, DH])
        mix_n = t.sb("mix_n", [P, C, DH])
        mix_block = t.sb("mix_block", [P, 2, C, HC, DH])
        mixT = t.sb("mixT", [P, 2, C, P])
        rolled = t.sb("rolled", [P, 2, 2, DH, H // 2])
        ident = t.sb("ident", [P, P])

        ps_spec = t.ps("ps_spec", [P, C, FX])
        ps_qv = t.ps("ps_qv", [P, 2 * D])
        ps_k = t.ps("ps_k", [P, 2, D])
        ps_corr = t.ps("ps_corr", [P, C, L])
        ps_mixT = t.ps("ps_mixT", [P, C, P])
        ps_rolled = t.ps("ps_rolled", [P, H // 2, 2, DH])
        ps_out = t.ps("ps_out", [P, D])

        consts_in = t.sem("consts_in")
        spec_made, spec_ready = t.sem("spec_made"), t.sem("spec_ready")
        t.xn_used = t.ctx_used = spec_made
        qkv_made = t.sem("qkv_made")
        qv_ready = t.sem("qv_ready")
        prod_ready = t.sem("prod_ready")
        corr_made, corr_ready = t.sem("corr_made"), t.sem("corr_ready")
        top_link = t.sem("top_link")
        below_ready = t.sem("below_ready")
        ew_ready = t.sem("ew_ready")
        mix_ready = t.sem("mix_ready")
        mixT_made, mixT_ready = t.sem("mixT_made"), t.sem("mixT_ready")
        rolled_made, rolled_ready = t.sem("rolled_made"), t.sem("rolled_ready")
        out_made, out_added = t.sem("out_made"), t.sem("out_added")
        TOP_LINKS = 9

        block = ctx.enter_context(nc.Block())

        @block.sync
        def _(sp):
            for w, name in ((wq, "wq"), (wk, "wk"), (wv, "wv"), (wo, "wo")):
                sp.dma_start(w[:], A[f"L0_xattn_{name}"].rearrange("(c p) n -> p c n", p=P)).then_inc(consts_in, 16)
            for tile, name in ((dft, "dft"), (iota, "iota"), (row_mod, "row_mod"), (ident, "ident")):
                sp.dma_start(tile[:], K[name]).then_inc(consts_in, 16)
            sp.dma_start(idft[:], K["idft"].rearrange("p (a n) -> p a n", a=2)).then_inc(consts_in, 16)
            sp.dma_start(head_mask[:], K["head_mask"].rearrange("p (a n) -> p a n", a=HC)).then_inc(consts_in, 16)
            load_context(sp, t, 0, 0)
            load_context(sp, t, 1, 1)

            def step(n, parity, one_ahead, two_ahead):
                if two_ahead:
                    load_context(sp, t, n + 2, parity)
            walk(sp, step)
        CONSTS = 10 * 16

        @block.tensor
        def _(pe):
            def spectra(n, parity):
                pe.wait_ge(t.xn_ready, n + 1)
                pe.wait_ge(t.ctx_ready[parity], context_count(n, parity))
                enough(pe, spec_ready, n)
                for c in range(C):
                    cs = slice(c * P, (c + 1) * P)
                    pe.matmul(ps_spec[:, c, 0:P], t.xn[:, parity, cs], dft[:, 0:P], start=True, stop=True)
                    last = pe.matmul(ps_spec[:, c, P:FX], t.ctx_in[:, parity, cs], dft[:], start=True, stop=True)
                last.then_inc(spec_made, 1)

            def project(n, parity):
                pe.wait_ge(spec_ready, n + 1)
                enough(pe, prod_ready, n)
                for c in range(C):
                    pe.matmul(ps_qv[:, 0:D], specT[:, parity, c, 0:P], wq[:, c, :], start=c == 0, stop=c == C - 1)
                for m in range(C):
                    for c in range(C):
                        pe.matmul(ps_qv[:, D + m * P:D + (m + 1) * P], wv[:, c, m * P:(m + 1) * P],
                                  specT[:, parity, c, 2 * P:3 * P], start=c == 0, stop=c == C - 1)
                for a, at in ((0, P), (1, 3 * P)):
                    for c in range(C):
                        last = pe.matmul(ps_k[:, a, :], specT[:, parity, c, at:at + P], wk[:, c, :],
                                         start=c == 0, stop=c == C - 1)
                last.then_inc(qkv_made, 1)

            def correlate(n, parity):
                pe.wait_ge(prod_ready, n + 1)
                enough(pe, corr_ready, n)
                for c in range(C):
                    for a in range(2):
                        last = pe.matmul(ps_corr[:, c, :], prod[:, parity, a, c * P:(c + 1) * P], idft[:, a, :],
                                         start=a == 0, stop=a == 1)
                last.then_inc(corr_made, 1)

            def turn_mix(n, parity):
                pe.wait_ge(mix_ready, n + 1)
                enough(pe, mixT_ready, n)
                for c in range(C):
                    last = pe.transpose(ps_mixT[:, c, :], mix_block[:, parity, c].rearrange("p h d -> p (h d)"),
                                        ident[:])
                last.then_inc(mixT_made, 1)

            def roll_values(n, parity):
                pe.wait_ge(mixT_ready, n + 1)
                enough(pe, rolled_ready, n)
                for c in range(C):
                    last = pe.matmul(ps_rolled[:, c * HC // 2:(c + 1) * HC // 2].rearrange("p k a d -> p (k a d)"),
                                     qv[:, parity, D + c * P:D + (c + 1) * P], mixT[:, parity, c, :],
                                     start=True, stop=True)
                last.then_inc(rolled_made, 1)

            def output(n, parity):
                pe.wait_ge(rolled_ready, n + 1)
                enough(pe, out_added, n)
                for a in range(2):
                    last = pe.matmul(ps_out[:], rolled[:, parity, a].rearrange("p d k -> p (d k)"), wo[:, a, :],
                                     start=a == 0, stop=a == 1)
                last.then_inc(out_made, 1)

            pe.wait_ge(consts_in, CONSTS)
            spectra(0, 0)
            project(0, 0)
            spectra(1, 1)
            correlate(0, 0)

            def step(n, parity, one_ahead, two_ahead):
                if one_ahead:
                    project(n + 1, 1 - parity)
                turn_mix(n, parity)
                if two_ahead:
                    spectra(n + 2, parity)
                roll_values(n, parity)
                if one_ahead:
                    correlate(n + 1, 1 - parity)
                output(n, parity)
            walk(pe, step)

        @block.scalar
        def _(act):
            def spectra_out(n, parity):
                act.wait_ge(spec_made, n + 1)
                enough(act, qkv_made, n - 1)
                act.activation(specT[:, parity], ps_spec[:], ACT.Copy).then_inc(spec_ready, 1)

            def qv_out(n, parity):
                act.wait_ge(qkv_made, n + 1)
                enough(act, rolled_made, n - 1)
                act.activation(qv[:, parity], ps_qv[:], ACT.Copy).then_inc(qv_ready, 1)

            def correlation_out(n, parity):
                act.wait_ge(corr_made, n + 1)
                enough(act, mix_ready, n - 1)
                act.activation(corr[:, parity], ps_corr[:], ACT.Copy).then_inc(corr_ready, 1)

            def weights(n, parity):
                act.wait_ge(below_ready, n + 1)
                enough(act, mix_ready, n)
                act.activation(ew[:], below[:], ACT.Exp).then_inc(ew_ready, 1)

            def mixT_out(n, parity):
                act.wait_ge(mixT_made, n + 1)
                enough(act, rolled_made, n - 1)
                act.activation(mixT[:, parity], ps_mixT[:], ACT.Copy).then_inc(mixT_ready, 1)

            def rolled_out(n, parity):
                act.wait_ge(rolled_made, n + 1)
                enough(act, out_made, n - 1)
                act.activation(rolled[:, parity], ps_rolled[:].rearrange("p k a d -> p a d k"),
                               ACT.Copy).then_inc(rolled_ready, 1)

            spectra_out(0, 0)
            qv_out(0, 0)
            spectra_out(1, 1)
            correlation_out(0, 0)

            def step(n, parity, one_ahead, two_ahead):
                weights(n, parity)
                if one_ahead:
                    qv_out(n + 1, 1 - parity)
                mixT_out(n, parity)
                if two_ahead:
                    spectra_out(n + 2, parity)
                rolled_out(n, parity)
                if one_ahead:
                    correlation_out(n + 1, 1 - parity)
            walk(act, step)

        @block.vector
        def _(dve):
            def products(n, parity):
                dve.wait_ge(qv_ready, n + 1)
                enough(dve, corr_made, n - 1)
                dve.tensor_tensor(prod[:, parity], qv[:, parity, 0:D].unsqueeze(1).to_broadcast([P, 2, D]), ps_k[:],
                                  ALU.mult).then_inc(prod_ready, 1)

            def make_mix(n, parity):
                link = Links(dve, top_link, TOP_LINKS, n)
                dve.max(top[:, 0, :], corr[:, parity, 0, :])
                link(dve.max(top[:, 1, :], corr[:, parity, 1, :]))
                dve.tensor_tensor(below[:], top[:, :, 0:4], top[:, :, 0:1].to_broadcast([P, C, 4]),
                                  ALU.subtract).then_inc(below_ready, 1)
                dve.max_index(lag[:, 0, :], top[:, 0, :], corr[:, parity, 0, :])
                link(dve.max_index(lag[:, 1, :], top[:, 1, :], corr[:, parity, 1, :]))
                link(dve.tensor_scalar(src_f[:], lag[:, :, 0:4], -1.0, row_mod[:, 0:1], ALU.mult, ALU.add))
                link(dve.tensor_copy(src_i[:], src_f[:]))
                link(dve.tensor_scalar(src[:], src_i[:], DH - 1, None, ALU.bitwise_and))
                link(dve.tensor_tensor(hit[:], iota[:].unsqueeze(1).unsqueeze(3).to_broadcast([P, C, DH, 4]),
                                       src[:].unsqueeze(2).to_broadcast([P, C, DH, 4]), ALU.is_equal))
                dve.wait_ge(ew_ready, n + 1)
                dve.tensor_tensor(hit_w[:], hit[:], ew[:].unsqueeze(2).to_broadcast([P, C, DH, 4]), ALU.mult)
                link(dve.tensor_reduce(ew_sum[:], ew[:], AX.X, ALU.add))
                dve.tensor_reduce(mix[:], hit_w[:], AX.X, ALU.add)
                link(dve.reciprocal(ew_inv[:], ew_sum[:]))
                link(dve.tensor_tensor(mix_n[:], mix[:], ew_inv[:].unsqueeze(2).to_broadcast([P, C, DH]), ALU.mult))
                enough(dve, mixT_made, n - 1)
                for c in range(C):
                    last = dve.tensor_tensor(mix_block[:, parity, c], head_mask[:],
                                             mix_n[:, c, :].unsqueeze(1).to_broadcast([P, HC, DH]), ALU.mult)
                last.then_inc(mix_ready, 1)
                link.done()

            layernorm_begin(dve, t)
            for n in range(2):
                layernorm_apply(dve, t, n, n)
            dve.wait_ge(consts_in, CONSTS)
            products(0, 0)

            def step(n, parity, one_ahead, two_ahead):
                dve.wait_ge(corr_ready, n + 1)
                if two_ahead:
                    layernorm_apply(dve, t, n + 2, parity)
                make_mix(n, parity)
                if one_ahead:
                    products(n + 1, 1 - parity)
                if not (isinstance(n, int) and n == 0):
                    add_to_x(dve, t, n - 1, ps_out[:], out_made, out_added)
            walk(dve, step)
            add_to_x(dve, t, B - 1, ps_out[:], out_made, out_added)


HUGE_NEGATIVE = -1e30
R = 4
HR = H // R
BANK_PAIRS = ((0, 1), (2, 3))


def attention(nc, env, layer, windowed=False, rotary=False):
    A, K = env.inputs, env.consts
    SCALE = float(DH) ** -0.5
    with ExitStack() as ctx:
        t = Tiles(nc, ctx, f"at{layer}")
        layernorm_tiles(t, env)
        context_tiles(t, A["ctx_1024"])
        t.add_link = t.sem("add_link")
        w_raw = t.sb("w_raw", [P, 4, C, D])
        wT = t.sb("wT", [P, 4, C, D])
        ident = t.sb("ident", [P, P])
        ident_b = t.sb("ident_b", [P, P], BF16)
        slot_sel = t.sb("slot_sel", [P, R, 4, P], BF16)
        head_of_row = t.sb("head_of_row", [P, HC])
        bias_cols = t.sb("bias_cols", [P, 2, C])
        bv = t.sb("bv", [P, D])
        bo = t.sb("bo", [P, D])
        xcT = t.sb("xcT", [P, 2, 2, C, P])
        qT = t.sb("qT", [P, C, P])
        kT = t.sb("kT", [P, C, P])
        k_parts = t.sb("k_parts", [P, 2, 2, C, P], F16)
        qz = t.sb("qz", [P, C, HC, P])
        qz_high = t.sb("qz_high", [P, 2, C, HC, P], F16)
        qz_low = t.sb("qz_low", [P, 2, C, HC, P], F16)
        v1 = t.sb("v1", [P, 2, H, 32])
        neg_max = t.sb("neg_max", [P, R, 32], BF16)
        neg_maxT = t.sb("neg_maxT", [P, P], BF16)
        probT = t.sb("probT", [P, R, HR, P])
        sumsT = t.sb("sumsT", [P, HR, P])
        inv_sum = t.sb("inv_sum", [P, HR, R, 1])
        att = t.sb("att", [P, D])
        attT = t.sb("attT", [P, C, P])
        change = t.sb("change", [P, D])

        ps_sc = t.ps("ps_sc", [P, R, 4, P])
        ps_a = t.ps("ps_a", [P, 2, C, P])
        ps_qk = t.ps("ps_qk", [P, 2, C, P])
        ps_d = t.ps("ps_d", [P, 4, P])
        ps_sums = ps_d[:].rearrange("p j (r i) -> p j r i", r=R)
        ps_v = ps_qk[:, 0].rearrange("p c l -> p (c l)")
        ps_max = ps_a[:, 0, 0, 0:P // 2].bitcast(BF16)
        flat = "p c l -> p (c l)"

        consts_in, weights_in = t.sem("consts_in"), t.sem("weights_in")
        made_consts = t.sem("made_consts")
        w_turned, w_ready = t.sem("w_turned"), t.sem("w_ready")
        turned, xcT_ready = t.sem("turned"), t.sem("xcT_ready")
        qk_made, q_ready, k_ready = (t.sem(n) for n in ("qk_made", "q_ready", "k_ready"))
        v_made, v_ready = t.sem("v_made"), t.sem("v_ready")
        scores_made, max_ready = t.sem("scores_made"), t.sem("max_ready")
        max_turned, maxT_ready = t.sem("max_turned"), t.sem("maxT_ready")
        shifted_made, prob_ready = t.sem("shifted_made"), t.sem("prob_ready")
        q_high_ready, q_low_ready, q_link = t.sem("q_high_ready"), t.sem("q_low_ready"), t.sem("q_link")
        k_high_ready, k_low_ready = t.sem("k_high_ready"), t.sem("k_low_ready")
        pv_made, sumsT_ready, sums_turned = t.sem("pv_made"), t.sem("sumsT_ready"), t.sem("sums_turned")
        att_link, att_ready = t.sem("att_link"), t.sem("att_ready")
        att_turned, attT_ready = t.sem("att_turned"), t.sem("attT_ready")
        out_made, out_taken, out_added = t.sem("out_made"), t.sem("out_taken"), t.sem("out_added")
        t.xn_used = t.ctx_used = turned
        consts = [(ident, "ident"), (head_of_row, "head_of_row")]
        if windowed:
            window = t.sb("window", [P, P])
            window_b = t.sb("window_b", [P, P], BF16)
            consts.append((window, "window"))
        if rotary:
            cosT, sinT, rot = t.sb("cosT", [P, P]), t.sb("sinT", [P, P]), t.sb("rot", [P, P])
            consts += [(cosT, "cosT"), (sinT, "sinT"), (rot, "rot")]
            wT_rot = t.sb("wT_rot", [P, 2, C, D])
            bias_rot = t.sb("bias_rot", [P, 2, C])
            ps_rot = t.ps("ps_rot", [P, 2, C, P])
            by_cos = t.sb("by_cos", [P, 2, C, P])
            by_sin = t.sb("by_sin", [P, 2, C, P])
            rope_link = t.sem("rope_link")
        CONSTS = 16 * (len(consts) + 4)
        MADE = 3 + windowed
        W_TURNED = 4 + (3 if rotary else 0)
        block = ctx.enter_context(nc.Block())

        @block.sync
        def _(sp):
            for i, name in enumerate(("Wq", "Wk", "Wv", "Wo")):
                sp.dma_start(w_raw[:, i], A[f"L{layer}_xattn_{name}"].rearrange("(c p) n -> p c n", p=P)).then_inc(weights_in, 16)
            for tile, name in consts:
                sp.dma_start(tile[:], K[name]).then_inc(consts_in, 16)
            for i, name in enumerate(("bq", "bk")):
                sp.dma_start(bias_cols[:, i], A[f"L{layer}_xattn_{name}"].rearrange("(c p) -> p c", p=P),
                             allow_slow_non_contiguous=True).then_inc(consts_in, 16)
            for tile, name in ((bv, "bv"), (bo, "bo")):
                sp.dma_start(tile[:], A[f"L{layer}_xattn_{name}"].unsqueeze(0).to_broadcast([P, D])).then_inc(consts_in, 16)
            load_context(sp, t, 0, 0)
            load_context(sp, t, 1, 1)

            def step(n, parity, one_ahead, two_ahead):
                if two_ahead:
                    load_context(sp, t, n + 2, parity)
            walk(sp, step)

        @block.tensor
        def _(pe):
            def turn_weights():
                pe.wait_ge(consts_in, CONSTS)
                pe.wait_ge(weights_in, 64)
                for i in range(4):
                    for k in range(C):
                        for o in range(C):
                            last = pe.transpose(ps_sc[:, i].rearrange("p a l -> p (a l)")[:, (k * C + o) * P:(k * C + o + 1) * P],
                                                w_raw[:, i, o, k * P:(k + 1) * P], ident[:])
                    last.then_inc(w_turned, 1)
                if rotary:
                    for i, ps in enumerate((ps_qk, ps_rot)):
                        for k in range(C):
                            for o in range(C):
                                last = pe.matmul(ps[:, k, o], w_raw[:, i, o, k * P:(k + 1) * P], rot[:], start=True, stop=True)
                        last.then_inc(w_turned, 1)
                    pe.matmul(ps_a[:, 0, 0, 0:4], rot[:], bias_cols[:].rearrange("p a c -> p (a c)"),
                              start=True, stop=True).then_inc(w_turned, 1)

            def turn_inputs(n, parity):
                pe.wait_ge(t.xn_ready, n + 1)
                pe.wait_ge(t.ctx_ready[parity], context_count(n, parity))
                enough(pe, xcT_ready, n)
                enough(pe, out_taken, n - 3)
                for c in range(C):
                    cs = slice(c * P, (c + 1) * P)
                    pe.transpose(ps_a[:, 0, c], t.xn[:, parity, cs], ident[:])
                    last = pe.transpose(ps_a[:, 1, c], t.ctx_in[:, parity, cs], ident[:])
                last.then_inc(turned, 1)

            def project_heads(n, parity):
                pe.wait_ge(xcT_ready, n + 1)
                enough(pe, v_ready, n)
                for i in range(2):
                    for o in range(C):
                        for k in range(C):
                            last = pe.matmul(ps_qk[:, i, o], wT[:, i, k, o * P:(o + 1) * P], xcT[:, parity, i, k],
                                             start=k == 0, stop=k == C - 1)
                        if rotary:
                            for k in range(C):
                                last = pe.matmul(ps_rot[:, i, o], wT_rot[:, i, k, o * P:(o + 1) * P], xcT[:, parity, i, k],
                                                 start=k == 0, stop=k == C - 1)
                last.then_inc(qk_made, 1)

            def project_values(n, parity):
                if rotary:
                    pe.wait_ge(rope_link, n + 1)
                else:
                    pe.wait_ge(k_ready, n + 1)
                for k in range(C):
                    last = pe.matmul(ps_v, xcT[:, parity, 1, k], wT[:, 2, k], start=k == 0, stop=k == C - 1)
                last.then_inc(v_made, 1)

            def add_window(banks):
                for r in banks:
                    pe.matmul(ps_sc[:, r], ident_b[:], window_b[:].unsqueeze(1).to_broadcast([P, 4, P]),
                              start=True, stop=False, skip_group_check=True)

            def scores(n, parity):
                pe.wait_ge(k_high_ready, n + 1)
                pe.wait_ge(q_high_ready, n + 1)
                for c, banks in enumerate(BANK_PAIRS):
                    enough(pe, prob_ready, R * (n - 1) + banks[1] + 1)
                    if windowed:
                        add_window(banks)
                    for i in range(HC):
                        last = pe.matmul(ps_sc[:, banks[i // HR], i % HR], qz_high[:, parity, c, i], k_parts[:, parity, 0, c],
                                         start=not windowed, stop=True, skip_group_check=windowed)
                    last.then_inc(scores_made, 1)

            def turn_maxima(n, inputs):
                pe.wait_ge(max_ready, 2 * (n + 1))
                pe.wait_ge(xcT_ready, inputs)
                enough(pe, out_taken, n - 2)
                pe.transpose(ps_max, neg_max[:].rearrange("p r i -> p (r i)"), ident_b[:]).then_inc(max_turned, 1)

            def shifted_scores(n, parity, r):
                c, half = r // 2, r % 2
                pe.wait_ge(maxT_ready, n + 1)
                pe.wait_ge(k_low_ready, n + 1)
                pe.wait_ge(q_low_ready, n + 1)
                if windowed:
                    add_window((r,))
                for a, (k, q) in enumerate(SPLIT):
                    pe.matmul(ps_sc[:, r], k_parts[:, parity, k, c],
                              (qz_low if q else qz_high)[:, parity, c, HR * half:HR * (half + 1)],
                              start=a == 0 and not windowed, stop=False, skip_group_check=True)
                for j in range(HR):
                    last = pe.matmul(ps_sc[:, r, j], slot_sel[:, r, j], neg_maxT[:],
                                     start=False, stop=True, skip_group_check=True)
                last.then_inc(shifted_made, 1)

            def weigh_values(n, parity):
                pe.wait_ge(prob_ready, R * (n + 1))
                pe.wait_ge(v_ready, n + 1)
                enough(pe, att_ready, n)
                for j in range(HR):
                    for r in range(R):
                        last = pe.matmul(ps_d[32 * r:32 * r + 32, j], v1[:, parity, HR * r + j], probT[:, r, j],
                                         start=True, stop=True)
                last.then_inc(pv_made, 1)

            def turn_sums(n):
                pe.wait_ge(sumsT_ready, n + 1)
                for j in range(HR):
                    last = pe.transpose(ps_d[:, j], sumsT[:, j], ident[:])
                last.then_inc(sums_turned, 1)

            def turn_attended(n):
                pe.wait_ge(att_ready, n + 1)
                enough(pe, out_taken, n)
                for c in range(C):
                    last = pe.transpose(ps_a[:, 0, c], att[:, c * P:(c + 1) * P], ident[:])
                last.then_inc(att_turned, 1)

            def output(n):
                pe.wait_ge(attT_ready, n + 1)
                for c in range(C):
                    last = pe.matmul(ps_a[:, 0].rearrange(flat), attT[:, c], wT[:, 3, c], start=c == 0, stop=c == C - 1)
                last.then_inc(out_made, 1)

            turn_weights()
            pe.wait_ge(w_ready, W_TURNED)
            pe.wait_ge(made_consts, MADE)
            turn_inputs(0, 0)
            project_heads(0, 0)
            project_values(0, 0)

            def step(n, parity, one_ahead, two_ahead):
                behind = not (isinstance(n, int) and n == 0)
                two_behind = not (isinstance(n, int) and n <= 1)
                if one_ahead:
                    turn_inputs(n + 1, 1 - parity)
                scores(n, parity)
                if one_ahead:
                    project_heads(n + 1, 1 - parity)
                if behind:
                    weigh_values(n - 1, 1 - parity)
                turn_maxima(n, n + 2 if one_ahead else B)
                if one_ahead and not rotary:
                    project_values(n + 1, 1 - parity)
                shifted_scores(n, parity, 0)
                shifted_scores(n, parity, 1)
                if one_ahead and rotary:
                    project_values(n + 1, 1 - parity)
                if two_behind:
                    turn_attended(n - 2)
                if behind:
                    turn_sums(n - 1)
                shifted_scores(n, parity, 2)
                if two_behind:
                    output(n - 2)
                shifted_scores(n, parity, 3)
            walk(pe, step)
            turn_attended(B - 2)
            weigh_values(B - 1, 1)
            output(B - 2)
            turn_sums(B - 1)
            turn_attended(B - 1)
            output(B - 1)

        @block.scalar
        def _(act):
            def inputs_out(n, parity):
                act.wait_ge(turned, n + 1)
                enough(act, v_made, n - 1)
                act.activation(xcT[:, parity], ps_a[:], ACT.Copy).then_inc(xcT_ready, 1)

            def heads_out(n, parity):
                if rotary:
                    return
                act.wait_ge(qk_made, n + 1)
                enough(act, q_high_ready, n)
                enough(act, q_low_ready, n)
                for c in range(C):
                    last = act.activation(qT[:, c], ps_qk[:, 0, c], ACT.Identity, bias=bias_cols[:, 0, c:c + 1])
                last.then_inc(q_ready, 1)
                enough(act, k_low_ready, n)
                for c in range(C):
                    last = act.activation(kT[:, c], ps_qk[:, 1, c], ACT.Identity, bias=bias_cols[:, 1, c:c + 1])
                last.then_inc(k_ready, 1)

            def maxima_out(n):
                act.wait_ge(max_turned, n + 1)
                enough(act, shifted_made, R * n)
                act.activation(neg_maxT[:], ps_max, ACT.Copy).then_inc(maxT_ready, 1)

            def sums_out(n):
                act.wait_ge(pv_made, n + 1)
                enough(act, sums_turned, n)
                act.activation(sumsT[:], ps_d[:], ACT.Copy).then_inc(sumsT_ready, 1)

            def exponentials(n, c):
                enough(act, pv_made, n)
                for r in BANK_PAIRS[c]:
                    act.wait_ge(shifted_made, R * n + r + 1)
                    act.activation(probT[:, r], ps_sc[:, r], ACT.Exp, scale=SCALE).then_inc(prob_ready, 1)

            def attended_out(n):
                act.wait_ge(att_turned, n + 1)
                enough(act, out_made, n)
                act.activation(attT[:], ps_a[:, 0], ACT.Copy).then_inc(attT_ready, 1)

            for i in range(4):
                act.wait_ge(w_turned, i + 1)
                act.activation(wT[:, i].rearrange("p c n -> p (c n)"), ps_sc[:, i].rearrange("p a l -> p (a l)"),
                               ACT.Copy).then_inc(w_ready, 1)
            if rotary:
                for i, ps in enumerate((ps_qk, ps_rot)):
                    act.wait_ge(w_turned, 5 + i)
                    act.activation(wT_rot[:, i].rearrange("p c n -> p (c n)"), ps[:].rearrange("p a c l -> p (a c l)"),
                                   ACT.Copy).then_inc(w_ready, 1)
                act.wait_ge(w_turned, 7)
                act.activation(bias_rot[:].rearrange("p a c -> p (a c)"), ps_a[:, 0, 0, 0:4], ACT.Copy).then_inc(w_ready, 1)
            act.wait_ge(made_consts, MADE)
            inputs_out(0, 0)
            heads_out(0, 0)

            def step(n, parity, one_ahead, two_ahead):
                behind = not (isinstance(n, int) and n == 0)
                two_behind = not (isinstance(n, int) and n <= 1)
                if one_ahead:
                    inputs_out(n + 1, 1 - parity)
                    heads_out(n + 1, 1 - parity)
                maxima_out(n)
                if behind:
                    sums_out(n - 1)
                exponentials(n, 0)
                if two_behind:
                    attended_out(n - 2)
                exponentials(n, 1)
            walk(act, step)
            attended_out(B - 2)
            sums_out(B - 1)
            attended_out(B - 1)

        @block.vector
        def _(dve):
            def prepare():
                dve.memset(neg_max[:], 0.0).then_inc(made_consts, 1)
                dve.memset(v1[:], 1.0).then_inc(made_consts, 1)
                dve.wait_ge(consts_in, CONSTS)
                if windowed:
                    dve.tensor_copy(window_b[:], window[:]).then_inc(made_consts, 1)
                dve.tensor_copy(ident_b[:], ident[:])
                dve.tensor_copy(slot_sel[:], ident[:].rearrange("p (r i) -> p r i", r=R)[:, :, 0:4].unsqueeze(3)
                                .to_broadcast([P, R, 4, P])).then_inc(made_consts, 1)
                dve.wait_ge(made_consts, MADE)

            def rope(n, parity):
                link = Links(dve, rope_link, 1, n)
                dve.wait_ge(qk_made, n + 1)
                for i in range(2):
                    for c in range(C):
                        dve.scalar_tensor_tensor(by_cos[:, i, c], ps_qk[:, i, c], bias_cols[:, i, c:c + 1], cosT[:], ALU.add, ALU.mult)
                        last = dve.scalar_tensor_tensor(by_sin[:, i, c], ps_rot[:, i, c], bias_rot[:, i, c:c + 1], sinT[:], ALU.add, ALU.mult)
                link(last)
                link.done()
                enough(dve, k_low_ready, n)
                dve.tensor_tensor(kT[:], by_cos[:, 1], by_sin[:, 1], ALU.add).then_inc(k_ready, 1)
                enough(dve, q_high_ready, n)
                enough(dve, q_low_ready, n)
                dve.tensor_tensor(qT[:], by_cos[:, 0], by_sin[:, 0], ALU.add).then_inc(q_ready, 1)

            def spread_heads(n, parity):
                dve.wait_ge(k_ready, n + 1)
                enough(dve, shifted_made, R * (n - 1))
                dve.tensor_copy(k_parts[:, parity, 0], kT[:]).then_inc(k_high_ready, 1)
                dve.wait_ge(q_ready, n + 1)
                dve.tensor_tensor(qz_high[:, parity], qT[:].unsqueeze(2).to_broadcast([P, C, HC, P]),
                                  head_of_row[:].unsqueeze(1).unsqueeze(3).to_broadcast([P, C, HC, P]),
                                  ALU.mult).then_inc(q_high_ready, 1)
                dve.wait_ge(k_high_ready, n + 1)
                dve.tensor_tensor(k_parts[:, parity, 1], kT[:], k_parts[:, parity, 0], ALU.subtract).then_inc(k_low_ready, 1)

            def values_out(n, parity):
                dve.wait_ge(v_made, n + 1)
                enough(dve, pv_made, n - 1)
                dve.tensor_tensor(v1[:, parity, :, 0:DH], ps_v.rearrange("p (h d) -> p h d", d=DH),
                                  bv[:].rearrange("p (h d) -> p h d", d=DH), ALU.add).then_inc(v_ready, 1)

            def maxima(n):
                for pair, banks in enumerate(BANK_PAIRS):
                    bs = slice(banks[0], banks[1] + 1)
                    dve.wait_ge(scores_made, 2 * n + pair + 1)
                    enough(dve, max_turned, n)
                    dve.tensor_reduce(neg_max[:, bs, 0:4], ps_sc[:, bs], AX.X, ALU.max, negate=True).then_inc(max_ready, 1)

            def normalise(n):
                link = Links(dve, att_link, 1, n)
                dve.wait_ge(sums_turned, n + 1)
                link(dve.reciprocal(inv_sum[:], ps_sums[:, :, :, DH:DH + 1]))
                link.done()
                enough(dve, att_turned, n)
                dve.tensor_tensor(att[:].rearrange("p (r j d) -> p j r d", r=R, j=HR), ps_sums[:, :, :, 0:DH],
                                  inv_sum[:].to_broadcast([P, HR, R, DH]), ALU.mult).then_inc(att_ready, 1)

            def add_output(n):
                link = Links(dve, out_taken, 1, n)
                dve.wait_ge(out_made, n + 1)
                link(dve.tensor_tensor(change[:], ps_a[:, 0].rearrange(flat), bo[:], ALU.add))
                link.done()
                add_to_x(dve, t, n, change[:], out_made, out_added)

            layernorm_begin(dve, t)
            prepare()
            for n in range(2):
                layernorm_apply(dve, t, n, n)
            if rotary:
                rope(0, 0)
            spread_heads(0, 0)
            values_out(0, 0)

            def step(n, parity, one_ahead, two_ahead):
                maxima(n)
                if one_ahead:
                    if rotary:
                        rope(n + 1, 1 - parity)
                    spread_heads(n + 1, 1 - parity)
                if two_ahead:
                    layernorm_apply(dve, t, n + 2, parity)
                if one_ahead:
                    values_out(n + 1, 1 - parity)
                if not (isinstance(n, int) and n == 0):
                    normalise(n - 1)
                if not (isinstance(n, int) and n <= 1):
                    add_output(n - 2)
            walk(dve, step)
            add_output(B - 2)
            normalise(B - 1)
            add_output(B - 1)

        @block.gpsimd
        def _(pool):
            def spread_heads(n, parity):
                link = Links(pool, q_link, 1, n)
                pool.wait_ge(q_ready, n + 1)
                link(pool.tensor_tensor(qz[:], qT[:].unsqueeze(2).to_broadcast([P, C, HC, P]),
                                        head_of_row[:].unsqueeze(1).unsqueeze(3).to_broadcast([P, C, HC, P]), ALU.mult))
                link.done()
                pool.wait_ge(q_high_ready, n + 1)
                enough(pool, shifted_made, R * (n - 1))
                pool.tensor_tensor(qz_low[:, parity], qz[:], qz_high[:, parity], ALU.subtract).then_inc(q_low_ready, 1)

            pool.wait_ge(consts_in, CONSTS)
            spread_heads(0, 0)

            def step(n, parity, one_ahead, two_ahead):
                if one_ahead:
                    spread_heads(n + 1, 1 - parity)
            walk(pool, step)


def windowed_attention(nc, env):
    attention(nc, env, 1, windowed=True)


def full_attention(nc, env):
    attention(nc, env, 2)


def rotary_attention(nc, env):
    attention(nc, env, 3, rotary=True)


def turned_tiles(t):
    t.xT = t.sb("xT", [P, C, B, L])
    t.ps_x = t.ps("ps_x", [P, 2, 512])
    t.x_turned = t.sem("x_turned")
    t.xT_ready = t.sem("xT_ready")
    t.xn_used = t.x_turned


def turn_x(pe, t, ident):
    def step(n, parity, one_ahead, two_ahead):
        pe.wait_ge(t.xn_ready, n + 1)
        enough(pe, t.xT_ready, n - 1)
        for c in range(C):
            last = pe.transpose(t.ps_x[:, parity, c * P:(c + 1) * P], t.xn[:, parity, c * P:(c + 1) * P], ident[:])
        last.then_inc(t.x_turned, 1)
    walk(pe, step)


def turned_x_out(act, t, high=None):
    def step(n, parity, one_ahead, two_ahead):
        act.wait_ge(t.x_turned, n + 1)
        if high is not None:
            act.activation(high[:, :, n, :], t.ps_x[:, parity, 0:D].rearrange("p (c l) -> p c l", c=C), ACT.Copy)
        act.activation(t.xT[:, :, n, :], t.ps_x[:, parity, 0:D].rearrange("p (c l) -> p c l", c=C),
                       ACT.Copy).then_inc(t.xT_ready, 1)
    walk(act, step)


def receptance_ffn(nc, env):
    A, K = env.inputs, env.consts
    with ExitStack() as ctx:
        t = Tiles(nc, ctx, "rf")
        layernorm_tiles(t, env)
        t.add_link = t.sem("add_link")
        w_raw = t.sb("w_raw", [P, 3, C, D])
        wT = t.sb("wT", [P, 3, C, D])
        ident = t.sb("ident", [P, P])
        mu = t.sb("mu", [P, 2, C])
        mu_rest = t.sb("mu_rest", [P, 2, C])
        xT = t.sb("xT", [P, 2, C, 1 + L])
        now = t.sb("now", [P, 2, 2, C, L])
        mixedT = t.sb("mixedT", [P, 2, 2, C, L])
        keyT = t.sb("keyT", [P, 2, C, L])
        gate = t.sb("gate", [P, 2, D])
        change = t.sb("change", [P, D])
        ps_x = t.ps("ps_x", [P, C, L])
        ps_w = t.ps("ps_w", [P, 3, 512])
        ps_r, ps_k, ps_v = (t.ps(f"ps_{n}", [P, D]) for n in "rkv")

        consts_in, weights_in = t.sem("consts_in"), t.sem("weights_in")
        w_turned, w_ready, made_consts = t.sem("w_turned"), t.sem("w_ready"), t.sem("made_consts")
        turned, xT_ready = t.sem("turned"), t.sem("xT_ready")
        mixed_ready, key_in = t.sem("mixed_ready"), t.sem("key_in")
        rk_made, key_ready, gate_ready = t.sem("rk_made"), t.sem("key_ready"), t.sem("gate_ready")
        v_made, change_made, out_added = t.sem("v_made"), t.sem("change_made"), t.sem("out_added")
        t.xn_used = turned
        block = ctx.enter_context(nc.Block())

        @block.sync
        def _(sp):
            for i, name in enumerate(("W_r", "W_k", "W_v")):
                sp.dma_start(w_raw[:, i], A[f"L2_ffn_{name}"].rearrange("(c p) n -> p c n", p=P)).then_inc(weights_in, 16)
            sp.dma_start(ident[:], K["ident"]).then_inc(consts_in, 16)
            for i, name in enumerate(("mu_r", "mu_k")):
                sp.dma_start(mu[:, i], A[f"L2_ffn_{name}"].rearrange("(c p) -> p c", p=P),
                             allow_slow_non_contiguous=True).then_inc(consts_in, 16)

        @block.tensor
        def _(pe):
            def turn(n, parity):
                pe.wait_ge(t.xn_ready, n + 1)
                enough(pe, xT_ready, n)
                for c in range(C):
                    last = pe.transpose(ps_x[:, c], t.xn[:, parity, c * P:(c + 1) * P], ident[:])
                last.then_inc(turned, 1)

            def receptance_and_key(n, parity):
                pe.wait_ge(mixed_ready, n + 1)
                enough(pe, gate_ready, n)
                enough(pe, key_in, n)
                for k in range(C):
                    pe.matmul(ps_r[:], mixedT[:, parity, 0, k], wT[:, 0, k], start=k == 0, stop=k == C - 1)
                for o in range(C):
                    for k in range(C):
                        last = pe.matmul(ps_k[:, o * P:(o + 1) * P], wT[:, 1, k, o * P:(o + 1) * P],
                                         mixedT[:, parity, 1, k], start=k == 0, stop=k == C - 1)
                last.then_inc(rk_made, 1)

            def value(n, parity):
                pe.wait_ge(key_ready, n + 1)
                enough(pe, out_added, n)
                for k in range(C):
                    last = pe.matmul(ps_v[:], keyT[:, parity, k], wT[:, 2, k], start=k == 0, stop=k == C - 1)
                last.then_inc(v_made, 1)

            pe.wait_ge(consts_in, 48)
            pe.wait_ge(weights_in, 48)
            for i in range(3):
                for k in range(C):
                    for o in range(C):
                        last = pe.transpose(ps_w[:, i, (k * C + o) * P:(k * C + o + 1) * P],
                                            w_raw[:, i, o, k * P:(k + 1) * P], ident[:])
                last.then_inc(w_turned, 1)
            turn(0, 0)
            turn(1, 1)
            pe.wait_ge(w_ready, 3)
            receptance_and_key(0, 0)

            def step(n, parity, one_ahead, two_ahead):
                value(n, parity)
                if two_ahead:
                    turn(n + 2, parity)
                if one_ahead:
                    receptance_and_key(n + 1, 1 - parity)
            walk(pe, step)

        @block.scalar
        def _(act):
            def x_out(n, parity):
                act.wait_ge(turned, n + 1)
                enough(act, mixed_ready, n - 1)
                for i in range(2):
                    for c in range(C):
                        act.activation(now[:, parity, i, c], ps_x[:, c], ACT.Copy, scale=mu[:, i, c:c + 1])
                act.activation(xT[:, parity, :, 1:1 + L], ps_x[:], ACT.Copy).then_inc(xT_ready, 1)

            def key_and_gate_out(n, parity):
                act.wait_ge(rk_made, n + 1)
                enough(act, v_made, n - 1)
                act.activation(keyT[:, parity].rearrange("p c l -> p (c l)"), ps_k[:], ACT.Relu).then_inc(key_in, 1)
                enough(act, out_added, n - 1)
                act.activation(gate[:, parity], ps_r[:], ACT.Sigmoid).then_inc(gate_ready, 1)

            for i in range(3):
                act.wait_ge(w_turned, i + 1)
                act.activation(wT[:, i].rearrange("p c n -> p (c n)"), ps_w[:, i], ACT.Copy).then_inc(w_ready, 1)
            act.wait_ge(consts_in, 48)
            act.wait_ge(made_consts, 1)
            x_out(0, 0)
            x_out(1, 1)
            key_and_gate_out(0, 0)

            def step(n, parity, one_ahead, two_ahead):
                if two_ahead:
                    x_out(n + 2, parity)
                if one_ahead:
                    key_and_gate_out(n + 1, 1 - parity)
            walk(act, step)

        @block.vector
        def _(dve):
            def mix(n, parity):
                dve.wait_ge(xT_ready, n + 1)
                enough(dve, rk_made, n - 1)
                for i in range(2):
                    for c in range(C):
                        last = dve.scalar_tensor_tensor(mixedT[:, parity, i, c], xT[:, parity, c, 0:L],
                                                        mu_rest[:, i, c:c + 1], now[:, parity, i, c], ALU.mult, ALU.add)
                last.then_inc(mixed_ready, 1)

            def key(n, parity):
                flat = keyT[:, parity].rearrange("p c l -> p (c l)")
                dve.wait_ge(key_in, n + 1)
                dve.tensor_tensor(flat, flat, flat, ALU.mult).then_inc(key_ready, 1)

            def add_output(n, parity):
                dve.wait_ge(v_made, n + 1)
                dve.wait_ge(gate_ready, n + 1)
                dve.tensor_tensor(change[:], gate[:, parity], ps_v[:], ALU.mult).then_inc(change_made, 1)
                add_to_x(dve, t, n, change[:], change_made, out_added)

            dve.memset(xT[:], 0.0).then_inc(made_consts, 1)
            layernorm_begin(dve, t)
            dve.wait_ge(consts_in, 48)
            dve.tensor_scalar(mu_rest[:], mu[:], -1.0, 1.0, ALU.mult, ALU.add).then_inc(made_consts, 1)
            dve.wait_ge(made_consts, 2)
            for n in range(2):
                layernorm_apply(dve, t, n, n)
            mix(0, 0)

            def step(n, parity, one_ahead, two_ahead):
                key(n, parity)
                if two_ahead:
                    layernorm_apply(dve, t, n + 2, parity)
                if one_ahead:
                    mix(n + 1, 1 - parity)
                add_output(n, parity)
            walk(dve, step)


ROUND = 1.5 * 2.0 ** 23
FF = 768
FC = FF // P
QBLOCK = 32
NBLOCKS = FF * D // P // QBLOCK
G4 = B // 4


def quantised_ffn(nc, env):
    A, K = env.inputs, env.consts
    QMAX, WQMAX, SIG_STEPS = 2.0 ** 15 - 1, 7.0, 65536.0
    with ExitStack() as ctx:
        t = Tiles(nc, ctx, "qf")
        layernorm_tiles(t, env)
        t.add_link = t.sem("add_link")
        turned_tiles(t)
        ident = t.sb("ident", [P, P])
        upT = t.sb("upT", [P, FC, B, L])
        gateT = t.sb("gateT", [P, FC, B, L])
        w_inT = t.sb("w_inT", [P, 2, 2, C, FF], F16)
        w_outT = t.sb("w_outT", [P, 2, FC, D], F16)
        wmax = t.sb("wmax", [P, 3, NBLOCKS])
        wscale = t.sb("wscale", [P, 3, NBLOCKS])
        winv = t.sb("winv", [P, 3, NBLOCKS])
        part_max = t.sb("part_max", [P, 5, G4 * FC, 1])
        own_max = t.sb("own_max", [P, 5])
        all_max = t.sb("all_max", [P, 5])
        scale = t.sb("scale", [P, 5])
        inv = t.sb("inv", [P, 5])
        unscale = t.sb("unscale", [P, 2])
        rounder = t.sb("rounder", [P, 1])
        neg_rounder = t.sb("neg_rounder", [P, 1])
        sig = t.sb("sig", [P, 2, B * L])
        prod_r = t.sb("prod_r", [P, 2, FC, L])
        prodT = t.sb("prodT", [P, 2, 2, FC, L], F16)
        xqT = sig[:].rearrange("p a n -> p (a n)").bitcast(F16).rearrange("p (a c n) -> p a c n", a=2, c=C)
        raw = [gateT[:, i].rearrange("p b l -> p (b l)")[:, 0:FF * C] for i in range(2)]
        raw_t = [gateT[:, 2 + i].rearrange("p b l -> p (b l)")[:, 0:FF * C] for i in range(2)]
        raw.append(prod_r[:].rearrange("p a c l -> p (a c l)"))
        raw_t.append(prodT[:].rearrange("p a h c l -> p (a h c l)").bitcast(F32))
        ps = t.ps("ps", [P, 4, 512])
        ps_out = t.ps("ps_out", [P, 2, 512])

        XS, US, GS, SS, PS = range(5)
        SCALE_STEPS = 4
        consts_in, weights_in = t.sem("consts_in"), t.sem("weights_in")
        made_consts = t.sem("made_consts")
        w_link, w_quantised = t.sem("w_link"), t.sem("w_quantised")
        w_turned, w_high, w_ready = t.sem("w_turned"), t.sem("w_high"), t.sem("w_ready")
        x_high, prod_high, unscale_made = t.sem("x_high"), t.sem("prod_high"), t.sem("unscale_made")
        x_max, max_made, max_all, scale_made = t.sem("x_max"), t.sem("max_made"), t.sem("max_all"), t.sem("scale_made")
        x_scaled, x_ready = t.sem("x_scaled"), t.sem("x_ready")
        hidden_made, hidden_out, hidden_max = t.sem("hidden_made"), t.sem("hidden_out"), t.sem("hidden_max")
        gate_scaled, gate_ready = t.sem("gate_scaled"), t.sem("gate_ready")
        sig_made, sig_ready = t.sem("sig_made"), t.sem("sig_ready")
        up_scaled, up_ready = t.sem("up_scaled"), t.sem("up_ready")
        silu_link, silu_ready = t.sem("silu_link"), t.sem("silu_ready")
        silu_scaled, prod_ready = t.sem("silu_scaled"), t.sem("prod_ready")
        prod_scaled, prodT_ready = t.sem("prod_scaled"), t.sem("prodT_ready")
        prod_link = t.sem("prod_link")
        out_made, out_added = t.sem("out_made"), t.sem("out_added")
        block = ctx.enter_context(nc.Block())
        TILES = 2 * FC
        UP_TILES = 2 * TILES
        UPS = 3

        def weights_tile(part, m):
            flat = (w_inT[:, part].rearrange("p i k n -> p (i k n)") if m < 6 else
                    w_outT[:, part].rearrange("p c n -> p (c n)"))
            return flat[:, m % 6 * 512:(m % 6 + 1) * 512]

        @block.sync
        def _(sp):
            sp.dma_start(ident[:], K["ident"]).then_inc(consts_in, 16)
            for i, name in enumerate(("w_up", "w_gate", "w_down")):
                w = A[f"L0_ffn_{name}"]
                sp.dma_start(raw[i].rearrange("p (c n) -> p c n", n=w.shape[1]),
                             w.rearrange("(c p) n -> p c n", p=P)).then_inc(weights_in, 16)

        @block.gpsimd
        def _(pool):
            for i in range(5):
                pool.wait_ge(max_made, i + 1)
                pool.partition_all_reduce(all_max[:, i:i + 1], own_max[:, i:i + 1], P, RMAX).then_inc(max_all, 1)
                if i == GS:
                    for c in range(FC):
                        pool.wait_ge(gate_scaled, c + 1)
                        pool.tensor_scalar(gateT[:, c], gateT[:, c], -ROUND, scale[:, GS:GS + 1],
                                           ALU.add, ALU.mult).then_inc(gate_ready, 1)

        @block.tensor
        def _(pe):
            pe.wait_ge(consts_in, 16)
            turn_x(pe, t, ident)

            def turn_weights(i):
                pe.wait_ge(w_quantised, i + 1)
                for m in range(3):
                    if 3 * i + m >= 4:
                        pe.wait_ge(w_ready, 3 * i + m - 3)
                    for a in range(4):
                        if i < 2:
                            k, o = (4 * m + a) // FC, (4 * m + a) % FC
                            block_in = raw[i][:, o * D + k * P:o * D + (k + 1) * P]
                        else:
                            k, o = (4 * m + a) // C, (4 * m + a) % C
                            block_in = raw[i][:, o * FF + k * P:o * FF + (k + 1) * P]
                        last = pe.transpose(ps[:, (3 * i + m) % 4, a * P:(a + 1) * P], block_in, ident[:])
                    last.then_inc(w_turned, 1)

            XT = xqT.rearrange("p a c (h g n) -> p a c h g n", h=2, g=2)

            def hidden(i, h):
                for g in range(2):
                    for c in range(FC):
                        q, tile = UP_TILES * i + TILES * h + FC * g + c, FC * g + c
                        enough(pe, hidden_out, q - 3)
                        for k in range(C):
                            for a, (w, x) in enumerate(SPLIT):
                                last = pe.matmul(ps[:, tile % 4], w_inT[:, w, i, k, c * P:(c + 1) * P], XT[:, x, k, h, g],
                                                 start=(k, a) == (0, 0), stop=(k, a) == (C - 1, 2))
                        last.then_inc(hidden_made, 1)
            turn_weights(0)
            pe.wait_ge(w_ready, 3)
            pe.wait_ge(x_ready, C)
            hidden(0, 0)
            pe.wait_ge(hidden_out, TILES)
            turn_weights(1)
            pe.wait_ge(w_ready, 6)
            hidden(0, 1)
            with pe.Fori(0, 2) as h:
                hidden(1, h)
            pe.wait_ge(hidden_out, 2 * UP_TILES)
            turn_weights(2)
            pe.wait_ge(w_ready, 9)

            def step(n, parity, one_ahead, two_ahead):
                pe.wait_ge(prodT_ready, n + 1)
                enough(pe, out_added, n - 1)
                for c in range(FC):
                    for a, (x, w) in enumerate(SPLIT):
                        last = pe.matmul(ps_out[:, parity, 0:D], prodT[:, parity, x, c], w_outT[:, w, c],
                                         start=(c, a) == (0, 0), stop=(c, a) == (FC - 1, 2))
                last.then_inc(out_made, 1)
            walk(pe, step)

        @block.scalar
        def _(act):
            turned_x_out(act, t)
            act.wait_ge(made_consts, 2)
            act.wait_ge(scale_made, SCALE_STEPS * (XS + 1))
            act.wait_ge(t.xT_ready, B)
            for c in range(C):
                act.activation(t.xT[:, c], t.xT[:, c], ACT.Identity, bias=rounder[:], scale=inv[:, XS:XS + 1]).then_inc(x_scaled, 1)
            for c in range(C):
                act.wait_ge(x_scaled, c + 1)
                act.activation(xqT[:, 0, c], t.xT[:, c].rearrange("p b l -> p (b l)"), ACT.Identity,
                               bias=neg_rounder[:]).then_inc(x_high, 1)

            def weights_out(tiles):
                for m in tiles:
                    act.wait_ge(w_turned, m + 1)
                    act.activation(weights_tile(0, m), ps[:, m % 4], ACT.Copy, scale=W_SCALE).then_inc(w_high, 1)

            def hidden(i, h):
                to = (upT, gateT)[i][:].rearrange("p c (h g b) l -> p c h g (b l)", h=2, g=2)
                for g in range(2):
                    for c in range(FC):
                        tile = FC * g + c
                        act.wait_ge(hidden_made, UP_TILES * i + TILES * h + tile + 1)
                        act.activation(to[:, c, h, g], ps[:, tile % 4], ACT.Copy, scale=unscale[:, 0:1]).then_inc(hidden_out, 1)
                        if i == 1 and tile % 4 == 3:
                            act.activation(upT[:, UPS * h + tile // 4], upT[:, UPS * h + tile // 4], ACT.Identity,
                                           bias=rounder[:], scale=inv[:, US:US + 1]).then_inc(up_scaled, 1)
            weights_out(range(3))
            act.wait_ge(unscale_made, 1)
            hidden(0, 0)
            weights_out(range(3, 6))
            hidden(0, 1)
            act.wait_ge(scale_made, SCALE_STEPS * (US + 1))
            with act.Fori(0, 2) as h:
                hidden(1, h)

            def scale_gate(c):
                act.activation(gateT[:, c], gateT[:, c], ACT.Identity, bias=rounder[:], scale=inv[:, GS:GS + 1]).then_inc(gate_scaled, 1)
            act.wait_ge(scale_made, SCALE_STEPS * (GS + 1))
            scale_gate(0)
            for c in range(FC):
                if c + 1 < FC:
                    scale_gate(c + 1)
                act.wait_ge(gate_ready, c + 1)
                if c >= 2:
                    act.wait_ge(silu_ready, c - 1)
                act.activation(sig[:, c % 2], gateT[:, c].rearrange("p b l -> p (b l)"), ACT.Sigmoid).then_inc(sig_made, 1)
                act.wait_ge(sig_made, c + 1)
                act.activation(sig[:, c % 2], sig[:, c % 2], ACT.Identity, bias=rounder[:], scale=SIG_STEPS).then_inc(sig_ready, 1)
            weights_out(range(6, 9))
            act.wait_ge(scale_made, SCALE_STEPS * (SS + 1))
            for c in range(FC):
                act.activation(gateT[:, c], gateT[:, c], ACT.Identity, bias=rounder[:], scale=inv[:, SS:SS + 1]).then_inc(silu_scaled, 1)
            act.wait_ge(scale_made, SCALE_STEPS * (PS + 1))

            def step(n, parity, one_ahead, two_ahead):
                enough(act, prodT_ready, n - 1)
                act.activation(prod_r[:, parity], gateT[:, :, n, :], ACT.Identity, bias=rounder[:],
                               scale=inv[:, PS:PS + 1]).then_inc(prod_scaled, 1)
                act.wait_ge(prod_scaled, n + 1)
                enough(act, out_made, n - 1)
                act.activation(prodT[:, parity, 0], prod_r[:, parity], ACT.Identity, bias=neg_rounder[:]).then_inc(prod_high, 1)
            walk(act, step)

        @block.vector
        def _(dve):
            def quantise_weights(i):
                link = Links(dve, w_link, 5, i)
                w = raw[i].rearrange("p (m q) -> p m q", q=QBLOCK)
                wt = raw_t[i].rearrange("p (m q) -> p m q", q=QBLOCK)
                wide = [P, NBLOCKS, QBLOCK]
                dve.wait_ge(weights_in, 48)
                link(dve.tensor_reduce(wmax[:, i], w, AX.X, ALU.max, apply_absolute_value=True))
                link(dve.tensor_scalar(wscale[:, i], wmax[:, i], 1.0 / WQMAX, 1e-12, ALU.mult, ALU.max))
                link(dve.reciprocal(winv[:, i], wscale[:, i]))
                link(dve.tensor_tensor(wt, w, winv[:, i].unsqueeze(2).to_broadcast(wide), ALU.mult))
                link(dve.tensor_scalar(wt, wt, ROUND, ROUND, ALU.add, ALU.subtract))
                link.done()
                dve.tensor_tensor(w, wt, wscale[:, i].unsqueeze(2).to_broadcast(wide), ALU.mult).then_inc(w_quantised, 1)

            def set_scale(i, count):
                link = Links(dve, scale_made, SCALE_STEPS, i)
                one = slice(i, i + 1)
                link(dve.tensor_reduce(own_max[:, one], part_max[:, i, 0:count, 0], AX.X, ALU.max))
                if i == PS:
                    dve.tensor_tensor(own_max[:, one], own_max[:, one], scale[:, SS:SS + 1], ALU.mult).then_inc(max_made, 1)
                else:
                    dve.tensor_copy(own_max[:, one], own_max[:, one]).then_inc(max_made, 1)
                dve.wait_ge(max_all, i + 1)
                link(dve.tensor_scalar(scale[:, one], all_max[:, one], 1.0 / QMAX, 1e-12, ALU.mult, ALU.max))
                link(dve.reciprocal(inv[:, one], scale[:, one]))
                if i == PS:
                    link(dve.tensor_tensor(inv[:, one], inv[:, one], scale[:, SS:SS + 1], ALU.mult))
                else:
                    link(dve.tensor_copy(inv[:, one], inv[:, one]))
                link.done()

            dve.memset(rounder[:], ROUND).then_inc(made_consts, 1)
            dve.memset(neg_rounder[:], -ROUND).then_inc(made_consts, 1)
            layernorm_begin(dve, t)

            def x_step(n, parity, one_ahead, two_ahead):
                layernorm_apply(dve, t, n, parity)
                dve.wait_ge(t.xn_ready, n + 1)
                dve.tensor_reduce(part_max[:, XS, n], t.xn[:, parity], AX.X, ALU.max,
                                  apply_absolute_value=True).then_inc(x_max, 1)
            walk(dve, x_step)
            dve.wait_ge(x_max, B)
            set_scale(XS, B)
            quantise_weights(0)
            dve.tensor_scalar(unscale[:, 0:1], scale[:, XS:XS + 1], 1.0 / W_SCALE, None, ALU.mult).then_inc(unscale_made, 1)
            for c in range(C):
                dve.wait_ge(x_high, c + 1)
                dve.scalar_tensor_tensor(xqT[:, 1, c], t.xT[:, c].rearrange("p b l -> p (b l)"), ROUND, xqT[:, 0, c],
                                         ALU.subtract, ALU.subtract).then_inc(x_ready, 1)

            def weights_rest(tiles):
                for m in tiles:
                    dve.wait_ge(w_high, m + 1)
                    dve.scalar_tensor_tensor(weights_tile(1, m), ps[:, m % 4], W_SCALE, weights_tile(0, m),
                                             ALU.mult, ALU.subtract).then_inc(w_ready, 1)
            weights_rest(range(3))
            quantise_weights(1)

            def hidden(i, h):
                hid = (upT, gateT)[i][:].rearrange("p c (h g b) l -> p c h g (b l)", h=2, g=2)
                maxima = part_max[:, (US, GS)[i]].rearrange("p (h g c) a -> p h g c a", h=2, g=2)
                for g in range(2):
                    for c in range(FC):
                        tile = FC * g + c
                        dve.wait_ge(hidden_out, UP_TILES * i + TILES * h + tile + 1)
                        dve.tensor_reduce(maxima[:, h, g, c], hid[:, c, h, g], AX.X, ALU.max,
                                          apply_absolute_value=True).then_inc(hidden_max, 1)
                        if i == 1 and tile % 4 == 3:
                            dve.wait_ge(up_scaled, UPS * h + tile // 4 + 1)
                            dve.tensor_scalar(upT[:, UPS * h + tile // 4], upT[:, UPS * h + tile // 4], ROUND, scale[:, US:US + 1],
                                              ALU.subtract, ALU.mult).then_inc(up_ready, 1)
            hidden(0, 0)
            weights_rest(range(3, 6))
            hidden(0, 1)
            dve.wait_ge(hidden_max, UP_TILES)
            set_scale(US, G4 * FC)
            quantise_weights(2)
            with dve.Fori(0, 2) as h:
                hidden(1, h)
            dve.wait_ge(hidden_max, 2 * UP_TILES)
            set_scale(GS, G4 * FC)
            for c in range(FC):
                flat = gateT[:, c].rearrange("p b l -> p (b l)")
                link = Links(dve, silu_link, 2, c)
                dve.wait_ge(sig_ready, c + 1)
                link(dve.tensor_scalar(sig[:, c % 2], sig[:, c % 2], ROUND, SIG_STEPS - 1, ALU.subtract, ALU.min))
                link(dve.scalar_tensor_tensor(flat, sig[:, c % 2], 1.0 / SIG_STEPS, flat, ALU.mult, ALU.mult))
                link.done()
                dve.tensor_reduce(part_max[:, SS, c], flat, AX.X, ALU.max, apply_absolute_value=True).then_inc(silu_ready, 1)
            dve.wait_ge(silu_ready, FC)
            set_scale(SS, FC)
            weights_rest(range(6, 9))
            for c in range(FC):
                flat = gateT[:, c].rearrange("p b l -> p (b l)")
                dve.wait_ge(silu_scaled, c + 1)
                dve.wait_ge(up_ready, c + 1)
                dve.scalar_tensor_tensor(flat, flat, ROUND, upT[:, c].rearrange("p b l -> p (b l)"),
                                         ALU.subtract, ALU.mult).then_inc(prod_link, 1)
                dve.wait_ge(prod_link, c + 1)
                dve.tensor_reduce(part_max[:, PS, c], flat, AX.X, ALU.max, apply_absolute_value=True).then_inc(prod_ready, 1)
            dve.wait_ge(prod_ready, FC)
            set_scale(PS, FC)
            dve.tensor_scalar(unscale[:, 1:2], scale[:, PS:PS + 1], 1.0 / W_SCALE, None, ALU.mult).then_inc(unscale_made, 1)

            def product_rest(n, parity):
                dve.wait_ge(prod_high, n + 1)
                dve.scalar_tensor_tensor(prodT[:, parity, 1], prod_r[:, parity], ROUND, prodT[:, parity, 0],
                                         ALU.subtract, ALU.subtract).then_inc(prodT_ready, 1)
            product_rest(0, 0)
            dve.wait_ge(unscale_made, 2)

            def step(n, parity, one_ahead, two_ahead):
                if one_ahead:
                    product_rest(n + 1, 1 - parity)
                link = Links(dve, t.add_link, 1, n)
                dve.wait_ge(out_made, n + 1)
                link(dve.scalar_tensor_tensor(t.X[:, n, :], ps_out[:, parity, 0:D], unscale[:, 1:2], t.X[:, n, :],
                                              ALU.mult, ALU.add))
                link.done()
                batch_stats(dve, t.X, t.stats, n).then_inc(out_added, 1)
            walk(dve, step)


E = 8
HID = 1024
HJ = HID // P
STEPS = E * G4


def expert_walk(eng, step, last_step):
    for half in range(2):
        for g in range(G4):
            step(half, half, g)
    with eng.Fori(1, E // 2) as j:
        for half in range(2):
            for g in range(G4):
                step(2 * j + half, half, g)
    last_step()


def before(half, g):
    return (half, g - 1) if g else (1 - half, G4 - 1)


def is_first(e, g):
    return isinstance(e, int) and e == 0 and g == 0


W_SCALE = 2.0 ** 8
SPLIT = ((0, 0), (0, 1), (1, 0))


def split_hidden(act, t, high, ps, function, bias, j, q, made, split, ready):
    enough(act, split, q - 1)
    act.wait_ge(made, q + 1)
    act.activation(t.h[:, j % 2], ps, function, bias=bias, scale=1.0 / W_SCALE).then_inc(ready, 1)
    act.wait_ge(ready, q + 1)
    act.activation(high, t.h[:, j % 2], ACT.Copy).then_inc(t.high_ready, 1)


def split_rest(dve, t, parts, j, q, split):
    dve.wait_ge(t.high_ready, q + 1)
    dve.tensor_tensor(parts[:, 1], t.h[:, j % 2], parts[:, 0], ALU.subtract).then_inc(split, 1)


def expert_weights(sp, t, w1, w2):
    def load(e):
        sp.dma_start(t.w1_in[:], w1[e].rearrange("(k p) h -> p k h", p=P)).then_inc(t.w_in, 16)
        sp.dma_start(t.w2_in[:], w2[e].rearrange("(j p) n -> p j n", p=P)).then_inc(t.w_in, 16)
    load(0)
    with sp.Fori(1, E) as e:
        sp.wait_ge(t.w_split, e)
        load(e)


def split_weights(pool, t, e, half):
    link = Links(pool, t.split_link, 2, e)
    scale1 = t.w_scale[:].unsqueeze(2).to_broadcast([P, C, HID])
    scale2 = t.w_scale[:].unsqueeze(2).to_broadcast([P, HJ, D])
    pool.wait_ge(t.w_in, 32 * (e + 1))
    enough(pool, t.eo_made, B * (e - 1))
    pool.tensor_tensor(t.w1[:, half, 0], t.w1_in[:], scale1, ALU.mult)
    link(pool.tensor_tensor(t.w2[:, half, 0], t.w2_in[:], scale2, ALU.mult))
    pool.tensor_tensor(t.w1_in[:], t.w1_in[:], scale1, ALU.mult)
    link(pool.tensor_tensor(t.w2_in[:], t.w2_in[:], scale2, ALU.mult))
    link.done()
    pool.tensor_tensor(t.w1[:, half, 1], t.w1_in[:], t.w1[:, half, 0], ALU.subtract)
    pool.tensor_tensor(t.w2[:, half, 1], t.w2_in[:], t.w2[:, half, 0], ALU.subtract).then_inc(t.w_split, 1)


def expert_tiles(t):
    t.w1_in = t.sb("w1_in", [P, C, HID])
    t.w2_in = t.sb("w2_in", [P, HJ, D])
    t.w1 = t.sb("w1", [P, 2, 2, C, HID], F16)
    t.w2 = t.sb("w2", [P, 2, 2, HJ, D], F16)
    t.w_scale = t.sb("w_scale", [P, 1])
    t.b1_rows = t.sb("b1_rows", [E * HJ, P])
    t.b1T = t.sb("b1T", [P, E, HJ])
    t.b1 = t.sb("b1", [P, 2, HJ])
    t.h = t.sb("h", [P, 2, 512])
    t.w_in, t.w_split, t.split_link = t.sem("w_in"), t.sem("w_split"), t.sem("split_link")
    t.scale_set = t.sem("scale_set")
    t.high_ready = t.sem("high_ready")
    t.eo_made = t.sem("eo_made")
    t.b1_ready = t.sem("b1_ready")


def routed_ffn(nc, env):
    A, K = env.inputs, env.consts
    with ExitStack() as ctx:
        t = Tiles(nc, ctx, "mo")
        layernorm_tiles(t, env)
        turned_tiles(t)
        expert_tiles(t)
        ident = t.sb("ident", [P, P])
        iota = t.sb("iota", [P, DH])
        wr = t.sb("wr", [P, C, E])
        br = t.sb("br", [E, 1])
        b2 = t.sb("b2", [E, D])
        logitsT = t.sb("logitsT", [E, B, L])
        logits = t.sb("logits", [P, B, E])
        top = t.sb("top", [P, B, 8])
        place = t.sb("place", [P, B, 8], U32)
        gap = t.sb("gap", [P, B, 1])
        ratio = t.sb("ratio", [P, B, 1])
        share = t.sb("share", [P, 2, B, 1])
        hit = t.sb("hit", [P, 2, B, E])
        route = t.sb("route", [P, B, E])
        route_scaled = t.sb("route_scaled", [P, B, E])
        routeT = t.sb("routeT", [E, B, P])
        route_e = t.sb("route_e", [P, 2, B])
        xT_high = t.sb("xT_high", [P, C, B, L], F16)
        xT_low = t.sb("xT_low", [P, C, B, L], F16)
        hT = t.sb("hT", [P, 2, 2, HJ, 512], F16)
        ps_h = t.ps("ps_h", [P, 4, 512])
        ps_eo = t.ps("ps_eo", [P, 2, 512])

        consts_in = t.sem("consts_in")
        logits_made, logits_out = t.sem("logits_made"), t.sem("logits_out")
        logits_turned, logits_ready = t.sem("logits_turned"), t.sem("logits_ready")
        route_link, gap_ready, ratio_ready, route_ready = (t.sem(n) for n in ("route_link", "gap_ready", "ratio_ready", "route_ready"))
        b1_turned = t.sem("b1_turned")
        route_turned, routeT_ready = t.sem("route_turned"), t.sem("routeT_ready")
        bias_made, bias_added = t.sem("bias_made"), t.sem("bias_added")
        x_split = t.sem("x_split")
        h_made, h_ready, h_split = t.sem("h_made"), t.sem("h_ready"), t.sem("h_split")
        expert_in, eo_added = t.sem("expert_in"), t.sem("eo_added")
        block = ctx.enter_context(nc.Block())
        CONSTS = 16 * 6
        XT, XT_high, XT_low = (x[:].rearrange("p c (g b) l -> p c g (b l)", g=G4) for x in (t.xT, xT_high, xT_low))

        @block.sync
        def _(sp):
            sp.dma_start(ident[:], K["ident"]).then_inc(consts_in, 16)
            sp.dma_start(iota[:], K["iota"]).then_inc(consts_in, 16)
            sp.dma_start(wr[:], A["L3_ffn_Wr"].rearrange("(c p) e -> p c e", p=P)).then_inc(consts_in, 16)
            sp.dma_start(br[:], A["L3_ffn_br"].unsqueeze(1)).then_inc(consts_in, 16)
            sp.dma_start(b2[:], A["L3_ffn_b2"]).then_inc(consts_in, 16)
            sp.dma_start(t.b1_rows[:], A["L3_ffn_b1"].rearrange("e (j p) -> (e j) p", p=P)).then_inc(consts_in, 16)
            expert_weights(sp, t, A["L3_ffn_W1"], A["L3_ffn_W2"])

        @block.tensor
        def _(pe):
            pe.wait_ge(consts_in, CONSTS)
            pe.transpose(ps_h[:, 0, 0:E * HJ], t.b1_rows[:], ident[0:E * HJ, 0:E * HJ]).then_inc(b1_turned, 1)
            turn_x(pe, t, ident)
            pe.wait_ge(t.xT_ready, B)
            for g in range(G4):
                if g >= 2:
                    pe.wait_ge(logits_out, g - 1)
                for k in range(C):
                    last = pe.matmul(ps_eo[0:E, g % 2], wr[:, k], XT[:, k, g], start=k == 0, stop=k == C - 1)
                last.then_inc(logits_made, 1)
            pe.wait_ge(logits_out, G4)
            for n in range(B):
                last = pe.transpose(t.ps_x[:, 0, n * E:(n + 1) * E], logitsT[:, n], ident[0:E, 0:E])
            last.then_inc(logits_turned, 1)

            def turn_routes():
                pe.wait_ge(route_ready, 1)
                for g in range(G4):
                    pe.wait_ge(logits_ready, 1)
                    if g >= 2:
                        pe.wait_ge(routeT_ready, g - 1)
                    for b in range(4):
                        last = pe.transpose(ps_eo[0:E, g % 2, b * P:(b + 1) * P], route[:, 4 * g + b], ident[:])
                    last.then_inc(route_turned, 1)
                pe.wait_ge(routeT_ready, G4)
                for n in range(B):
                    if n >= 2:
                        pe.wait_ge(bias_added, n - 1)
                    pe.matmul(ps_eo[:, n % 2, 0:D], routeT[:, n], b2[:], start=True, stop=True).then_inc(bias_made, 1)

            def hidden(e, half, g):
                pe.wait_ge(t.w_split, e + 1)
                if isinstance(e, int) and e == 0:
                    pe.wait_ge(x_split, g + 1)
                for j in range(HJ):
                    q = 8 * (G4 * e + g) + j
                    enough(pe, h_ready, q - 3)
                    for k in range(C):
                        for a, (w, x) in enumerate(SPLIT):
                            last = pe.matmul(ps_h[:, j % 4], t.w1[:, half, w, k, j * P:(j + 1) * P],
                                             (XT_low if x else XT_high)[:, k, g],
                                             start=(k, a) == (0, 0), stop=(k, a) == (C - 1, 2))
                    last.then_inc(h_made, 1)

            def out(e, half, g, counted_from):
                pe.wait_ge(h_split, 8 * (counted_from + 1))
                for b in range(4):
                    n = 4 * counted_from + b
                    bank = b % 2
                    enough(pe, eo_added, n - 1)
                    for j in range(HJ):
                        for a, (h, w) in enumerate(SPLIT):
                            last = pe.matmul(ps_eo[:, bank, 0:D], hT[:, g % 2, h, j, b * P:(b + 1) * P], t.w2[:, half, w, j],
                                             start=(j, a) == (0, 0), stop=(j, a) == (HJ - 1, 2))
                    last.then_inc(t.eo_made, 1)

            def step(e, half, g):
                hidden(e, half, g)
                if is_first(e, g):
                    turn_routes()
                    pe.wait_ge(bias_added, B)
                else:
                    out(e, *before(half, g), G4 * e + g - 1)
            expert_walk(pe, step, lambda: out(E - 1, 1, G4 - 1, STEPS - 1))

        @block.scalar
        def _(act):
            act.wait_ge(b1_turned, 1)
            act.activation(t.b1T[:].rearrange("p e j -> p (e j)"), ps_h[:, 0, 0:E * HJ], ACT.Copy).then_inc(t.b1_ready, 1)
            turned_x_out(act, t, xT_high)
            act.wait_ge(consts_in, CONSTS)
            for g in range(G4):
                act.wait_ge(logits_made, g + 1)
                act.activation(logitsT[:, 4 * g:4 * g + 4].rearrange("e b l -> e (b l)"), ps_eo[0:E, g % 2], ACT.Identity,
                               bias=br[:]).then_inc(logits_out, 1)
            act.wait_ge(logits_turned, 1)
            act.activation(logits[:].rearrange("p b e -> p (b e)"), t.ps_x[:, 0, 0:B * E], ACT.Copy).then_inc(logits_ready, 1)
            act.wait_ge(gap_ready, 1)
            act.activation(ratio[:], gap[:], ACT.Exp).then_inc(ratio_ready, 1)

            def step(e, half, g):
                act.wait_ge(expert_in, e + 1)
                for j in range(HJ):
                    q = 8 * (G4 * e + g) + j
                    split_hidden(act, t, hT[:, g % 2, 0, j], ps_h[:, j % 4], ACT.Relu,
                                 t.b1[:, half, j:j + 1], j, q, h_made, h_split, h_ready)
                if is_first(e, g):
                    for g2 in range(G4):
                        act.wait_ge(route_turned, g2 + 1)
                        act.activation(routeT[:, 4 * g2:4 * g2 + 4].rearrange("e b l -> e (b l)"), ps_eo[0:E, g2 % 2],
                                       ACT.Copy).then_inc(routeT_ready, 1)
            expert_walk(act, step, lambda: None)

        @block.gpsimd
        def _(pool):
            pool.memset(t.w_scale[:], W_SCALE).then_inc(t.scale_set, 1)
            pool.wait_ge(t.scale_set, 1)
            split_weights(pool, t, 0, 0)
            pool.wait_ge(t.b1_ready, 1)
            pool.wait_ge(route_ready, 2)

            def fetch(e, half):
                pool.tensor_copy(t.b1[:, half], t.b1T[:, e])
                pool.tensor_copy(route_e[:, half], route_scaled[:, :, e]).then_inc(expert_in, 1)
            fetch(0, 0)
            split_weights(pool, t, 1, 1)
            fetch(1, 1)
            with pool.Fori(1, E // 2) as i:
                for half in range(2):
                    split_weights(pool, t, 2 * i + half, half)
                    pool.wait_ge(eo_added, B * (2 * i + half - 1))
                    fetch(2 * i + half, half)

        @block.vector
        def _(dve):
            layernorm_begin(dve, t)

            def x_step(n, parity, one_ahead, two_ahead):
                layernorm_apply(dve, t, n, parity)
            walk(dve, x_step)
            for g in range(G4):
                dve.wait_ge(t.xT_ready, 4 * (g + 1))
                dve.tensor_tensor(XT_low[:, :, g], XT[:, :, g], XT_high[:, :, g], ALU.subtract).then_inc(x_split, 1)
            dve.wait_ge(consts_in, CONSTS)
            link = Links(dve, route_link, 7, 0)
            dve.wait_ge(logits_ready, 1)
            for n in range(B):
                last = dve.max(top[:, n], logits[:, n])
            link(last)
            dve.tensor_tensor(gap[:], top[:, :, 1:2], top[:, :, 0:1], ALU.subtract).then_inc(gap_ready, 1)
            for n in range(B):
                last = dve.max_index(place[:, n], top[:, n], logits[:, n])
            link(last)
            for i in range(2):
                last = dve.tensor_tensor(hit[:, i], iota[:, 0:E].unsqueeze(1).to_broadcast([P, B, E]),
                                         place[:, :, i:i + 1].to_broadcast([P, B, E]), ALU.is_equal)
            link(last)
            dve.wait_ge(ratio_ready, 1)
            link(dve.tensor_scalar(share[:, 1], ratio[:], 1.0, None, ALU.add))
            link(dve.reciprocal(share[:, 0], share[:, 1]))
            link(dve.tensor_tensor(share[:, 1], share[:, 0], ratio[:], ALU.mult))
            for i in range(2):
                last = dve.tensor_tensor(hit[:, i], hit[:, i], share[:, i].to_broadcast([P, B, E]), ALU.mult)
            link(last)
            link.done()
            dve.tensor_tensor(route[:], hit[:, 0], hit[:, 1], ALU.add).then_inc(route_ready, 1)
            dve.wait_ge(route_ready, 1)
            dve.tensor_scalar(route_scaled[:], route[:], 1.0 / W_SCALE, None, ALU.mult).then_inc(route_ready, 1)

            def add_biases():
                for n in range(B):
                    dve.wait_ge(bias_made, n + 1)
                    dve.tensor_tensor(t.X[:, n], t.X[:, n], ps_eo[:, n % 2, 0:D], ALU.add).then_inc(bias_added, 1)

            def rest_of_hidden(e, g):
                for j in range(HJ):
                    split_rest(dve, t, hT[:, g % 2, :, j], j, 8 * (G4 * e + g) + j, h_split)

            def add(half, g, counted_from):
                for b in range(4):
                    n = 4 * counted_from + b
                    dve.wait_ge(t.eo_made, n + 1)
                    at = 4 * g + b
                    dve.scalar_tensor_tensor(t.X[:, at], ps_eo[:, b % 2, 0:D], route_e[:, half, at:at + 1], t.X[:, at],
                                             ALU.mult, ALU.add).then_inc(eo_added, 1)

            def step(e, half, g):
                rest_of_hidden(e, g)
                if is_first(e, g):
                    add_biases()
                else:
                    add(*before(half, g), G4 * e + g - 1)
                if g == 0:
                    dve.wait_ge(expert_in, e + 1)
            expert_walk(dve, step, lambda: add(1, G4 - 1, STEPS - 1))


def newton_rsqrt(dve, link, out, var, half, tmp):
    link(dve.tensor_scalar(half, var.bitcast(I32), 1, None, ALU.logical_shift_right))
    link(dve.tensor_scalar(out.bitcast(I32), half, -1.0, RSQRT_MAGIC, ALU.mult, ALU.add))
    for _ in range(NEWTON_STEPS):
        link(dve.scalar_tensor_tensor(tmp, out, -0.5, out, ALU.mult, ALU.mult))
        link(dve.tensor_tensor(tmp, tmp, var, ALU.mult))
        link(dve.scalar_tensor_tensor(out, tmp, 1.5, out, ALU.add, ALU.mult))


def has_two_before(e, g):
    return not (isinstance(e, int) and G4 * e + g < 2)


def slot_ffn(nc, env):
    A, K = env.inputs, env.consts
    ES = E * P
    NT = B + E
    with ExitStack() as ctx:
        t = Tiles(nc, ctx, "sl")
        layernorm_tiles(t, env)
        expert_tiles(t)
        ident = t.sb("ident", [P, P])
        ident_b = t.sb("ident_b", [P, P], BF16)
        row_sel = t.sb("row_sel", [P, B, P], BF16)
        gamma = t.sb("gamma", [P, 2, D])
        b2 = t.sb("b2", [P, E, D])
        xr = t.sb("xr", [P, B, D])
        xr_parts = t.sb("xr_parts", [P, 2, B, D], F16)
        xrT = t.sb("xrT", [P, 2, C, B, L], F16)
        slotsT = t.sb("slotsT", [P, 2, C, E, P], F16)
        slotT_e = t.sb("slotT_e", [P, 2, 2, C, P], F16)
        norm2 = t.sb("norm2", [P, NT])
        r_half = t.sb("r_half", [P, NT], I32)
        r_tmp = t.sb("r_tmp", [P, NT])
        r_norm = t.sb("r_norm", [P, NT])
        neg_rmax = t.sb("neg_rmax", [P, P], BF16)
        neg_rmaxT = t.sb("neg_rmaxT", [P, P], BF16)
        neg_smax = t.sb("neg_smax", [P, 2, 4])
        dispT = t.sb("dispT", [P, 2, 4, L])
        disp_sum = t.sb("disp_sum", [P, 2, 4, 1])
        disp_inv = t.sb("disp_inv", [P, 2, 4, 1])
        disp = t.sb("disp", [P, 2, 2, 4, P], F16)
        combT = t.sb("combT", [P, 4, L])
        comb_parts = t.sb("comb_parts", [P, 2, 2, 4, L], F16)
        slot_inT = t.sb("slot_inT", [P, 2, 2, C, 4, P], F16)
        hT = t.sb("hT", [P, 2, HJ, 512], F16)
        slots = hT[:, 0].rearrange("p j n -> p (j n)").bitcast(F32).rearrange("p (e d) -> p e d", e=E)
        acc_max = t.sb("acc_max", [P, B, 2, 1])
        result = t.sb("result", [P, 2, D])
        result_parts = t.sb("result_parts", [P, 2, 2, D + 1], F16)
        acc = t.sb("acc", [P, B, D + 1])
        squares = acc[:, 0:2, 0:D]
        ps_lt = t.ps("ps_lt", [P, 4, L])
        ps_in = t.ps("ps_in", [P, C, 4, P])
        ps_h = t.ps("ps_h", [P, 2, 512])
        ps_eo = t.ps("ps_eo", [P, 2, 512])
        ps_out = t.ps("ps_out", [P, 512])

        ps_rows = [ps_h[:, 0], ps_h[:, 1], ps_eo[:, 0], ps_eo[:, 1]]

        slots_in, consts_in, made_consts = t.sem("slots_in"), t.sem("consts_in"), t.sem("made_consts")
        rows_high, xr_high, xr_split, disp_link = (t.sem(n) for n in ("rows_high", "xr_high", "xr_split", "disp_link"))
        squared, rms_link, rms_ready = t.sem("squared"), t.sem("rms_link"), t.sem("rms_ready")
        rows_turned, rowsT_ready = t.sem("rows_turned"), t.sem("rowsT_ready")
        b1_turned, expert_in = t.sem("b1_turned"), t.sem("expert_in")
        all_logits, rmax_ready, rmax_turned, rmaxT_ready = (t.sem(n) for n in ("all_logits", "rmax_ready", "rmax_turned", "rmaxT_ready"))
        logits_made, smax_ready, dispT_made = t.sem("logits_made"), t.sem("smax_ready"), t.sem("dispT_made")
        disp_norm_link, dispT_ready = t.sem("disp_norm_link"), t.sem("dispT_ready")
        disp_turned, disp_ready = t.sem("disp_turned"), t.sem("disp_ready")
        shifted, comb_ready, comb_high, comb_split = (t.sem(n) for n in ("shifted", "comb_ready", "comb_high", "comb_split"))
        result_high, result_split = t.sem("result_high"), t.sem("result_split")
        in_made, in_ready, in_split = t.sem("in_made"), t.sem("in_ready"), t.sem("in_split")
        h_made, h_ready, h_split = t.sem("h_made"), t.sem("h_ready"), t.sem("h_split")
        result_ready, out_made, out_added = t.sem("result_ready"), t.sem("out_made"), t.sem("out_added")
        end_link = t.sem("end_link")
        block = ctx.enter_context(nc.Block())
        CONSTS = 16 * 5
        XT = xrT[:].rearrange("p a c (g b) l -> p a c g (b l)", g=G4)

        @block.sync
        def _(sp):
            sp.dma_start(slots, A["L1_ffn_slot_embeds"].rearrange("e s d -> s e d")).then_inc(slots_in, 16)
            sp.dma_start(ident[:], K["ident"]).then_inc(consts_in, 16)
            for i, name in enumerate(("norm_gamma", "slot_norm_gamma")):
                sp.dma_start(gamma[:, i], A[f"L1_ffn_{name}"].unsqueeze(0).to_broadcast([P, D])).then_inc(consts_in, 16)
            sp.dma_start(b2[:], A["L1_ffn_b2"].unsqueeze(0).to_broadcast([P, E, D])).then_inc(consts_in, 16)
            sp.dma_start(t.b1_rows[:], A["L1_ffn_b1"].rearrange("e (j p) -> (e j) p", p=P)).then_inc(consts_in, 16)
            expert_weights(sp, t, A["L1_ffn_w1"], A["L1_ffn_w2"])

        @block.tensor
        def _(pe):
            pe.wait_ge(consts_in, CONSTS)
            pe.transpose(ps_out[:, 0:E * HJ], t.b1_rows[:], ident[0:E * HJ, 0:E * HJ]).then_inc(b1_turned, 1)
            for m in range(NT):
                pe.wait_ge(rms_ready, m + 1)
                if m >= 4:
                    pe.wait_ge(rowsT_ready, m - 3)
                rows = slots[:, m] if m < E else xr[:, m - E]
                for c in range(C):
                    last = pe.transpose(ps_rows[m % 4][:, c * P:(c + 1) * P], rows[:, c * P:(c + 1) * P], ident[:])
                last.then_inc(rows_turned, 1)
            pe.wait_ge(rowsT_ready, NT)
            for n in range(B):
                for i in range(2):
                    q = 2 * n + i
                    if q >= 2:
                        pe.wait_ge(rmax_ready, q - 1)
                    for k in range(C):
                        last = pe.matmul(ps_eo[:, i], xrT[:, 0, k, n], slotsT[:, 0, k, 4 * i:4 * i + 4].rearrange("p e s -> p (e s)"),
                                         start=k == 0, stop=k == C - 1)
                    last.then_inc(all_logits, 1)
            pe.wait_ge(rmax_ready, 2 * B + 1)
            pe.wait_ge(made_consts, 5)
            pe.transpose(ps_lt[:].rearrange("p b l -> p (b l)").bitcast(BF16)[:, 0:P], neg_rmax[:], ident_b[:]).then_inc(rmax_turned, 1)
            pe.wait_ge(rmaxT_ready, 1)

            def logits(e, half, g, q):
                pe.wait_ge(expert_in, e + 1)
                enough(pe, comb_ready, q)
                for k in range(C):
                    for a, (w, x) in enumerate(SPLIT):
                        last = pe.matmul(ps_lt[:].rearrange("p b l -> p (b l)"), slotT_e[:, half, w, k], XT[:, x, k, g],
                                         start=(k, a) == (0, 0), stop=(k, a) == (C - 1, 2))
                last.then_inc(logits_made, 1)

            def turn_dispatch(g, q):
                pe.wait_ge(dispT_ready, q + 1)
                enough(pe, in_split, q)
                for b in range(4):
                    last = pe.transpose(ps_in[:, 0, b], dispT[:, g % 2, b], ident[:])
                last.then_inc(disp_turned, 1)

            def shift(g, q):
                pe.wait_ge(dispT_made, 4 * (q + 1))
                for b in range(4):
                    last = pe.matmul(ps_lt[:, b], row_sel[:, 4 * g + b], neg_rmaxT[:], start=False, stop=True,
                                     skip_group_check=True)
                last.then_inc(shifted, 1)

            def slot_inputs(g, q):
                pe.wait_ge(disp_ready, q + 1)
                if isinstance(q, int) and q == 0:
                    pe.wait_ge(xr_split, B)
                for b in range(4):
                    for c in range(C):
                        for a, (x, w) in enumerate(SPLIT):
                            last = pe.matmul(ps_in[:, c, b], xr_parts[:, x, 4 * g + b, c * P:(c + 1) * P], disp[:, g % 2, w, b],
                                             start=a == 0, stop=a == 2)
                last.then_inc(in_made, 1)

            def hidden(half, g, q, e):
                pe.wait_ge(t.w_split, e + 1)
                pe.wait_ge(in_split, q + 1)
                for j in range(HJ):
                    enough(pe, h_ready, 8 * q + j - 1)
                    for k in range(C):
                        for a, (w, x) in enumerate(SPLIT):
                            last = pe.matmul(ps_h[:, j % 2], t.w1[:, half, w, k, j * P:(j + 1) * P],
                                             slot_inT[:, g % 2, x, k].rearrange("p b s -> p (b s)"),
                                             start=(k, a) == (0, 0), stop=(k, a) == (C - 1, 2))
                    last.then_inc(h_made, 1)

            def combine(g, q, b):
                pe.wait_ge(result_split, 4 * q + b + 1)
                enough(pe, out_added, 4 * q + b)
                for a, (w, x) in enumerate(SPLIT):
                    last = pe.matmul(ps_out[:, 0:D + 1], comb_parts[:, g % 2, w, b], result_parts[:, b % 2, x],
                                     start=a == 0, stop=a == 2)
                last.then_inc(out_made, 1)

            def result_of(b, half, g, q):
                if b == 0:
                    pe.wait_ge(h_split, 8 * (q + 1))
                    pe.wait_ge(comb_split, q + 1)
                enough(pe, result_ready, 4 * q + b - 1)
                for j in range(HJ):
                    for a, (h, w) in enumerate(SPLIT):
                        last = pe.matmul(ps_eo[:, b % 2, 0:D], hT[:, h, j, b * P:(b + 1) * P], t.w2[:, half, w, j],
                                         start=(j, a) == (0, 0), stop=(j, a) == (HJ - 1, 2))
                last.then_inc(t.eo_made, 1)
                if b >= 1:
                    combine(g, q, b - 1)

            def step(e, half, g):
                q = G4 * e + g
                if is_first(e, g):
                    logits(e, half, g, q)
                    turn_dispatch(g, q)
                    shift(g, q)
                    slot_inputs(g, q)
                    return
                h0, g0 = before(half, g)
                hidden(h0, g0, q - 1, e if g else e - 1)
                logits(e, half, g, q)
                if has_two_before(e, g):
                    combine((g0 - 1) % G4, q - 2, 3)
                result_of(0, h0, g0, q - 1)
                result_of(1, h0, g0, q - 1)
                turn_dispatch(g, q)
                shift(g, q)
                result_of(2, h0, g0, q - 1)
                slot_inputs(g, q)
                result_of(3, h0, g0, q - 1)

            def last_step():
                hidden(1, G4 - 1, STEPS - 1, E - 1)
                combine(G4 - 2, STEPS - 2, 3)
                for b in range(4):
                    result_of(b, 1, G4 - 1, STEPS - 1)
                combine(G4 - 1, STEPS - 1, 3)
            expert_walk(pe, step, last_step)

        @block.scalar
        def _(act):
            act.wait_ge(slots_in, 16)
            for m in range(NT):
                if m >= E:
                    act.wait_ge(t.xn_ready, m - E + 1)
                if m >= 2:
                    act.wait_ge(squared, m - 1)
                rows = slots[:, m] if m < E else xr[:, m - E]
                act.activation(squares[:, m % 2], rows, ACT.Square, accum_out=norm2[:, m:m + 1]).then_inc(squared, 1)
            act.wait_ge(b1_turned, 1)
            act.activation(t.b1T[:].rearrange("p e j -> p (e j)"), ps_out[:, 0:E * HJ], ACT.Copy).then_inc(t.b1_ready, 1)
            for m in range(NT):
                act.wait_ge(rows_turned, m + 1)
                to = slotsT[:, 0, :, m] if m < E else xrT[:, 0, :, m - E]
                act.activation(to, ps_rows[m % 4][:, 0:D].rearrange("p (c l) -> p c l", c=C), ACT.Copy).then_inc(rows_high, 1)
                if m >= E:
                    act.activation(xr_parts[:, 0, m - E], xr[:, m - E], ACT.Copy).then_inc(xr_high, 1)
            act.wait_ge(rmax_turned, 1)
            act.activation(neg_rmaxT[:], ps_lt[:].rearrange("p b l -> p (b l)").bitcast(BF16)[:, 0:P], ACT.Copy).then_inc(rmaxT_ready, 1)

            def weights(g, q):
                act.wait_ge(smax_ready, q + 1)
                enough(act, disp_turned, q - 1)
                for b in range(4):
                    act.activation(dispT[:, g % 2, b], ps_lt[:, b], ACT.Exp, bias=neg_smax[:, g % 2, b:b + 1],
                                   accum_out=disp_sum[:, g % 2, b]).then_inc(dispT_made, 1)

            def combine_weights(g, q):
                act.wait_ge(shifted, q + 1)
                enough(act, comb_split, q)
                act.activation(combT[:], ps_lt[:], ACT.Exp).then_inc(comb_ready, 1)

            def combine_high(g, q):
                act.wait_ge(comb_ready, q + 1)
                enough(act, out_made, 4 * (q - 1))
                act.activation(comb_parts[:, g % 2, 0], combT[:], ACT.Copy).then_inc(comb_high, 1)

            def inputs_out(g, q):
                act.wait_ge(in_made, q + 1)
                enough(act, h_made, 8 * (q - 1))
                act.activation(slot_inT[:, g % 2, 0], ps_in[:], ACT.Copy).then_inc(in_ready, 1)

            def hidden(half, g, q):
                for j in range(HJ):
                    split_hidden(act, t, hT[:, 0, j], ps_h[:, j % 2], ACT.Gelu, t.b1[:, half, j:j + 1], j, 8 * q + j,
                                 h_made, h_split, h_ready)

            def step(e, half, g):
                q = G4 * e + g
                if not is_first(e, g):
                    h0, g0 = before(half, g)
                    hidden(h0, g0, q - 1)
                weights(g, q)
                combine_weights(g, q)
                inputs_out(g, q)
                combine_high(g, q)
            expert_walk(act, step, lambda: hidden(1, G4 - 1, STEPS - 1))

        @block.gpsimd
        def _(pool):
            pool.memset(t.w_scale[:], W_SCALE).then_inc(t.scale_set, 1)
            pool.wait_ge(t.scale_set, 1)
            split_weights(pool, t, 0, 0)
            for n in range(B):
                pool.wait_ge(xr_high, n + 1)
                pool.tensor_tensor(xr_parts[:, 1, n], xr[:, n], xr_parts[:, 0, n], ALU.subtract).then_inc(xr_split, 1)
            pool.wait_ge(squared, NT)
            pool.memset(acc[:], 0.0).then_inc(made_consts, 1)
            pool.wait_ge(t.b1_ready, 1)
            pool.wait_ge(rowsT_ready, E)

            def fetch(e, half):
                pool.tensor_copy(t.b1[:, half], t.b1T[:, e])
                pool.tensor_copy(slotT_e[:, half], slotsT[:, :, :, e]).then_inc(expert_in, 1)
            fetch(0, 0)
            split_weights(pool, t, 1, 1)
            fetch(1, 1)
            with pool.Fori(1, E // 2) as i:
                for half in range(2):
                    split_weights(pool, t, 2 * i + half, half)
                    pool.wait_ge(t.eo_made, B * (2 * i + half - 1))
                    fetch(2 * i + half, half)

        @block.vector
        def _(dve):
            layernorm_begin(dve, t)
            for n in range(B):
                dve.tensor_scalar(xr[:, n], t.X[:, n], t.meanvar[:, n, 0:1], t.rstd[:, n], ALU.subtract, ALU.mult).then_inc(t.xn_ready, 1)
            dve.wait_ge(consts_in, CONSTS)
            dve.tensor_copy(ident_b[:], ident[:])
            dve.tensor_copy(row_sel[:], ident[:, 0:B].unsqueeze(2).to_broadcast([P, B, P])).then_inc(made_consts, 1)
            dve.wait_ge(squared, NT)
            dve.wait_ge(t.xn_ready, B)
            link = Links(dve, rms_link, 4 + 3 * NEWTON_STEPS, 0)
            link(dve.tensor_scalar(norm2[:], norm2[:], 1e-24, None, ALU.max))
            newton_rsqrt(dve, link, r_norm[:], norm2[:], r_half[:], r_tmp[:])
            link(dve.tensor_scalar(r_norm[:], r_norm[:], float(D) ** 0.5, None, ALU.mult))
            link.done()

            def rows_rest(m):
                to = slotsT[:, :, :, m] if m < E else xrT[:, :, :, m - E]
                dve.wait_ge(rows_high, m + 1)
                dve.tensor_tensor(to[:, 1], ps_rows[m % 4][:, 0:D].rearrange("p (c l) -> p c l", c=C), to[:, 0],
                                  ALU.subtract).then_inc(rowsT_ready, 1)

            for m in range(NT):
                rows = slots[:, m] if m < E else xr[:, m - E]
                dve.scalar_tensor_tensor(rows, rows, r_norm[:, m:m + 1], gamma[:, int(m < E)], ALU.mult, ALU.mult).then_inc(rms_ready, 1)
                if m >= 3:
                    rows_rest(m - 3)
            for m in range(NT - 3, NT):
                rows_rest(m)
            dve.memset(neg_rmax[:], 0.0).then_inc(made_consts, 1)
            dve.memset(result_parts[:, :, 0], 1.0).then_inc(made_consts, 1)
            dve.memset(result_parts[:, :, 1], 0.0).then_inc(made_consts, 1)
            for q in range(2 * B):
                dve.wait_ge(all_logits, q + 1)
                dve.tensor_reduce(acc_max[:, q // 2, q % 2], ps_eo[:, q % 2], AX.X, ALU.max, negate=True).then_inc(rmax_ready, 1)
            dve.wait_ge(rmax_ready, 2 * B)
            dve.wait_ge(made_consts, 5)
            dve.tensor_tensor(neg_rmax[:, 0:B], acc_max[:, :, 0, 0], acc_max[:, :, 1, 0], ALU.min).then_inc(rmax_ready, 1)

            def slot_max(g, q):
                dve.wait_ge(logits_made, q + 1)
                dve.tensor_reduce(neg_smax[:, g % 2], ps_lt[:], AX.X, ALU.max, negate=True).then_inc(smax_ready, 1)

            def normalise_dispatch(g, q):
                link = Links(dve, disp_norm_link, 1, q)
                dve.wait_ge(dispT_made, 4 * (q + 1))
                link(dve.reciprocal(disp_inv[:, g % 2], disp_sum[:, g % 2]))
                link.done()
                dve.tensor_tensor(dispT[:, g % 2], dispT[:, g % 2], disp_inv[:, g % 2].to_broadcast([P, 4, L]),
                                  ALU.mult).then_inc(dispT_ready, 1)

            def inputs_rest(g, q):
                dve.wait_ge(in_ready, q + 1)
                dve.tensor_tensor(slot_inT[:, g % 2, 1], ps_in[:], slot_inT[:, g % 2, 0], ALU.subtract).then_inc(in_split, 1)

            def combine_rest(g, q):
                dve.wait_ge(comb_high, q + 1)
                dve.tensor_tensor(comb_parts[:, g % 2, 1], combT[:], comb_parts[:, g % 2, 0], ALU.subtract).then_inc(comb_split, 1)

            def rest_of_hidden(q):
                for j in range(HJ):
                    split_rest(dve, t, hT[:, :, j], j, 8 * q + j, h_split)

            def dispatch_out(g, q):
                dve.wait_ge(disp_turned, q + 1)
                enough(dve, in_made, q - 1)
                link = Links(dve, disp_link, 1, q)
                link(dve.tensor_copy(disp[:, g % 2, 0], ps_in[:, 0]))
                link.done()
                dve.tensor_tensor(disp[:, g % 2, 1], ps_in[:, 0], disp[:, g % 2, 0], ALU.subtract).then_inc(disp_ready, 1)

            def add(g, q, b):
                at = 4 * g + b
                dve.wait_ge(out_made, 4 * q + b + 1)
                dve.tensor_tensor(acc[:, at], acc[:, at], ps_out[:, 0:D + 1], ALU.add).then_inc(out_added, 1)

            def result_of(b, e, g, q):
                dve.wait_ge(t.eo_made, 4 * q + b + 1)
                enough(dve, out_made, 4 * q + b - 1)
                dve.scalar_tensor_tensor(result[:, b % 2], ps_eo[:, b % 2, 0:D], 1.0 / W_SCALE, b2[:, e],
                                         ALU.mult, ALU.add).then_inc(result_ready, 1)
                dve.wait_ge(result_ready, 4 * q + b + 1)
                dve.tensor_copy(result_parts[:, b % 2, 0, 0:D], result[:, b % 2]).then_inc(result_high, 1)
                dve.wait_ge(result_high, 4 * q + b + 1)
                dve.tensor_tensor(result_parts[:, b % 2, 1, 0:D], result[:, b % 2], result_parts[:, b % 2, 0, 0:D],
                                  ALU.subtract).then_inc(result_split, 1)
                if b >= 1:
                    add(g, q, b - 1)

            def step(e, half, g):
                q = G4 * e + g
                if is_first(e, g):
                    slot_max(g, q)
                    normalise_dispatch(g, q)
                    dispatch_out(g, q)
                    inputs_rest(g, q)
                    combine_rest(g, q)
                    return
                e0, g0 = e if g else e - 1, before(half, g)[1]
                rest_of_hidden(q - 1)
                slot_max(g, q)
                if has_two_before(e, g):
                    add((g0 - 1) % G4, q - 2, 3)
                result_of(0, e0, g0, q - 1)
                normalise_dispatch(g, q)
                result_of(1, e0, g0, q - 1)
                dispatch_out(g, q)
                result_of(2, e0, g0, q - 1)
                inputs_rest(g, q)
                result_of(3, e0, g0, q - 1)
                combine_rest(g, q)

            def last_step():
                link = Links(dve, end_link, 10, 0)

                def invert_sums(first, end):
                    dve.wait_ge(out_added, B * (E - 1) + end)
                    link(dve.reciprocal(acc[:, first:end, D:D + 1], acc[:, first:end, D:D + 1]))

                def finish(first, end):
                    for n in range(first, end):
                        last = dve.scalar_tensor_tensor(t.X[:, n], acc[:, n, 0:D], acc[:, n, D:D + 1], t.X[:, n],
                                                        ALU.mult, ALU.add)
                    link(last)
                    for n in range(first, end):
                        batch_stats(dve, t.X, t.stats, n)

                q = STEPS - 1
                invert_sums(0, 2 * 4)
                for j in range(HJ):
                    split_rest(dve, t, hT[:, :, j], j, 8 * q + j, h_split)
                    if j % 2 == 1:
                        finish(j - 1, j + 1)
                add(G4 - 2, q - 1, 3)
                invert_sums(2 * 4, 3 * 4)
                for b in range(4):
                    result_of(b, E - 1, G4 - 1, q)
                    if b in (1, 2):
                        finish(2 * 4 + 2 * (b - 1), 2 * 4 + 2 * b)
                add(G4 - 1, q, 3)
                invert_sums(3 * 4, B)
                finish(3 * 4, B)
                link.done()
            expert_walk(dve, step, last_step)


PHASES = [autocorrelation, quantised_ffn, windowed_attention, slot_ffn, full_attention, receptance_ffn, rotary_attention, routed_ffn]


class Env:

    def __init__(self, inputs, consts, X, stats):
        self.inputs, self.consts, self.X, self.stats = inputs, consts, X, stats


def load_x(nc, env):
    with ExitStack() as ctx:
        x_in = ctx.enter_context(nc.semaphore("x_in"))
        block = ctx.enter_context(nc.Block())

        @block.sync
        def _(sp):
            sp.dma_start(env.X[:], env.inputs["x"].rearrange("b l d -> l b d")).then_inc(x_in, 16)

        @block.vector
        def _(dve):
            dve.wait_ge(x_in, 16)
            for n in range(B):
                batch_stats(dve, env.X, env.stats, n)


def store_x(nc, env, out):
    with ExitStack() as ctx:
        x_out = ctx.enter_context(nc.semaphore("x_out"))
        block = ctx.enter_context(nc.Block())

        @block.sync
        def _(sp):
            sp.dma_start(out.rearrange("b l d -> l b d"), env.X[:]).then_inc(x_out, 16)
            sp.wait_ge(x_out, 16)


def build_program(nc, inputs, consts, out):
    with ExitStack() as ctx:
        X = ctx.enter_context(nc.sbuf_tensor("X", [P, B, D], F32))
        stats = ctx.enter_context(nc.sbuf_tensor("stats", [P, B, 6], F32))
        env = Env(inputs, consts, X, stats)
        load_x(nc, env)
        for phase in PHASES:
            phase(nc, env)
        store_x(nc, env, out)


def constants():
    f8 = np.float64
    tok = np.arange(L, dtype=f8)[:, None]
    freq = np.arange(L // 2, dtype=f8)[None, :]
    angle = 2 * np.pi * tok * freq / L
    cos, sin = np.cos(angle), np.sin(angle)
    sin[:, 0] = np.cos(np.pi * tok[:, 0])
    dft = np.concatenate([cos, sin, np.eye(L), sin, cos], axis=1)
    even = 2.0 / L * np.cos(angle).T
    odd = 2.0 / L * np.sin(angle).T
    nyquist = even.copy()
    even[0] = 1.0 / L
    nyquist[0] = np.cos(np.pi * tok[:, 0]) / L
    idft = np.concatenate([np.concatenate([even, nyquist]), np.concatenate([-odd, odd])], axis=1)
    row = np.arange(P)
    inv_freq = 1.0 / np.float32(10000.0) ** (np.arange(0, DH, 2, dtype=np.float32) / DH)
    position_angle = np.arange(L, dtype=np.float32)[None, :] * inv_freq[row % (DH // 2)][:, None]
    rot = np.zeros((P, P))
    rot[row, np.where(row % DH < DH // 2, row + DH // 2, row - DH // 2)] = np.where(row % DH < DH // 2, 1, -1)
    tables = {
        "head_of_row": row[:, None] // DH == np.arange(HC)[None, :],
        "window": np.where(np.abs(row[:, None] - row[None, :]) <= WINDOW, 0.0, HUGE_NEGATIVE),
        "cosT": np.cos(position_angle),
        "sinT": np.sin(position_angle),
        "rot": rot,
        "dft": dft,
        "idft": idft,
        "iota": np.broadcast_to(np.arange(DH), (P, DH)),
        "row_mod": (row % DH + P)[:, None],
        "head_mask": np.repeat((row[:, None] // DH == np.arange(HC)[None, :]), DH, axis=1),
        "ident": np.eye(P),
    }
    return {k: np.ascontiguousarray(v, dtype=np.float32) for k, v in tables.items()}


def kernel(**inputs):
    import concourse.bacc as bacc
    from concourse.bass_utils import run_bass_kernel_spmd

    nc = bacc.Bacc("TRN2", target_bir_lowering=False, num_devices=1)
    arrays = {}

    def dram(name, a):
        arrays[name] = np.ascontiguousarray(a)
        return nc.dram_tensor(name, arrays[name].shape, F32, kind="ExternalInput").ap()

    ins = {name: dram(f"in_{name}", a) for name, a in inputs.items()}
    consts = {name: dram(f"const_{name}", a) for name, a in constants().items()}
    out = nc.dram_tensor("out", [B, L, D], F32, kind="ExternalOutput").ap()
    build_program(nc, ins, consts, out)
    r = run_bass_kernel_spmd(nc, [arrays], core_ids=[0])
    return r.results[0]["out"]
```
